# Optimizing a Trainium2 kernel written in Bass

```python
import numpy as np
import jax
import jax.numpy as jnp

def _softmax(x, axis=-1):
    return jax.nn.softmax(x, axis=axis)

def _gelu(x):
    return jax.nn.gelu(x, approximate=True)

def _silu(x):
    return jax.nn.silu(x)

def _sigmoid(x):
    return jax.nn.sigmoid(x)

def _layernorm(x, axis=-1, eps=1e-05):
    m = jnp.mean(x, axis=axis, keepdims=True)
    v = jnp.var(x, axis=axis, keepdims=True)
    return (x - m) / jnp.sqrt(v + eps)

def _scatter_add(tgt, idx, src, axis=0):
    return tgt.at[idx].add(src)

def _segment_sum(src, seg, n):
    return jax.ops.segment_sum(src, seg, n)
kernel_name = 'mk_decoder_preln_d1_seqx_r4_ac97d9'

def setup_inputs(seed: int=0):
    np.random.seed(seed)
    _w = jnp.asarray

    def _rec_inputs():
        import jax
        import jax.numpy as jnp
        _rk = jax.random.key(seed)
        x = 7.22e-05 + 1 * jax.random.normal(jax.random.fold_in(_rk, 1), (4, 512, 256), jnp.float32)
        _lenS = 512 - jax.random.randint(jax.random.fold_in(_rk, 7), (4,), 0, max(1, 512 // 4) + 1, jnp.int32)
        _lenS2 = 512 - jax.random.randint(jax.random.fold_in(_rk, 8), (4,), 0, max(1, 512 // 4) + 1, jnp.int32)
        _ctx_1024P = jax.random.normal(jax.random.fold_in(_rk, 11), (4, 16, 256), jnp.float32)
        _ctx_1024c = jax.random.dirichlet(jax.random.fold_in(_rk, 511), 0.3 * jnp.ones((16,), jnp.float32), (4, 512))
        _ctx_1024t = jnp.einsum('bsk,bkd->bsd', _ctx_1024c, _ctx_1024P)
        _ctx_1024t = _ctx_1024t * jax.lax.rsqrt(jnp.mean(jnp.square(_ctx_1024t)) + 1e-12) * 0.953939
        ctx_1024 = 4.13588e-05 + 0.999923 * (_ctx_1024t + 0.3 * jax.random.normal(jax.random.fold_in(_rk, 611), (4, 512, 256), jnp.float32))
        _validS = jnp.arange(512)[None, :] < _lenS[:, None]
        _validS2 = jnp.arange(512)[None, :] < _lenS2[:, None]
        _causal = jnp.tril(jnp.ones((512, 512), dtype=bool))
        mask_Bx1xSxS2_if1 = jnp.where(jnp.ones((4, 1, 512, 512), dtype=bool), 1, 0).astype(jnp.int32)
        return (x, ctx_1024, mask_Bx1xSxS2_if1)
    x, ctx_1024, mask_Bx1xSxS2_if1 = _rec_inputs()

    def _L0_attn_setup():
        import jax, jax.numpy as jnp
        import numpy as np
        B, N, D, H = (2, 512, 256, 16)
        HD = D // H
        SCALING = (D / H) ** 0.5
        EPS = 1e-05
        key = jax.random.key(seed)
        k1, k2, k3 = jax.random.split(key, 3)
        return {'z': jax.random.normal(k1, (B, N, D), dtype=jnp.float32), 'ln_scale': jnp.ones((D,), dtype=jnp.float32), 'ln_bias': jnp.zeros((D,), dtype=jnp.float32), 'w_qkv': jax.random.normal(k2, (D, 3 * D), dtype=jnp.float32) * D ** (-0.5), 'w_proj': jax.random.normal(k3, (D, D), dtype=jnp.float32) * D ** (-0.5), 'b_proj': jnp.zeros((D,), dtype=jnp.float32)}
    _L0_attn_all = _L0_attn_setup()
    _L0_attn_in = {k: v for k, v in _L0_attn_all.items() if k in ('ln_scale', 'ln_bias', 'w_qkv', 'w_proj', 'b_proj')}
    del _L0_attn_all

    def _L0_xattn_setup():
        import jax, jax.numpy as jnp
        import numpy as np
        D_MODEL = 256
        HEADS = 16
        D_K = D_MODEL // HEADS
        BS, SEQ = (4, 512)
        key = jax.random.key(seed)
        ks = jax.random.split(key, 12)
        s = 1.0 / np.sqrt(D_MODEL)
        inp = {'q': jax.random.normal(ks[0], (BS, SEQ, D_MODEL), jnp.float32), 'k': jax.random.normal(ks[1], (BS, SEQ, D_MODEL), jnp.float32), 'v': jax.random.normal(ks[2], (BS, SEQ, D_MODEL), jnp.float32), 'mask': jnp.ones((BS, 1, SEQ, SEQ), jnp.int32), 'Wq': jax.random.normal(ks[3], (D_MODEL, D_MODEL), jnp.float32) * s, 'bq': jnp.zeros((D_MODEL,), jnp.float32), 'Wk': jax.random.normal(ks[4], (D_MODEL, D_MODEL), jnp.float32) * s, 'bk': jnp.zeros((D_MODEL,), jnp.float32), 'Wv': jax.random.normal(ks[5], (D_MODEL, D_MODEL), jnp.float32) * s, 'bv': jnp.zeros((D_MODEL,), jnp.float32), 'Wo': jax.random.normal(ks[6], (D_MODEL, D_MODEL), jnp.float32) * s, 'bo': jnp.zeros((D_MODEL,), jnp.float32)}
        return inp
    _L0_xattn_all = _L0_xattn_setup()
    _L0_xattn_in = {k: v for k, v in _L0_xattn_all.items() if k in ('Wq', 'bq', 'Wk', 'bk', 'Wv', 'bv', 'Wo', 'bo')}
    del _L0_xattn_all

    def _L0_ffn_setup():
        import jax, jax.numpy as jnp
        import numpy as np
        NUM_EXPERTS = 8
        TOP_K = 2
        NUM_GRIDS = 8
        INV_DENOM = 0.5
        GRID = np.linspace(-1.2, 0.2, NUM_GRIDS).astype(np.float32)
        LN_EPS = 1e-05

        def _layernorm(x, g, b):
            mu = x.mean(-1, keepdims=True)
            var = x.var(-1, keepdims=True)
            return (x - mu) * jax.lax.rsqrt(var + LN_EPS) * g + b

        def _rswaf(x, grid):
            t = jnp.tanh((x[..., None] - grid) * INV_DENOM)
            return 1.0 - t * t
        key = jax.random.key(seed)
        ks = jax.random.split(key, 8)
        B, S, H, F = (1, 512, 256, 1024)
        F2 = F // 2
        E2 = NUM_EXPERTS // 2
        G = NUM_GRIDS
        s = 0.02
        return {'hidden_states': jax.random.normal(ks[0], (B, S, H), jnp.float32), 'gate_W': jax.random.normal(ks[1], (H, NUM_EXPERTS), jnp.float32) * s, 'mlp_W1': jax.random.normal(ks[2], (E2, H, F), jnp.float32) * s, 'mlp_b1': jnp.zeros((E2, F), jnp.float32), 'mlp_W2': jax.random.normal(ks[3], (E2, F, H), jnp.float32) * s, 'mlp_b2': jnp.zeros((E2, H), jnp.float32), 'kan_ln_g0': jnp.ones((E2, H), jnp.float32), 'kan_ln_b0': jnp.zeros((E2, H), jnp.float32), 'kan_sl_W0': jax.random.normal(ks[4], (E2, H * G, F2), jnp.float32) * s, 'kan_sl_b0': jnp.zeros((E2, F2), jnp.float32), 'kan_ln_g1': jnp.ones((E2, F2), jnp.float32), 'kan_ln_b1': jnp.zeros((E2, F2), jnp.float32), 'kan_sl_W1': jax.random.normal(ks[5], (E2, F2 * G, H), jnp.float32) * s, 'kan_sl_b1': jnp.zeros((E2, H), jnp.float32)}
    _L0_ffn_all = _L0_ffn_setup()
    _L0_ffn_in = {k: v for k, v in _L0_ffn_all.items() if k in ('gate_W', 'mlp_W1', 'mlp_b1', 'mlp_W2', 'mlp_b2', 'kan_ln_g0', 'kan_ln_b0', 'kan_sl_W0', 'kan_sl_b0', 'kan_ln_g1', 'kan_ln_b1', 'kan_sl_W1', 'kan_sl_b1')}
    del _L0_ffn_all
    return {'x': x, 'ctx_1024': ctx_1024, 'mask_Bx1xSxS2_if1': mask_Bx1xSxS2_if1, 'L0_attn_ln_scale': _L0_attn_in['ln_scale'], 'L0_attn_ln_bias': _L0_attn_in['ln_bias'], 'L0_attn_w_qkv': _L0_attn_in['w_qkv'], 'L0_attn_w_proj': _L0_attn_in['w_proj'], 'L0_attn_b_proj': _L0_attn_in['b_proj'], 'L0_xattn_Wq': _L0_xattn_in['Wq'], 'L0_xattn_bq': _L0_xattn_in['bq'], 'L0_xattn_Wk': _L0_xattn_in['Wk'], 'L0_xattn_bk': _L0_xattn_in['bk'], 'L0_xattn_Wv': _L0_xattn_in['Wv'], 'L0_xattn_bv': _L0_xattn_in['bv'], 'L0_xattn_Wo': _L0_xattn_in['Wo'], 'L0_xattn_bo': _L0_xattn_in['bo'], 'L0_ffn_gate_W': _L0_ffn_in['gate_W'], 'L0_ffn_mlp_W1': _L0_ffn_in['mlp_W1'], 'L0_ffn_mlp_b1': _L0_ffn_in['mlp_b1'], 'L0_ffn_mlp_W2': _L0_ffn_in['mlp_W2'], 'L0_ffn_mlp_b2': _L0_ffn_in['mlp_b2'], 'L0_ffn_kan_ln_g0': _L0_ffn_in['kan_ln_g0'], 'L0_ffn_kan_ln_b0': _L0_ffn_in['kan_ln_b0'], 'L0_ffn_kan_sl_W0': _L0_ffn_in['kan_sl_W0'], 'L0_ffn_kan_sl_b0': _L0_ffn_in['kan_sl_b0'], 'L0_ffn_kan_ln_g1': _L0_ffn_in['kan_ln_g1'], 'L0_ffn_kan_ln_b1': _L0_ffn_in['kan_ln_b1'], 'L0_ffn_kan_sl_W1': _L0_ffn_in['kan_sl_W1'], 'L0_ffn_kan_sl_b1': _L0_ffn_in['kan_sl_b1']}

def reference(x, ctx_1024, mask_Bx1xSxS2_if1, L0_attn_ln_scale, L0_attn_ln_bias, L0_attn_w_qkv, L0_attn_w_proj, L0_attn_b_proj, L0_xattn_Wq, L0_xattn_bq, L0_xattn_Wk, L0_xattn_bk, L0_xattn_Wv, L0_xattn_bv, L0_xattn_Wo, L0_xattn_bo, L0_ffn_gate_W, L0_ffn_mlp_W1, L0_ffn_mlp_b1, L0_ffn_mlp_W2, L0_ffn_mlp_b2, L0_ffn_kan_ln_g0, L0_ffn_kan_ln_b0, L0_ffn_kan_sl_W0, L0_ffn_kan_sl_b0, L0_ffn_kan_ln_g1, L0_ffn_kan_ln_b1, L0_ffn_kan_sl_W1, L0_ffn_kan_sl_b1):
    import jax
    import jax.numpy as jnp

    def _L0_attn_ref(z, ln_scale, ln_bias, w_qkv, w_proj, b_proj):
        import jax, jax.numpy as jnp
        import numpy as np
        B, N, D, H = (2, 512, 256, 16)
        HD = D // H
        SCALING = (D / H) ** 0.5
        EPS = 1e-05
        b, n, d = z.shape
        mu = jnp.mean(z, axis=-1, keepdims=True)
        var = jnp.mean(jnp.square(z - mu), axis=-1, keepdims=True)
        zn = (z - mu) / jnp.sqrt(var + EPS) * ln_scale + ln_bias
        qkv = zn @ w_qkv
        qkv5 = qkv.reshape(b, n, H, HD, 3)
        q = jnp.transpose(qkv5[..., 0], (0, 2, 1, 3))
        k = jnp.transpose(qkv5[..., 1], (0, 2, 1, 3))
        v = jnp.transpose(qkv5[..., 2], (0, 2, 1, 3))
        scores = jnp.einsum('bhqd,bhkd->bhqk', q, k) / SCALING
        att = jax.nn.softmax(scores, axis=-1)
        out = jnp.einsum('bhal,bhlv->bhav', att, v)
        out = jnp.transpose(out, (0, 2, 1, 3)).reshape(b, n, d)
        out = out @ w_proj + b_proj
        return z + out

    def _L0_xattn_ref(q, k, v, mask, Wq, bq, Wk, bk, Wv, bv, Wo, bo):
        import jax, jax.numpy as jnp
        import numpy as np
        D_MODEL = 256
        HEADS = 16
        D_K = D_MODEL // HEADS
        BS, SEQ = (4, 512)
        bs = q.shape[0]

        def proj(x, W, b):
            y = jnp.einsum('bsd,ed->bse', x, W) + b
            return y.reshape(bs, -1, HEADS, D_K).transpose(0, 2, 1, 3)
        qh, kh, vh = (proj(q, Wq, bq), proj(k, Wk, bk), proj(v, Wv, bv))
        scores = jnp.einsum('bhqd,bhkd->bhqk', qh, kh) / jnp.sqrt(jnp.float32(D_K))
        scores = jnp.where(mask == 0, jnp.float32(-1000000000.0), scores)
        attn = jax.nn.softmax(scores, axis=-1)
        out = jnp.einsum('bhqk,bhkd->bhqd', attn, vh)
        concat = out.transpose(0, 2, 1, 3).reshape(bs, -1, D_MODEL)
        return jnp.einsum('bsd,ed->bse', concat, Wo) + bo

    def _L0_ffn_ref(hidden_states, gate_W, mlp_W1, mlp_b1, mlp_W2, mlp_b2, kan_ln_g0, kan_ln_b0, kan_sl_W0, kan_sl_b0, kan_ln_g1, kan_ln_b1, kan_sl_W1, kan_sl_b1):
        import jax, jax.numpy as jnp
        import numpy as np
        NUM_EXPERTS = 8
        TOP_K = 2
        NUM_GRIDS = 8
        INV_DENOM = 0.5
        GRID = np.linspace(-1.2, 0.2, NUM_GRIDS).astype(np.float32)
        LN_EPS = 1e-05

        def _layernorm(x, g, b):
            mu = x.mean(-1, keepdims=True)
            var = x.var(-1, keepdims=True)
            return (x - mu) * jax.lax.rsqrt(var + LN_EPS) * g + b

        def _rswaf(x, grid):
            t = jnp.tanh((x[..., None] - grid) * INV_DENOM)
            return 1.0 - t * t
        B, S, H = hidden_states.shape
        E2, _, F2 = (kan_sl_W0.shape[0], kan_sl_W0.shape[1], kan_sl_W0.shape[2])
        G = NUM_GRIDS
        x = hidden_states.reshape(-1, H)
        T = x.shape[0]
        logits = x @ gate_W
        probs = jax.nn.softmax(logits.astype(jnp.float32), axis=-1)
        rw, sel = jax.lax.top_k(probs, TOP_K)
        rw = rw / rw.sum(axis=-1, keepdims=True)
        w_full = jnp.sum(jax.nn.one_hot(sel, NUM_EXPERTS, dtype=rw.dtype) * rw[..., None], axis=1)
        w_full = w_full.astype(x.dtype)
        h = jnp.einsum('th,ehf->etf', x, mlp_W1) + mlp_b1[:, None, :]
        h = jax.nn.gelu(h, approximate=False)
        mlp_out = jnp.einsum('etf,efh->eth', h, mlp_W2) + mlp_b2[:, None, :]
        grid = jnp.asarray(GRID)
        h0 = _layernorm(x[None], kan_ln_g0[:, None, :], kan_ln_b0[:, None, :])
        basis0 = _rswaf(h0, grid).reshape(E2, T, H * G)
        z = jnp.einsum('eti,eio->eto', basis0, kan_sl_W0) + kan_sl_b0[:, None, :]
        h1 = _layernorm(z, kan_ln_g1[:, None, :], kan_ln_b1[:, None, :])
        basis1 = _rswaf(h1, grid).reshape(E2, T, F2 * G)
        kan_out = jnp.einsum('eti,eio->eto', basis1, kan_sl_W1) + kan_sl_b1[:, None, :]
        expert_out = jnp.concatenate([mlp_out, kan_out], axis=0)
        out = jnp.einsum('eth,te->th', expert_out, w_full)
        return out.reshape(B, S, H)
    x = x + _L0_attn_ref(_layernorm(x, axis=-1), L0_attn_ln_scale, L0_attn_ln_bias, L0_attn_w_qkv, L0_attn_w_proj, L0_attn_b_proj)
    x = x + _L0_xattn_ref(_layernorm(x, axis=-1), ctx_1024, ctx_1024, mask_Bx1xSxS2_if1, L0_xattn_Wq, L0_xattn_bq, L0_xattn_Wk, L0_xattn_bk, L0_xattn_Wv, L0_xattn_bv, L0_xattn_Wo, L0_xattn_bo)
    x = x + _L0_ffn_ref(_layernorm(x, axis=-1), L0_ffn_gate_W, L0_ffn_mlp_W1, L0_ffn_mlp_b1, L0_ffn_mlp_W2, L0_ffn_mlp_b2, L0_ffn_kan_ln_g0, L0_ffn_kan_ln_b0, L0_ffn_kan_sl_W0, L0_ffn_kan_sl_b0, L0_ffn_kan_ln_g1, L0_ffn_kan_ln_b1, L0_ffn_kan_sl_W1, L0_ffn_kan_sl_b1)
    return x

_drawn_inputs = setup_inputs


def setup_inputs(seed=0):
    import zlib

    import numpy as np

    out = dict(_drawn_inputs(seed))
    spreads = {'L0_attn_ln_scale': (1.0, 0.2),
     'L0_attn_ln_bias': (0.0, 0.1),
     'L0_attn_b_proj': (0.0, 0.1),
     'L0_xattn_bq': (0.0, 0.315),
     'L0_xattn_bk': (0.0, 2.0),
     'L0_xattn_bv': (0.0, 0.1),
     'L0_xattn_bo': (0.0, 0.1),
     'L0_ffn_mlp_b1': (0.0, 0.8),
     'L0_ffn_mlp_b2': (0.0, 0.35),
     'L0_ffn_kan_ln_g0': (1.0, 0.6),
     'L0_ffn_kan_ln_b0': (0.0, 2.0),
     'L0_ffn_kan_sl_b0': (0.0, 0.638),
     'L0_ffn_kan_ln_g1': (1.0, 0.6),
     'L0_ffn_kan_ln_b1': (0.0, 0.8),
     'L0_ffn_kan_sl_b1': (0.0, 0.352)}
    factors = {}
    for name, (base, spread) in spreads.items():
        noise = np.random.default_rng([zlib.crc32(name.encode()), seed]).standard_normal(out[name].shape)
        drawn = base * np.exp(spread * noise) if base else spread * noise
        out[name] = jnp.asarray(drawn.astype(out[name].dtype))
    for name, factor in factors.items():
        out[name] = (out[name] * factor).astype(out[name].dtype)
    return out
```

```python
from contextlib import ExitStack

import numpy as np

import concourse.bass as bass
from concourse import mybir

F32 = mybir.dt.float32
F32R = mybir.dt.float32r
BF16 = mybir.dt.bfloat16
I32 = mybir.dt.int32
U32 = mybir.dt.uint32
ALU = mybir.AluOpType
ACT = mybir.ActivationFunctionType
AX_X = mybir.AxisListType.X

P = 128
B, S, D = 4, 512, 256
TT = S // P
NT = B * TT
KC = D // P
H, HD = 16, 16
HP = H // 2
HG = H // 4
REP = 4
PAD = 32
EPS = 1e-5
MASKED = -2.0 ** 30
SCORE_SCALE = 1.0 / float(np.sqrt(HD))


class Count:

    def __init__(self, eng, sem, base=0):
        self.eng, self.sem, self.base, self.n = eng, sem, base, 0

    def link(self, ins):
        self.n += 1
        ins.then_inc(self.sem, 1)

    def settle(self):
        self.eng.wait_ge(self.sem, self.base + self.n)


def layer_norm_vector(dve, steps, src, dst, tiles, stats, moments, root, inverse,
                      variance_ready, root_ready, waited, at, last=None):
    for t in range(tiles):
        steps.link(dve.bn_stats(stats[:, t, :], src(t)))
    steps.settle()
    dve.sem_inc(waited, 1)
    for t in range(tiles):
        ins = dve.bn_aggr(moments[:, t, :], stats[:, t, :])
        if t == tiles - 1:
            ins.then_inc(variance_ready, 1)
        else:
            steps.link(ins)
    dve.wait_ge(variance_ready, at)
    dve.wait_ge(root_ready, at)
    steps.link(dve.reciprocal(inverse[:, 0:tiles], root[:, 0:tiles]))
    steps.settle()
    for t in range(tiles):
        ins = dve.tensor_scalar(dst(t), src(t), moments[:, t, 0:1], inverse[:, t:t + 1],
                                ALU.subtract, ALU.mult)
        if t == tiles - 1 and last is not None:
            ins.then_inc(last, 1)
        else:
            steps.link(ins)
    if last is None:
        steps.settle()


def attention(nc, cross, X, psum, const, dram):
    k = "x" if cross else "s"
    SRC = 2 if cross else 1
    HALF = 2
    QH = TT // HALF
    UNITS = H * HALF
    SETS = HG * HALF
    ITEMS = [("K", p) for p in range(HP)] + [("V", t) for t in range(TT)] + [("Q", p) for p in range(HP)]
    KQ = [i for i in ITEMS if i[0] != "V"]
    units = [(g, half, j) for g in range(HG) for half in range(HALF) for j in range(4)]
    LAG_AV = 5
    TURNS = UNITS + 4
    LN = 1 if cross else 2
    STEPS = 3 * TT * LN - 1 + SRC + 2 * HG
    BANKS = 4
    T_BANK, O_BANK, I_BANK = 4, 6, 7

    with ExitStack() as ctx:
        def sb(name, shape, dt=F32):
            return ctx.enter_context(nc.sbuf_tensor(f"{k}_{name}", shape, dt))

        def sem(name):
            return ctx.enter_context(nc.semaphore(f"{k}_{name}"))

        wk_h, wk_l = sb("wk_h", [P, KC, HP, P], F32R), sb("wk_l", [P, KC, HP, P], F32R)
        wq_h, wq_l = sb("wq_h", [P, KC, HP, P], F32R), sb("wq_l", [P, KC, HP, P], F32R)
        wv_h, wv_l = sb("wv_h", [P, KC, D], F32R), sb("wv_l", [P, KC, D], F32R)
        wo_h, wo_l = sb("wo_h", [P, HG, D], F32R), sb("wo_l", [P, HG, D], F32R)
        bias_out = sb("bias_out", [P, D])

        stats = sb("stats", [P, TT, 6])
        moments = sb("moments", [P, TT, 2])
        root, inverse = sb("root", [P, TT]), sb("inverse", [P, TT])
        Z = sb("Z", [P, TT, D])
        residual = sb("residual", [P, TT, D])
        srcT = sb("srcT", [P, KC, S])
        split = [sb("split_a", [P, 2 * KC, S], F32R), sb("split_b", [P, 2 * KC, S], F32R)]
        full = sb("full", [P, 2, S])
        high = sb("high", [P, 2, S], F32R)
        KT = sb("KT", [P, HP, S], F32R)
        QT = sb("QT", [P, H, S], F32R)
        V = sb("V", [P, TT, H, PAD])
        neg_max = sb("neg_max", [P, 2, QH])
        probs = sb("probs", [P, 2, QH, S])
        probsT = sb("probsT", [P, 2, 4, TT, QH * P])
        den, inv_den = sb("den", [P, H, TT]), sb("inv_den", [P, H, TT])
        inv_rows = sb("inv_rows", [P, 2, TT, 4, PAD])
        OT_h, OT_l = split

        weights_in, wo_cleared, wo_placed = sem("weights_in"), sem("wo_cleared"), sem("wo_placed")
        w_transposed, prep, cleared = sem("w_transposed"), sem("prep"), sem("cleared")
        step = sem("step")
        variance_ready, root_ready = sem("variance_ready"), sem("root_ready")
        z_ready, residual_ready, pool_step = sem("z_ready"), sem("residual_ready"), sem("pool_step")
        src_psum, srcT_ready, split_ready = sem("src_psum"), sem("srcT_ready"), sem("split_ready")
        item_psum, kq_out, kq_ready, v_ready = sem("item_psum"), sem("kq_out"), sem("kq_ready"), sem("v_ready")
        scores_ready, max_ready, probs_ready = sem("scores_ready"), sem("max_ready"), sem("probs_ready")
        probsT_psum, probsT_v, probsT_s = sem("probsT_psum"), sem("probsT_v"), sem("probsT_s")
        av_ready, o_out = sem("av_ready"), sem("o_out")
        inv_ready, inv_rows_ready, inv_psum = sem("inv_ready"), sem("inv_rows_ready"), sem("inv_psum")
        norm_ready, out_psum, x_done = sem("norm_ready"), sem("out_psum"), sem("x_done")
        if cross:
            CTX = sb("CTX", [P, TT, D])
            mask = probs[:].rearrange("p a q s -> p (a q) s").bitcast(I32)
            mask_bias = sb("mask_bias", [P, TT, S], BF16)
            bias_kq = sb("bias_kq", [P, 2, HP])
            bias_v = sb("bias_v", [P, D])
            ctx_in, mask_in, mask_ready = sem("ctx_in"), sem("mask_in"), sem("mask_ready")
        else:
            X1 = sb("X1", [P, TT, D])
            ln_affine = sb("ln_affine", [P, 2, KC])

        room = probsT[:].rearrange("p a j t q -> p (a j t q)")
        w_all = room[:, 0:KC * 3 * D].rearrange("p (c e) -> p c e", c=KC)
        wo_pad = room[:, 1536:2560].rearrange("p (g e) -> p g e", g=HG)
        w_nat = [room[:, 2560 + 512 * i:3072 + 512 * i].rearrange("p (c d) -> p c d", c=KC) for i in range(4)]
        wo_cols = room[:, 4608:5632].rearrange("p (c h d) -> p c h d", c=KC, h=H)
        with nc.Block() as block:
            loads = 4 + 16 + 2 if cross else 9

            @block.sync
            def _(sp):
                n = 0

                def load(dst, src):
                    nonlocal n
                    n += 1
                    sp.dma_start(dst, src).then_inc(weights_in, 16)

                if cross:
                    for i, name in enumerate(("Wq", "Wk", "Wv", "Wo")):
                        load(w_nat[i], dram[name].rearrange("(c p) d -> p c d", p=P))
                    for i, name in enumerate(("bq", "bk")):
                        rows = dram[name].rearrange("(p h d) -> h d p", h=2, d=HD)
                        for h in range(2):
                            for r in range(REP):
                                at = 64 * h + HD * r
                                with nc.allow_non_contiguous_dma(reason="256 bias values, once"):
                                    load(bias_kq[at:at + HD, i, :], rows[h])
                    load(bias_v[:], dram["bv"].partition_broadcast(P))
                    load(bias_out[:], dram["bo"].partition_broadcast(P))
                else:
                    load(X[:], dram["x"].rearrange("(t p) d -> p t d", p=P))
                    load(w_all, dram["w_qkv"].rearrange("(c p) e -> p c e", p=P))
                    for i, name in enumerate(("ln_scale", "ln_bias")):
                        with nc.allow_non_contiguous_dma(reason="256 values, once"):
                            load(ln_affine[:, i, :], dram[name].rearrange("(c p) -> p c", p=P))
                    load(bias_out[:], dram["b_proj"].partition_broadcast(P))
                    sp.wait_ge(wo_cleared, 1)
                    rows = dram["w_proj"].rearrange("(g j d) e -> j d g e", g=HG, j=4)
                    for j in range(4):
                        load(wo_pad[PAD * j:PAD * j + HD], rows[j])
                assert n == loads

            @block.tensor
            def _(pe):
                if not cross:
                    return
                pe.wait_ge(weights_in, 16 * loads)
                for i in range(3):
                    for c in range(KC):
                        for e in range(KC):
                            ins = pe.transpose(psum[:, i, (c * KC + e) * P:(c * KC + e + 1) * P],
                                               w_nat[i][:, e, c * P:(c + 1) * P], const["ident"])
                ins.then_inc(w_transposed, 1)
                pe.wait_ge(wo_placed, 1)
                for g in range(HG):
                    for e in range(KC):
                        n = g * KC + e
                        ins = pe.transpose(psum[:, 4 + n // 4, (n % 4) * P:(n % 4 + 1) * P],
                                           wo_cols[:, e, 4 * g:4 * g + 4, :].rearrange("p h d -> p (h d)"),
                                           const["ident"])
                ins.then_inc(w_transposed, 1)

            @block.vector
            def _(dve):
                steps = Count(dve, prep)
                if cross:
                    dve.memset(wo_cols, 0.0).then_inc(wo_cleared, 1)
                    dve.wait_ge(wo_cleared, 1)
                    dve.wait_ge(weights_in, 16 * loads)
                    steps.link(dve.tensor_scalar(bias_kq[:, 0, :], bias_kq[:, 0, :], SCORE_SCALE, None, ALU.mult))
                    for e in range(KC):
                        ins = dve.tensor_copy(wo_cols[:, e, :, 0:HD],
                                              w_nat[3][:, e, :].rearrange("p (h d) -> p h d", h=H))
                    ins.then_inc(wo_placed, 1)
                    dve.wait_ge(w_transposed, 1)
                    for i in range(3):
                        steps.link(dve.tensor_copy(w_all[:, :, i * D:(i + 1) * D],
                                                   psum[:, i, :].rearrange("p (c e) -> p c e", c=KC)))
                    dve.wait_ge(w_transposed, 2)
                    for n in range(2):
                        steps.link(dve.tensor_copy(wo_pad[:, 2 * n:2 * n + 2, :],
                                                   psum[:, 4 + n, :].rearrange("p (g e) -> p g e", g=2)))
                    steps.settle()
                else:
                    dve.memset(wo_pad, 0.0).then_inc(wo_cleared, 1)
                    dve.wait_ge(wo_cleared, 1)
                    dve.wait_ge(weights_in, 16 * loads)

                def split_weight(hi, lo, one):
                    steps.link(dve.tensor_copy(hi, one))
                    steps.settle()
                    steps.link(dve.tensor_tensor(lo, one, hi.bitcast(F32), ALU.subtract))

                for c in range(KC):
                    if cross:
                        w = [w_all[:, c, i * D:(i + 1) * D] for i in range(3)]
                    else:
                        w = [w_all[:, c, :].rearrange("p (e w) -> p e w", w=3)[:, :, i] for i in range(3)]
                    for i, wh, wl in ((0, wq_h, wq_l), (1, wk_h, wk_l)):
                        one = w[i].rearrange("p (h d) -> p h d", h=H)
                        for r in range(REP):
                            split_weight(*(x[:, c, :, :].rearrange("p q (h r d) -> p (q h) r d", h=2, r=REP)[:, :, r, :]
                                           for x in (wh, wl)), one)
                    split_weight(wv_h[:, c, :], wv_l[:, c, :], w[2])
                split_weight(wo_h[:], wo_l[:], wo_pad)
                steps.settle()

            @block.gpsimd
            def _(pool):
                pool.memset(QT[:].bitcast(F32), 0.0).then_inc(cleared, 1)
                pool.memset(V[:], 0.0).then_inc(cleared, 1)
                pool.wait_ge(cleared, 2)

        def source(i):
            s = split[i if cross else 0]
            return s[:, 0:KC, :], s[:, KC:2 * KC, :]

        with nc.Block() as block:
            @block.sync
            def _(sp):
                if not cross:
                    return
                ctx_rows = dram["ctx"].rearrange("(b t p) d -> b p t d", b=B, p=P)
                mask_rows = dram["mask"].rearrange("b (t p) s -> b p t s", p=P)
                sp.dma_start(CTX[:], ctx_rows[0]).then_inc(ctx_in, 16)
                sp.dma_start(mask, mask_rows[0]).then_inc(mask_in, 16)
                with sp.Fori(1, B) as b:
                    sp.wait_ge(src_psum, b * SRC - 1)
                    sp.dma_start(CTX[:], ctx_rows[bass.ds(b, 1)].rearrange("o p t d -> (o p) t d")).then_inc(ctx_in, 16)
                    sp.wait_ge(probsT_psum, b * UNITS)
                    sp.dma_start(mask, mask_rows[bass.ds(b, 1)].rearrange("o p t s -> (o p) t s")).then_inc(mask_in, 16)

            @block.gpsimd
            def _(pool):
                tiles = bias_out[:].unsqueeze(1).to_broadcast([P, TT, D])
                with pool.Fori(0, B) as b:
                    pool.wait_ge(z_ready, b + 1)
                    Xb = X[:, bass.ds(b * TT, TT), :]
                    if cross:
                        pool.tensor_tensor(residual[:], Xb, tiles, ALU.add).then_inc(residual_ready, 1)
                    else:
                        pool.tensor_tensor(residual[:], Xb, X1[:], ALU.add).then_inc(pool_step, 1)
                        pool.wait_ge(pool_step, b + 1)
                        pool.tensor_tensor(residual[:], residual[:], tiles, ALU.add).then_inc(residual_ready, 1)
                    for g in range(HG):
                        pool.wait_ge(inv_ready, b * HG + g + 1)
                        if g >= 2:
                            pool.wait_ge(inv_psum, b * HG + g - 1)
                        pool.sem_inc(const["pool_waited"], 1)
                        pool.tensor_copy(inv_rows[:, g % 2].rearrange("p t j d -> p j t d"),
                                         inv_den[:, 4 * g:4 * g + 4, :].unsqueeze(3).to_broadcast([P, 4, TT, PAD])
                                         ).then_inc(inv_rows_ready, 1)

            @block.tensor
            def _(pe):
                ident, ident_b = const["ident"], const["ident_b"]

                def transposes(b, i, what):
                    if i > 0:
                        pe.wait_ge(srcT_ready, b * SRC + i)
                    for c in range(KC):
                        for t in range(TT):
                            ins = pe.transpose(psum[:, T_BANK + c, t * P:(t + 1) * P],
                                               what[:, t, c * P:(c + 1) * P], ident)
                    ins.then_inc(src_psum, 1)

                def project(b, n):
                    kind, m = ITEMS[n]
                    out = psum[:, n % BANKS, :]
                    if n >= BANKS:
                        last_kind = ITEMS[n - BANKS][0]
                        if last_kind == "V":
                            pe.wait_ge(v_ready, b * TT + ITEMS[n - BANKS][1] + 1)
                        else:
                            pe.wait_ge(kq_out, b * len(KQ) + KQ.index(ITEMS[n - BANKS]) + 1)
                    sh, sl = source(1 if kind == "Q" else 0)
                    if kind == "V":
                        at = slice(m * P, (m + 1) * P)
                        terms = [(sh[:, c, at], w[:, c, :]) for c in range(KC) for w in (wv_h, wv_l)]
                        terms += [(sl[:, c, at], wv_h[:, c, :]) for c in range(KC)]
                        out = out[:, 0:D]
                    else:
                        wh, wl = (wk_h, wk_l) if kind == "K" else (wq_h, wq_l)
                        terms = [(wh[:, c, m, :], s[:, c, :]) for c in range(KC) for s in (sh, sl)]
                        terms += [(wl[:, c, m, :], sh[:, c, :]) for c in range(KC)]
                    for i, (lhsT, rhs) in enumerate(terms):
                        ins = pe.matmul(out, lhsT, rhs, start=(i == 0), stop=(i == len(terms) - 1))
                    ins.then_inc(item_psum, 1)

                def scores(b, u):
                    g, half, j = units[u]
                    h = 4 * g + j
                    if u >= 2:
                        pe.wait_ge(probs_ready, b * UNITS + u - 1)
                    for q in range(QH):
                        t = QH * half + q
                        out = psum[:, 2 * (u % 2) + q, :]
                        ins = pe.matmul(out, QT[:, h, t * P:(t + 1) * P], KT[:, h // 2, :],
                                        start=True, stop=not cross)
                        if cross:
                            ins = pe.matmul(out, ident_b, mask_bias[:, t, :], start=False, stop=True)
                    ins.then_inc(scores_ready, 1)

                def transpose_probs(b, u):
                    pe.wait_ge(probs_ready, b * UNITS + u + 1)
                    if u >= 1:
                        pe.wait_ge(probsT_v, b * UNITS + u)
                        pe.wait_ge(probsT_s, b * UNITS + u)
                    for t in range(TT):
                        for q in range(QH):
                            at = (t % 2) * QH + q
                            ins = pe.transpose(psum[:, T_BANK + t // 2, at * P:(at + 1) * P],
                                               probs[:, u % 2, q, t * P:(t + 1) * P], ident)
                    ins.then_inc(probsT_psum, 1)

                def weighted_values(b, s):
                    g, half = s // HALF, s % HALF
                    pe.wait_ge(probsT_v, b * UNITS + 4 * (s + 1))
                    pe.wait_ge(probsT_s, b * UNITS + 4 * (s + 1))
                    if half == 0 and g > 0:
                        pe.wait_ge(o_out, b * HG + g)
                    for t in range(TT):
                        for j in range(4):
                            ins = pe.matmul(psum[PAD * j:PAD * j + PAD, O_BANK, half * QH * P:(half + 1) * QH * P],
                                            V[:, t, 4 * g + j, :], probsT[:, s % 2, j, t, :],
                                            start=(t == 0), stop=(t == TT - 1),
                                            tile_position=(0, PAD * j))
                    ins.then_inc(av_ready, 1)

                def spread_inverse(b, g):
                    pe.wait_ge(inv_rows_ready, b * HG + g + 1)
                    if g > 0:
                        pe.wait_ge(norm_ready, b * HG + g)
                    for t in range(TT):
                        ins = pe.matmul(psum[:, I_BANK, t * P:(t + 1) * P],
                                        inv_rows[:, g % 2, t].rearrange("p j d -> p (j d)"), ident,
                                        start=True, stop=True)
                    ins.then_inc(inv_psum, 1)

                with pe.Fori(0, B) as b:
                    if cross:
                        pe.wait_ge(ctx_in, b * 16 + 16)
                        transposes(b, 0, CTX)
                    pe.wait_ge(z_ready, b + 1)
                    transposes(b, SRC - 1, Z)
                    pe.wait_ge(split_ready, b * SRC + 1)
                    for n, item in enumerate(ITEMS):
                        if item == ("Q", 0):
                            pe.wait_ge(split_ready, b * SRC + SRC)
                        project(b, n)
                    pe.wait_ge(kq_ready, b * len(KQ) + len(KQ))
                    pe.wait_ge(v_ready, b * TT + TT)
                    if cross:
                        pe.wait_ge(mask_ready, b + 1)
                    for u in range(TURNS):
                        if u < UNITS:
                            scores(b, u)
                        if 1 <= u <= UNITS:
                            transpose_probs(b, u - 1)
                        s, phase = divmod(u - LAG_AV, 4)
                        if phase == 0 and 0 <= s < SETS:
                            weighted_values(b, s)
                            if s % HALF == HALF - 1:
                                spread_inverse(b, s // HALF)
                    pe.wait_ge(norm_ready, b * HG + HG)
                    for t in range(TT):
                        at = slice(t * P, (t + 1) * P)
                        terms = [(OT_h[:, g, at], w[:, g, :]) for g in range(HG) for w in (wo_h, wo_l)]
                        terms += [(OT_l[:, g, at], wo_h[:, g, :]) for g in range(HG)]
                        for i, (lhsT, rhs) in enumerate(terms):
                            ins = pe.matmul(psum[:, t, 0:D], lhsT, rhs, start=(i == 0), stop=(i == len(terms) - 1))
                        ins.then_inc(out_psum, 1)

            @block.scalar
            def _(act):
                def transposed(b, i):
                    act.wait_ge(src_psum, b * SRC + i + 1)
                    if i > 0:
                        act.wait_ge(split_ready, b * SRC + i)
                    for c in range(KC):
                        if cross:
                            ins = act.copy(srcT[:, c, :], psum[:, T_BANK + c, :])
                        else:
                            ins = act.activation(srcT[:, c, :], psum[:, T_BANK + c, :], ACT.Identity,
                                                 bias=ln_affine[:, 1, c:c + 1], scale=ln_affine[:, 0, c:c + 1])
                    ins.then_inc(srcT_ready, 1)

                def root_of_variance(b, i):
                    act.wait_ge(variance_ready, b * LN + i + 1)
                    act.activation(root[:], moments[:, :, 1], ACT.Sqrt, bias=const["eps"]).then_inc(root_ready, 1)

                with act.Fori(0, B) as b:
                    if cross:
                        transposed(b, 0)
                    for i in range(LN):
                        root_of_variance(b, i)
                    transposed(b, SRC - 1)
                    for n, (kind, p) in enumerate(ITEMS):
                        if kind == "V":
                            continue
                        m = KQ.index((kind, p))
                        act.wait_ge(item_psum, b * len(ITEMS) + n + 1)
                        if m >= 2:
                            act.wait_ge(kq_ready, b * len(KQ) + m - 1)
                        for out in (full[:, m % 2, :], high[:, m % 2, :]):
                            scale = SCORE_SCALE if kind == "Q" else 1.0
                            if cross:
                                i = 0 if kind == "Q" else 1
                                ins = act.activation(out, psum[:, n % BANKS, :], ACT.Identity,
                                                     bias=bias_kq[:, i, p:p + 1], scale=scale)
                            else:
                                ins = act.activation(out, psum[:, n % BANKS, :], ACT.Copy, scale=scale)
                        ins.then_inc(kq_out, 1)
                    for u in range(TURNS):
                        if u < UNITS:
                            g, half, j = units[u]
                            act.wait_ge(max_ready, b * UNITS + u + 1)
                            if u >= 2:
                                act.wait_ge(probsT_psum, b * UNITS + u - 1)
                            for q in range(QH):
                                t = QH * half + q
                                ins = act.activation(probs[:, u % 2, q, :], psum[:, 2 * (u % 2) + q, :], ACT.Exp,
                                                     bias=neg_max[:, u % 2, q:q + 1],
                                                     accum_out=den[:, 4 * g + j, t:t + 1])
                            ins.then_inc(probs_ready, 1)
                        if 1 <= u <= UNITS:
                            v = u - 1
                            act.wait_ge(probsT_psum, b * UNITS + v + 1)
                            if v >= 8:
                                act.wait_ge(av_ready, b * SETS + v // 4 - 1)
                            act.copy(probsT[:, v // 4 % 2, v % 4, 2:4, :],
                                     psum[:, T_BANK + 1, :].rearrange("p (t q) -> p t q", t=2)).then_inc(probsT_s, 1)
                        s, phase = divmod(u - LAG_AV, 4)
                        if phase == 1 and 0 <= s < SETS and s % HALF == HALF - 1:
                            g = s // HALF
                            act.wait_ge(av_ready, b * SETS + s + 1)
                            if g >= 2:
                                act.wait_ge(norm_ready, b * HG + g - 1)
                            act.copy(full[:, g % 2, :], psum[:, O_BANK, :]).then_inc(o_out, 1)

            @block.vector
            def _(dve):
                neg_low, low_first = const["neg_low_rows"], const["neg_low_halves"]
                bias_v_heads = bias_v[:].rearrange("p (h d) -> p h d", h=H) if cross else None

                def norm_group(b, steps, g):
                    out, at = full[:, g % 2, :], slice(g, g + 1)
                    dve.wait_ge(o_out, b * HG + g + 1)
                    dve.wait_ge(inv_psum, b * HG + g + 1)
                    steps.link(dve.tensor_tensor(out, out, psum[:, I_BANK, :], ALU.mult))
                    steps.settle()
                    steps.link(dve.tensor_copy(OT_h[:, g, :], out))
                    steps.settle()
                    dve.tensor_tensor(OT_l[:, g, :], out, OT_h[:, g, :].bitcast(F32), ALU.subtract).then_inc(norm_ready, 1)

                with dve.Fori(0, B) as b:
                    steps = Count(dve, step, b * STEPS)
                    Xt = lambda t: X[:, bass.ds(b * TT + t, 1), :].rearrange("p o d -> p (o d)")
                    Zt = lambda t: Z[:, t, :]
                    norm = (dve, steps)
                    rooms = (stats, moments, root, inverse, variance_ready, root_ready, const["vector_waited"])
                    if cross:
                        layer_norm_vector(*norm, Xt, Zt, TT, *rooms, b + 1, z_ready)
                        dve.wait_ge(mask_in, b * 16 + 16)
                        dve.tensor_scalar(mask_bias[:], mask, 0.0, MASKED, ALU.is_equal, ALU.mult).then_inc(mask_ready, 1)
                    else:
                        X1t = lambda t: X1[:, t, :]
                        layer_norm_vector(*norm, Xt, X1t, TT, *rooms, b * 2 + 1)
                        layer_norm_vector(*norm, X1t, Zt, TT, *rooms, b * 2 + 2, z_ready)
                    for i in range(SRC):
                        dve.wait_ge(srcT_ready, b * SRC + i + 1)
                        sh, sl = source(i)
                        steps.link(dve.tensor_copy(sh, srcT[:]))
                        steps.settle()
                        dve.tensor_tensor(sl, srcT[:], sh.bitcast(F32), ALU.subtract).then_inc(split_ready, 1)
                    for n, (kind, m) in enumerate(ITEMS):
                        if kind == "V":
                            dve.wait_ge(item_psum, b * len(ITEMS) + n + 1)
                            out, src = V[:, m, :, 0:HD], psum[:, n % BANKS, 0:D].rearrange("p (h d) -> p h d", h=H)
                            if cross:
                                ins = dve.tensor_tensor(out, src, bias_v_heads, ALU.add)
                            else:
                                ins = dve.tensor_copy(out, src)
                            ins.then_inc(v_ready, 1)
                            continue
                        i = KQ.index((kind, m))
                        dve.wait_ge(kq_out, b * len(KQ) + i + 1)
                        hi, all_ = high[:, i % 2, :].bitcast(F32), full[:, i % 2, :]
                        if kind == "K":
                            ins = dve.scalar_tensor_tensor(KT[:, m, :], hi, neg_low, all_, ALU.mult, ALU.add)
                        else:
                            for h in range(2):
                                at = slice(64 * h, 64 * h + 64)
                                ins = dve.scalar_tensor_tensor(QT[at, 2 * m + h, :], hi[at], low_first[at], all_[at],
                                                               ALU.mult, ALU.add)
                        ins.then_inc(kq_ready, 1)
                    for u in range(TURNS):
                        if u < UNITS:
                            dve.wait_ge(scores_ready, b * UNITS + u + 1)
                            dve.tensor_reduce(neg_max[:, u % 2, :], psum[:, 2 * (u % 2):2 * (u % 2) + 2, :], AX_X,
                                              ALU.max, negate=True).then_inc(max_ready, 1)
                        if 1 <= u <= UNITS:
                            v = u - 1
                            dve.wait_ge(probsT_psum, b * UNITS + v + 1)
                            if v >= 8:
                                dve.wait_ge(av_ready, b * SETS + v // 4 - 1)
                            dve.tensor_copy(probsT[:, v // 4 % 2, v % 4, 0:2, :],
                                            psum[:, T_BANK, :].rearrange("p (t q) -> p t q", t=2)).then_inc(probsT_v, 1)
                        if u >= 8 and u % 8 == 0:
                            g = u // 8 - 1
                            at = slice(4 * g, 4 * g + 4)
                            dve.wait_ge(probs_ready, b * UNITS + 8 * g + 8)
                            dve.reciprocal(inv_den[:, at, :], den[:, at, :]).then_inc(inv_ready, 1)
                        if u >= 11 and (u - 11) % 8 == 0:
                            norm_group(b, steps, (u - 11) // 8)
                    dve.wait_ge(residual_ready, b + 1)
                    for t in range(TT):
                        dve.wait_ge(out_psum, b * TT + t + 1)
                        dve.tensor_tensor(Xt(t), psum[:, t, 0:D], residual[:, t, :], ALU.add).then_inc(x_done, 1)
                    assert steps.n == STEPS, (steps.n, STEPS)


E = 4
F = 1024
FC = F // P
F2 = 512
C2 = F2 // P
G = 8
GRID = np.linspace(-1.2, 0.2, G).astype(np.float32)
N8 = 2 * E


def experts(nc, X, psum, const, dram):
    with ExitStack() as ctx:
        share = ctx.enter_context(nc.sbuf_tensor("share", [P, NT, N8], F32))
        h0T_dram = nc.dram_tensor("h0T_scratch", (B, P, KC * S), F32).ap()
        with ExitStack() as inner:
            hT_h = inner.enter_context(nc.sbuf_tensor("hT_h", [P, KC, NT * P], F32R))
            hT_l = inner.enter_context(nc.sbuf_tensor("hT_l", [P, KC, NT * P], F32R))
            route(nc, X, psum, const, dram, share, hT_h, hT_l, h0T_dram)
            mlp_experts(nc, X, psum, const, dram, share, hT_h, hT_l)
        kan_experts(nc, X, psum, const, dram, share, h0T_dram)


def route(nc, X, psum, const, dram, share, hT_h, hT_l, h0T_dram):
    LN = 2
    STEPS = LN * (3 * TT - 1) + 1 + 2 + 2 * TT + 4 + (2 * TT - 1) + 1
    with ExitStack() as ctx:
        def sb(name, shape, dt=F32):
            return ctx.enter_context(nc.sbuf_tensor(f"r_{name}", shape, dt))

        def sem(name):
            return ctx.enter_context(nc.semaphore(f"r_{name}"))

        gate = sb("gate", [P, KC, N8])
        bias8 = sb("bias8", [N8, D])
        stats, moments = sb("stats", [P, TT, 6]), sb("moments", [P, TT, 2])
        root, inverse = sb("root", [P, TT]), sb("inverse", [P, TT])
        Hn, H0 = sb("Hn", [P, TT, D]), sb("H0", [P, TT, D])
        hT, h0T = sb("hT", [P, KC, S]), sb("h0T", [P, KC, S])
        neg_top, total, inv_total = sb("neg_top", [P, TT]), sb("total", [P, TT]), sb("inv_total", [P, TT])
        expd, chance = sb("expd", [P, TT, N8]), sb("chance", [P, TT, N8])
        best, where = sb("best", [P, TT, 8]), sb("where", [P, TT, 8], U32)
        where_f = sb("where_f", [P, TT, 2])
        pair_sum, pair_inv, pair_share = sb("pair_sum", [P, TT]), sb("pair_inv", [P, TT]), sb("pair_share", [P, TT, 2])
        picked, shares = sb("picked", [P, 2, N8]), sb("shares", [P, TT, N8])
        sharesT = sb("sharesT", [N8, TT, P])

        weights_in, step = sem("weights_in"), sem("step")
        variance_ready, root_ready = sem("variance_ready"), sem("root_ready")
        h_ready, h0_ready, hT_psum, hT_ready = sem("h_ready"), sem("h0_ready"), sem("hT_psum"), sem("hT_ready")
        split_ready, stored = sem("split_ready"), sem("stored")
        logits_psum, top_ready, exp_ready = sem("logits_psum"), sem("top_ready"), sem("exp_ready")
        shares_ready, sharesT_psum, sharesT_ready = sem("shares_ready"), sem("sharesT_psum"), sem("sharesT_ready")
        bias_psum, x_done = sem("bias_psum"), sem("x_done")

        with nc.Block() as block:
            @block.sync
            def _(sp):
                with nc.allow_non_contiguous_dma(reason="the gate, once"):
                    sp.dma_start(gate[:], dram["gate_W"].rearrange("(c p) e -> p c e", p=P)).then_inc(weights_in, 16)
                sp.dma_start(bias8[0:E, :], dram["mlp_b2"]).then_inc(weights_in, 16)
                sp.dma_start(bias8[E:N8, :], dram["kan_sl_b1"]).then_inc(stored, 16)
                with sp.Fori(0, B) as b:
                    sp.wait_ge(hT_ready, b * 2 + 2)
                    sp.dma_start(h0T_dram[bass.ds(b, 1)].rearrange("o p s -> (o p) s"),
                                 h0T[:].rearrange("p c s -> p (c s)")).then_inc(stored, 16)
                sp.wait_ge(stored, 16 * B + 16)

            @block.tensor
            def _(pe):
                ident = const["ident"]
                pe.wait_ge(weights_in, 32)
                pe.wait_ge(stored, 16)
                with pe.Fori(0, B) as b:
                    for i, (src, ready) in enumerate(((Hn, h_ready), (H0, h0_ready))):
                        pe.wait_ge(ready, b + 1)
                        for c in range(KC):
                            for t in range(TT):
                                ins = pe.transpose(psum[:, 2 * i + c, t * P:(t + 1) * P],
                                                   src[:, t, c * P:(c + 1) * P], ident)
                        ins.then_inc(hT_psum, 1)
                    pe.wait_ge(hT_ready, b * 2 + 1)
                    for t in range(TT):
                        for c in range(KC):
                            ins = pe.matmul(psum[:, 4, t * N8:(t + 1) * N8], hT[:, c, t * P:(t + 1) * P],
                                            gate[:, c, :], start=(c == 0), stop=(c == KC - 1))
                    ins.then_inc(logits_psum, 1)
                    pe.wait_ge(shares_ready, b + 1)
                    for t in range(TT):
                        ins = pe.transpose(psum[0:N8, 5, t * P:(t + 1) * P], shares[:, t, :], ident)
                    ins.then_inc(sharesT_psum, 1)
                    pe.wait_ge(sharesT_ready, b + 1)
                    for t in range(TT):
                        ins = pe.matmul(psum[:, 6 + t // 2, t % 2 * D:(t % 2 + 1) * D], sharesT[:, t, :], bias8[:],
                                        start=True, stop=True)
                    ins.then_inc(bias_psum, 1)

            @block.scalar
            def _(act):
                with act.Fori(0, B) as b:
                    for i in range(LN):
                        act.wait_ge(variance_ready, b * LN + i + 1)
                        act.activation(root[:], moments[:, :, 1], ACT.Sqrt, bias=const["eps"]).then_inc(root_ready, 1)
                    for i, out in enumerate((hT, h0T)):
                        act.wait_ge(hT_psum, b * 2 + i + 1)
                        if i == 1:
                            act.wait_ge(stored, b * 16 + 16)
                        act.copy(out[:], psum[:, 2 * i:2 * i + 2, :]).then_inc(hT_ready, 1)
                    act.wait_ge(top_ready, b + 1)
                    for t in range(TT):
                        ins = act.activation(expd[:, t, :], psum[:, 4, t * N8:(t + 1) * N8], ACT.Exp,
                                             bias=neg_top[:, t:t + 1], accum_out=total[:, t:t + 1])
                    ins.then_inc(exp_ready, 1)
                    act.wait_ge(sharesT_psum, b + 1)
                    act.copy(sharesT[:].rearrange("e t p -> e (t p)"), psum[0:N8, 5, :]).then_inc(sharesT_ready, 1)

            @block.vector
            def _(dve):
                experts_row, signs = const["experts"], const["signs"]
                with dve.Fori(0, B) as b:
                    steps = Count(dve, step, b * STEPS)

                    def settled(ins):
                        steps.link(ins)
                        steps.settle()

                    Xt = lambda t: X[:, bass.ds(b * TT + t, 1), :].rearrange("p o d -> p (o d)")
                    rooms = (stats, moments, root, inverse, variance_ready, root_ready, const["vector_waited"])
                    layer_norm_vector(dve, steps, Xt, lambda t: Hn[:, t, :], TT, *rooms, b * LN + 1, h_ready)
                    dve.wait_ge(h_ready, b + 1)
                    layer_norm_vector(dve, steps, lambda t: Hn[:, t, :], lambda t: H0[:, t, :], TT, *rooms,
                                      b * LN + 2, h0_ready)
                    dve.wait_ge(hT_ready, b * 2 + 1)
                    at = bass.ds(b * S, S)
                    settled(dve.tensor_copy(hT_h[:, :, at], hT[:]))
                    dve.tensor_tensor(hT_l[:, :, at], hT[:], hT_h[:, :, at].bitcast(F32), ALU.subtract).then_inc(split_ready, 1)
                    dve.wait_ge(logits_psum, b + 1)
                    logits = psum[:, 4, 0:TT * N8].rearrange("p (t e) -> p t e", t=TT)
                    dve.tensor_reduce(neg_top[:], logits, AX_X, ALU.max, negate=True).then_inc(top_ready, 1)
                    dve.wait_ge(exp_ready, b + 1)
                    settled(dve.reciprocal(inv_total[:], total[:]))
                    steps.link(dve.tensor_tensor(chance[:], expd[:],
                                                 inv_total[:].unsqueeze(2).to_broadcast([P, TT, N8]), ALU.mult))
                    steps.settle()
                    dve.sem_inc(const["vector_waited"], 1)
                    for t in range(TT):
                        steps.link(dve.max(best[:, t, :], chance[:, t, :]))
                    steps.settle()
                    dve.sem_inc(const["vector_waited"], 1)
                    for t in range(TT):
                        steps.link(dve.max_index(where[:, t, :], best[:, t, :], chance[:, t, :]))
                    steps.settle()
                    settled(dve.tensor_copy(where_f[:], where[:, :, 0:2]))
                    settled(dve.tensor_tensor(pair_sum[:], best[:, :, 0], best[:, :, 1], ALU.add))
                    settled(dve.reciprocal(pair_inv[:], pair_sum[:]))
                    settled(dve.tensor_tensor(pair_share[:], best[:, :, 0:2],
                                              pair_inv[:].unsqueeze(2).to_broadcast([P, TT, 2]), ALU.mult))
                    for t in range(TT):
                        for i in range(2):
                            ins = dve.tensor_scalar(picked[:, i, :], experts_row, where_f[:, t, i:i + 1],
                                                    pair_share[:, t, i:i + 1], ALU.is_equal, ALU.mult)
                            if i == 1:
                                settled(ins)
                            else:
                                ins.then_inc(split_ready, 1)
                        ins = dve.tensor_tensor(shares[:, t, :], picked[:, 0, :], picked[:, 1, :], ALU.add)
                        if t == TT - 1:
                            ins.then_inc(shares_ready, 1)
                        else:
                            settled(ins)
                    dve.wait_ge(shares_ready, b + 1)
                    settled(dve.tensor_tensor(share[:, bass.ds(b * TT, TT), :], shares[:],
                                              signs.unsqueeze(1).to_broadcast([P, TT, N8]), ALU.mult))
                    dve.wait_ge(bias_psum, b + 1)
                    Xb = X[:, bass.ds(b * TT, TT), :]
                    dve.tensor_tensor(Xb, Xb, psum[:, 6:8, :].rearrange("p k (t d) -> p (k t) d", d=D),
                                      ALU.add).then_inc(x_done, 1)
                    assert steps.n == STEPS, (steps.n, STEPS)


def mlp_experts(nc, X, psum, const, dram, share, hT_h, hT_l):
    TURNS = E * B
    LAG = 2
    RING = 3
    UP_BANKS, DOWN_BANK = 4, 4
    CH = KC * P
    with ExitStack() as ctx:
        def sb(name, shape, dt=F32):
            return ctx.enter_context(nc.sbuf_tensor(f"m_{name}", shape, dt))

        def sem(name):
            return ctx.enter_context(nc.semaphore(f"m_{name}"))

        w1_h, w1_l = sb("w1_h", [P, FC, KC, P], F32R), sb("w1_l", [P, FC, KC, P], F32R)
        w2_h, w2_l = sb("w2_h", [P, FC, D], F32R), sb("w2_l", [P, FC, D], F32R)
        raw = sb("raw", [P, 2, FC, CH])
        b1 = sb("b1", [P, E, FC])
        hidden = sb("hidden", [P, 2, S])
        hid_h, hid_l = sb("hid_h", [P, 4, S], F32R), sb("hid_l", [P, 4, S], F32R)

        b1_in, w1_in, w2_in = sem("b1_in"), sem("w1_in"), sem("w2_in")
        high_ready, w1_ready, w2_ready = sem("high_ready"), sem("w1_ready"), sem("w2_ready")
        up_psum, gelu_ready, high_hidden, hidden_ready = (
            sem("up_psum"), sem("gelu_ready"), sem("high_hidden"), sem("hidden_ready"))
        down_used, out_ready, x_done = sem("down_used"), sem("out_ready"), sem("x_done")

        with nc.Block() as block:
            @block.sync
            def _(sp):
                with nc.allow_non_contiguous_dma(reason="4096 bias values, once"):
                    sp.dma_start(b1[:], dram["mlp_b1"].rearrange("e (f p) -> p e f", p=P)).then_inc(b1_in, 16)

                def load(e):
                    w1 = dram["mlp_W1"][e].rearrange("(c p) (f n) -> f p c n", p=P, f=FC)
                    w2 = dram["mlp_W2"][e].rearrange("(f p) d -> f p d", p=P)
                    return w1, w2

                w1 = dram["mlp_W1"].rearrange("e (c p) (f n) -> e c p f n", p=P, f=FC)
                w2 = dram["mlp_W2"].rearrange("e (f p) d -> e p f d", p=P)

                def fetch(e, first):
                    if not first:
                        sp.wait_ge(w1_ready, e * FC)
                    for c in range(KC):
                        src = w1[0, c] if first else w1[bass.ds(e, 1), c].rearrange("o p f n -> (o p) f n")
                        sp.dma_start(raw[:, 0].rearrange("p f (c n) -> p f c n", c=KC)[:, :, c, :],
                                     src).then_inc(w1_in, 16)
                    if not first:
                        sp.wait_ge(w2_ready, e * FC)
                    src = w2[0] if first else w2[bass.ds(e, 1)].rearrange("o p f d -> (o p) f d")
                    sp.dma_start(raw[:, 1], src).then_inc(w2_in, 16)

                fetch(0, True)
                with sp.Fori(1, E) as e:
                    fetch(e, False)

            @block.gpsimd
            def _(pool):
                def split_weights(e, first):
                    pool.wait_ge(w1_in, (e + 1) * 16 * KC)
                    pool.wait_ge(w2_in, (e + 1) * 16)
                    for f in range(FC):
                        last = (e * B - 1) * FC + f + 1
                        for i, (hi, lo, ready, used) in enumerate(
                                ((w1_h[:, f].rearrange("p c n -> p (c n)"), w1_l[:, f].rearrange("p c n -> p (c n)"),
                                  w1_ready, up_psum), (w2_h[:, f], w2_l[:, f], w2_ready, down_used))):
                            if not first:
                                pool.wait_ge(used, last)
                            pool.sem_inc(const["pool_waited"], 1)
                            pool.tensor_scalar(hi, raw[:, i, f], 1.0, 0.0, ALU.mult, ALU.add).then_inc(high_ready, 1)
                            pool.wait_ge(high_ready, e * 2 * FC + 2 * f + i + 1)
                            pool.tensor_tensor(lo, raw[:, i, f], hi.bitcast(F32), ALU.subtract).then_inc(ready, 1)

                split_weights(0, True)
                with pool.Fori(1, E) as e:
                    split_weights(e, False)

            @block.tensor
            def _(pe):
                def up(turn, e, batch, f):
                    pe.wait_ge(w1_ready, e * FC + f + 1)
                    n = turn * FC + f
                    if not (isinstance(turn, int) and f < UP_BANKS):
                        pe.wait_ge(gelu_ready, n - UP_BANKS + 1)
                    at = bass.ds(batch * S, S)
                    terms = [(w1_h[:, f, c, :], h[:, c, at]) for c in range(KC) for h in (hT_h, hT_l)]
                    terms += [(w1_l[:, f, c, :], hT_h[:, c, at]) for c in range(KC)]
                    for i, (lhsT, rhs) in enumerate(terms):
                        ins = pe.matmul(psum[:, f % UP_BANKS, :], lhsT, rhs, start=(i == 0), stop=(i == len(terms) - 1))
                    ins.then_inc(up_psum, 1)

                def down(turn, e, f):
                    pe.wait_ge(w2_ready, e * FC + f + 1)
                    pe.wait_ge(hidden_ready, turn * FC + f + 1)
                    if f == 0 and not isinstance(turn, int):
                        pe.wait_ge(x_done, turn * TT)
                    for t in range(TT):
                        out = psum[:, DOWN_BANK + t // 2, t % 2 * D:(t % 2 + 1) * D]
                        at = slice(t * P, (t + 1) * P)
                        for i, (hid, w) in enumerate(((hid_h, w2_h), (hid_h, w2_l), (hid_l, w2_h))):
                            ins = pe.matmul(out, hid[:, f % 4, at], w[:, f, :],
                                            start=(f == 0 and i == 0 and t % 2 == 0), stop=(f == FC - 1 and i == 2),
                                            skip_group_check=True)
                    ins.then_inc(down_used, 1)

                for f in range(FC):
                    up(0, 0, 0, f)
                    if f >= LAG:
                        down(0, 0, f - LAG)
                with pe.Fori(1, TURNS) as turn:
                    e, batch = turn // B, turn % B
                    before, e_before = turn - 1, (turn - 1) // B
                    for f in range(FC):
                        up(turn, e, batch, f)
                        if f >= LAG:
                            down(turn, e, f - LAG)
                        else:
                            down(before, e_before, FC + f - LAG)
                for f in range(FC - LAG, FC):
                    down(TURNS - 1, E - 1, f)

            @block.scalar
            def _(act):
                def gelu(turn, e, f):
                    n = turn * FC + f
                    act.wait_ge(up_psum, n + 1)
                    if not (isinstance(turn, int) and f < 2):
                        act.wait_ge(hidden_ready, n - 1)
                    act.activation(hidden[:, f % 2, :], psum[:, f % UP_BANKS, :], ACT.Gelu,
                                   bias=b1[:, bass.ds(e, 1), f]).then_inc(gelu_ready, 1)

                act.wait_ge(b1_in, 16)
                for f in range(FC):
                    gelu(0, 0, f)
                with act.Fori(1, TURNS) as turn:
                    e = turn // B
                    for f in range(FC):
                        gelu(turn, e, f)

            @block.vector
            def _(dve):
                def split_hidden(turn, f):
                    n = turn * FC + f
                    dve.wait_ge(gelu_ready, n + 1)
                    if not (isinstance(turn, int) and f < 4):
                        dve.wait_ge(down_used, n - 3)
                    dve.tensor_copy(hid_h[:, f % 4, :], hidden[:, f % 2, :]).then_inc(high_hidden, 1)
                    dve.wait_ge(high_hidden, n + 1)
                    dve.tensor_tensor(hid_l[:, f % 4, :], hidden[:, f % 2, :], hid_h[:, f % 4, :].bitcast(F32),
                                      ALU.subtract).then_inc(hidden_ready, 1)

                def add_output(turn, e, batch):
                    dve.wait_ge(down_used, turn * FC + FC)
                    for t in range(TT):
                        tile = batch * TT + t
                        Xt = X[:, bass.ds(tile, 1), :].rearrange("p o d -> p (o d)")
                        dve.scalar_tensor_tensor(Xt, psum[:, DOWN_BANK + t // 2, t % 2 * D:(t % 2 + 1) * D],
                                                 share_flat[:, bass.ds(tile * N8 + e, 1)], Xt,
                                                 ALU.mult, ALU.add).then_inc(x_done, 1)

                share_flat = share[:].rearrange("p t e -> p (t e)")
                for f in range(FC):
                    split_hidden(0, f)
                with dve.Fori(1, TURNS) as turn:
                    for f in range(FC):
                        split_hidden(turn, f)
                        if f == LAG - 1:
                            add_output(turn - 1, (turn - 1) // B, (turn - 1) % B)
                add_output(TURNS - 1, E - 1, B - 1)


def m_parity(layer, p):
    return p % 2


def kan_experts(nc, X, psum, const, dram, share, h0T_dram):
    TURNS = E * B
    PAIRS0, PAIRS1 = KC * G // 2, C2 * G // 2
    BODY = PAIRS0 + PAIRS1
    CHUNK = 1024
    CH0, CH1 = KC * G * F2 // CHUNK, C2 * G * D // CHUNK
    Z_BANKS, Y_BANK, T_BANK = TT, 4, 6
    LN_AT, T_AT, EVAC_AT = (1, 2, 3), (4, 6), 2
    STEPS = TT + TT + 3 + 4 * 3 + TT - 1

    def pair0(turn, p):
        return p if isinstance(turn, int) and turn == 0 else PAIRS0 + (turn - 1) * BODY + p

    def pair1(turn, p):
        if isinstance(turn, int) and turn == TURNS - 1:
            return PAIRS0 + (TURNS - 1) * BODY + p
        return PAIRS0 + turn * BODY + PAIRS0 + p

    with ExitStack() as ctx:
        def sb(name, shape, dt=F32):
            return ctx.enter_context(nc.sbuf_tensor(f"k_{name}", shape, dt))

        def sem(name):
            return ctx.enter_context(nc.semaphore(f"k_{name}"))

        w0_h, w0_l = sb("w0_h", [P, KC * G, F2], F32R), sb("w0_l", [P, KC * G, F2], F32R)
        w1_h, w1_l = sb("w1_h", [P, C2 * G, D], F32R), sb("w1_l", [P, C2 * G, D], F32R)
        raw = sb("raw", [P, 2, CHUNK])
        bias0 = sb("bias0", [P, E, F2])
        gains0, offsets0 = sb("gains0", [P, E * KC]), sb("offsets0", [P, E * KC])
        gains1, offsets1 = sb("gains1", [P, E * C2]), sb("offsets1", [P, E * C2])
        shifts0, shifts1 = sb("shifts0", [P, E * KC, G]), sb("shifts1", [P, E * C2, G])
        h0T = sb("h0T", [P, KC, S])
        h1T = sb("h1T", [P, C2, S])
        square = sb("square", [P, 2, 2, S])
        basis_h, basis_l = sb("basis_h", [P, 2, 2, S], F32R), sb("basis_l", [P, 2, 2, S], F32R)
        Z = sb("Z", [P, TT, F2])
        stats, moments = sb("stats", [P, TT, 6]), sb("moments", [P, TT, 2])
        variance, inverse = sb("variance", [P, TT]), sb("inverse", [P, TT])
        work = sb("work", [P, 2, TT])

        params_in, params_ready, params_step = sem("params_in"), sem("params_ready"), sem("params_step")
        raw_in = [sem("raw_in0"), sem("raw_in1")]
        w_high, w_ready = sem("w_high"), sem("w_ready")
        h0_in = sem("h0_in")
        tanh_ready, square_ready, basis_high, basis_ready, pair_used = (
            sem("tanh_ready"), sem("square_ready"), sem("basis_high"), sem("basis_ready"), sem("pair_used"))
        z_out, norm_step, z_normed, h1T_psum, h1T_ready = (
            sem("z_out"), sem("norm_step"), sem("z_normed"), sem("h1T_psum"), sem("h1T_ready"))
        z_tile, x_done = sem("z_tile"), sem("x_done")
        layers = ((KC, h0T, gains0, shifts0), (C2, h1T, gains1, shifts1))

        with nc.Block() as block:
            @block.sync
            def _(sp):
                with nc.allow_non_contiguous_dma(reason="6144 values, once"):
                    for name, dst in (("kan_ln_g0", gains0), ("kan_ln_b0", offsets0),
                                      ("kan_ln_g1", gains1), ("kan_ln_b1", offsets1)):
                        sp.dma_start(dst[:], dram[name].rearrange("e (c p) -> p (e c)", p=P)).then_inc(params_in, 16)
                for e in range(E):
                    sp.dma_start(bias0[:, e, :], dram["kan_sl_b0"][e].partition_broadcast(P)).then_inc(params_in, 16)
                w0 = dram["kan_sl_W0"].rearrange("e (c p g) n -> e c p g n", p=P, g=G)
                w1 = dram["kan_sl_W1"].rearrange("e (c p g) n -> e c p g n", p=P, g=G)
                G0, G1 = CHUNK // F2, CHUNK // D

                def fetch(e, first):
                    for layer, (w, step, chunks) in enumerate(((w0, G0, CH0), (w1, G1, CH1))):
                        for n in range(chunks):
                            place = e * (CH0 + CH1) + layer * CH0 + n
                            if not (first and place < 2):
                                sp.wait_ge(w_ready, place - 1)
                            c, g = divmod(n * step, G)
                            src = w[0, c] if first else w[bass.ds(e, 1), c].rearrange("o p g n -> (o p) g n")
                            sp.dma_start(raw[:, n % 2].rearrange("p (g n) -> p g n", g=step),
                                         src[:, g:g + step, :]).then_inc(raw_in[n % 2], 16)

                fetch(0, True)
                with sp.Fori(1, E) as e:
                    fetch(e, False)

            @block.gpsimd
            def _(pool):
                def split_weights(e, first):
                    for layer, (wh, wl, chunks) in enumerate(((w0_h, w0_l, CH0), (w1_h, w1_l, CH1))):
                        rows = wh.shape[1] // chunks
                        for n in range(chunks):
                            place = e * (CH0 + CH1) + layer * CH0 + n
                            pool.wait_ge(raw_in[n % 2], e * 8 * (CH0 + CH1) + (layer * CH0 + n) // 2 * 16 + 16)
                            if not first:
                                last = pair0(e * B - 1, n) if layer == 0 else pair1(e * B - 1, 2 * n + 1)
                                pool.wait_ge(pair_used, last + 1)
                            hi, lo = (w[:, n * rows:(n + 1) * rows, :].rearrange("p k n -> p (k n)") for w in (wh, wl))
                            pool.sem_inc(const["pool_waited"], 1)
                            pool.tensor_scalar(hi, raw[:, n % 2], 1.0, 0.0, ALU.mult, ALU.add).then_inc(w_high, 1)
                            pool.wait_ge(w_high, place + 1)
                            pool.tensor_tensor(lo, raw[:, n % 2], hi.bitcast(F32), ALU.subtract).then_inc(w_ready, 1)

                split_weights(0, True)
                with pool.Fori(1, E) as e:
                    split_weights(e, False)

            @block.scalar
            def _(act):
                def fetch_h0(batch):
                    src = h0T_dram[batch] if isinstance(batch, int) else h0T_dram[bass.ds(batch, 1)].rearrange(
                        "o p s -> (o p) s")
                    act.dma_start(h0T[:].rearrange("p c s -> p (c s)"), src).then_inc(h0_in, 16)

                def basis(layer, e, p, m):
                    chunks, x, gains, shifts = layers[layer]
                    c, g = divmod(2 * p, G)
                    room = square[:, m_parity(layer, p), :, :]
                    if not (isinstance(m, int) and m < 2):
                        act.wait_ge(basis_ready, m - 1)
                    at = bass.ds(e * chunks + c, 1)
                    for q in range(2):
                        ins = act.activation(room[:, q, :], x[:, c, :], ACT.Tanh, bias=shifts[:, at, g + q],
                                             scale=gains[:, at])
                    ins.then_inc(tanh_ready, 1)
                    act.wait_ge(tanh_ready, m + 1)
                    act.activation(room, room, ACT.Square).then_inc(square_ready, 1)

                def transposed(turn):
                    act.wait_ge(h1T_psum, turn * 2 + 1)
                    act.copy(h1T[:, 0:2, :], psum[:, T_BANK:T_BANK + 2, :]).then_inc(h1T_ready, 1)

                def transposed_rest(turn):
                    act.wait_ge(h1T_psum, turn * 2 + 2)
                    act.copy(h1T[:, 2:4, :], psum[:, T_BANK:T_BANK + 2, :]).then_inc(h1T_ready, 1)

                def first_layer(turn, e, with_last=True):
                    act.wait_ge(h0_in, turn * 16 + 16)
                    for p in range(PAIRS0):
                        basis(0, e, p, pair0(turn, p))
                        if with_last and p == T_AT[0]:
                            transposed(turn - 1)
                        if with_last and p == T_AT[1]:
                            transposed_rest(turn - 1)
                    fetch_h0((turn + 1) % B)

                def second_layer(turn, e):
                    act.wait_ge(h1T_ready, turn * 2 + 2)
                    for p in range(PAIRS1):
                        basis(1, e, p, pair1(turn, p))

                act.wait_ge(params_ready, 1)
                fetch_h0(0)
                first_layer(0, 0, with_last=False)
                first_layer(1, 0)
                second_layer(0, 0)
                with act.Fori(2, TURNS) as turn:
                    first_layer(turn, turn // B)
                    second_layer(turn - 1, (turn - 1) // B)
                transposed(TURNS - 1)
                transposed_rest(TURNS - 1)
                second_layer(TURNS - 1, E - 1)
                act.wait_ge(h0_in, 16 * TURNS + 16)

            @block.tensor
            def _(pe):
                def products(outs, layer, p, m, w_h, w_l, first, last):
                    pe.wait_ge(basis_ready, m + 1)
                    r = m_parity(layer, p)
                    for q in range(2):
                        k = 2 * p + q
                        for t, (out, opens) in enumerate(outs):
                            at = slice(t * P, (t + 1) * P)
                            for i, (x, w) in enumerate(((basis_h, w_h), (basis_h, w_l), (basis_l, w_h))):
                                ins = pe.matmul(out, x[:, r, q, at], w[:, k, :],
                                                start=(first and q == 0 and i == 0 and opens),
                                                stop=(last and q == 1 and i == 2), skip_group_check=True)
                    ins.then_inc(pair_used, 1)

                def transposes(turn, half):
                    pe.wait_ge(z_normed, turn + 1)
                    n = turn * 2 + half
                    if not (isinstance(turn, int) and n == 0):
                        pe.wait_ge(h1T_ready, n)
                    for c in range(2):
                        for t in range(TT):
                            ins = pe.transpose(psum[:, T_BANK + c, t * P:(t + 1) * P],
                                               Z[:, t, (2 * half + c) * P:(2 * half + c + 1) * P], const["ident"])
                    ins.then_inc(h1T_psum, 1)

                def first_layer(turn, e, with_last=True):
                    if with_last:
                        pe.wait_ge(z_out, turn)
                    for p in range(PAIRS0):
                        pe.wait_ge(w_ready, e * (CH0 + CH1) + p + 1)
                        products([(psum[:, t, :], True) for t in range(TT)], 0, p, pair0(turn, p),
                                 w0_h, w0_l, p == 0, p == PAIRS0 - 1)
                        if with_last and p + 1 in T_AT:
                            transposes(turn - 1, T_AT.index(p + 1))

                def second_layer(turn, e):
                    if not (isinstance(turn, int) and turn == 0):
                        pe.wait_ge(x_done, turn * TT)
                    for p in range(PAIRS1):
                        pe.wait_ge(w_ready, e * (CH0 + CH1) + CH0 + p // 2 + 1)
                        products([(psum[:, Y_BANK + t // 2, t % 2 * D:(t % 2 + 1) * D], t % 2 == 0)
                                  for t in range(TT)], 1, p, pair1(turn, p), w1_h, w1_l, p == 0, p == PAIRS1 - 1)

                first_layer(0, 0, with_last=False)
                first_layer(1, 0)
                second_layer(0, 0)
                with pe.Fori(2, TURNS) as turn:
                    first_layer(turn, turn // B)
                    second_layer(turn - 1, (turn - 1) // B)
                for half in range(2):
                    transposes(TURNS - 1, half)
                second_layer(TURNS - 1, E - 1)

            @block.vector
            def _(dve):
                share_flat = share[:].rearrange("p t e -> p (t e)")

                def basis(layer, p, m):
                    r = m_parity(layer, p)
                    dve.wait_ge(square_ready, m + 1)
                    if not (isinstance(m, int) and m < 2):
                        dve.wait_ge(pair_used, m - 1)
                    dve.tensor_scalar(basis_h[:, r], square[:, r], -1.0, None, ALU.add).then_inc(basis_high, 1)
                    dve.wait_ge(basis_high, m + 1)
                    flat = [x[:, r].rearrange("p q s -> p (q s)") for x in (basis_l, square, basis_h)]
                    dve.scalar_tensor_tensor(flat[0], flat[1], 1.0, flat[2].bitcast(F32),
                                             ALU.subtract, ALU.subtract).then_inc(basis_ready, 1)

                def evacuate(turn, e):
                    dve.wait_ge(pair_used, pair0(turn, PAIRS0 - 1) + 1)
                    if not (isinstance(turn, int) and turn == 0):
                        dve.wait_ge(h1T_psum, turn * 2)
                    for t in range(TT):
                        ins = dve.scalar_tensor_tensor(Z[:, t, :], psum[:, t, :], -1.0, bias0[:, bass.ds(e, 1), :].rearrange(
                            "p o n -> p (o n)"), ALU.mult, ALU.add)
                        ins.then_inc(z_out, 1) if t == TT - 1 else ins.then_inc(z_tile, 1)

                def layer_norm(turn, part, steps):
                    if part == 0:
                        dve.wait_ge(z_out, turn + 1)
                        for t in range(TT):
                            steps.link(dve.bn_stats(stats[:, t, :], Z[:, t, :]))
                        steps.settle()
                    elif part == 1:
                        for t in range(TT):
                            steps.link(dve.bn_aggr(moments[:, t, :], stats[:, t, :]))
                        steps.settle()
                        def settled(ins):
                            steps.link(ins)
                            steps.settle()

                        guess, bits = work[:, 0, :], work[:, 1, :].bitcast(I32)
                        settled(dve.tensor_scalar(variance[:], moments[:, :, 1], EPS, None, ALU.add))
                        settled(dve.tensor_scalar(bits, variance[:].bitcast(I32), 1, None, ALU.logical_shift_right))
                        settled(dve.tensor_scalar(inverse[:].bitcast(I32), bits, -1.0, float(0x5F3759DF),
                                                  ALU.mult, ALU.add))
                        for _ in range(3):
                            settled(dve.tensor_tensor(guess, inverse[:], inverse[:], ALU.mult))
                            settled(dve.tensor_tensor(guess, guess, variance[:], ALU.mult))
                            settled(dve.tensor_scalar(guess, guess, -0.5, 1.5, ALU.mult, ALU.add))
                            settled(dve.tensor_tensor(inverse[:], inverse[:], guess, ALU.mult))
                    else:
                        for t in range(TT):
                            ins = dve.tensor_scalar(Z[:, t, :], Z[:, t, :], moments[:, t, 0:1], inverse[:, t:t + 1],
                                                    ALU.subtract, ALU.mult)
                            if t == TT - 1:
                                ins.then_inc(z_normed, 1)
                            else:
                                steps.link(ins)
                        assert steps.n == STEPS, (steps.n, STEPS)

                def add_output(turn, e, batch):
                    dve.wait_ge(pair_used, pair1(turn, PAIRS1 - 1) + 1)
                    for t in range(TT):
                        tile = batch * TT + t
                        Xt = X[:, bass.ds(tile, 1), :].rearrange("p o d -> p (o d)")
                        dve.scalar_tensor_tensor(Xt, psum[:, Y_BANK + t // 2, t % 2 * D:(t % 2 + 1) * D],
                                                 share_flat[:, bass.ds(tile * N8 + E + e, 1)], Xt,
                                                 ALU.mult, ALU.add).then_inc(x_done, 1)

                def body(turn, e, before, e_before, second=False):
                    steps = Count(dve, norm_step, before * STEPS)
                    for p in range(PAIRS0):
                        basis(0, p, pair0(turn, p))
                        if p == 0 and not second:
                            add_output(turn - 2, (turn - 2) // B, (turn - 2) % B)
                        if p in LN_AT:
                            layer_norm(before, LN_AT.index(p), steps)
                    for p in range(PAIRS1):
                        basis(1, p, pair1(before, p))
                        if p == EVAC_AT:
                            evacuate(turn, e)

                dve.wait_ge(params_in, 16 * (4 + E))
                n = 0
                for gains in (gains0, gains1):
                    dve.tensor_scalar(gains[:], gains[:], 0.5, None, ALU.mult).then_inc(params_step, 1)
                    n += 1
                for offsets, shifts in ((offsets0, shifts0), (offsets1, shifts1)):
                    for g in range(G):
                        dve.tensor_scalar(shifts[:, :, g], offsets[:], float(-GRID[g]), 0.5,
                                          ALU.add, ALU.mult).then_inc(params_step, 1)
                        n += 1
                dve.wait_ge(params_step, n)
                dve.tensor_copy(work[:, 0, :], gains0[:, 0:TT]).then_inc(params_ready, 1)

                for p in range(PAIRS0):
                    basis(0, p, pair0(0, p))
                evacuate(0, 0)
                body(1, 0, 0, 0, second=True)
                with dve.Fori(2, TURNS) as turn:
                    body(turn, turn // B, turn - 1, (turn - 1) // B)
                add_output(TURNS - 2, E - 1, B - 2)
                steps = Count(dve, norm_step, (TURNS - 1) * STEPS)
                for part in range(3):
                    layer_norm(TURNS - 1, part, steps)
                for p in range(PAIRS1):
                    basis(1, p, pair1(TURNS - 1, p))
                add_output(TURNS - 1, E - 1, B - 1)


def constants_on_host():
    r = np.arange(P) // HD % REP
    ident = np.eye(P, dtype=np.float32)
    marks = np.zeros((P, 24), np.float32)
    marks[:, 0] = np.where(r % 2 == 1, -1, 0)
    marks[:, 1] = np.where(r >= 2, -1, 0)
    marks[:, 2] = EPS
    marks[:, 8:16] = np.arange(8)
    marks[:, 16:24] = np.where(np.arange(8) < 4, 1, -1)
    return ident, marks


def build(nc, dram, out):
    with ExitStack() as ctx:
        X = ctx.enter_context(nc.sbuf_tensor("X", [P, NT, D], F32))
        ident = ctx.enter_context(nc.sbuf_tensor("ident", [P, P], F32))
        ident_b = ctx.enter_context(nc.sbuf_tensor("ident_b", [P, P], BF16))
        marks = ctx.enter_context(nc.sbuf_tensor("marks", [P, 24], F32))
        psum = ctx.enter_context(nc.psum_tensor("psum", [P, 8, 512], F32))
        const_in, const_ready, vector_waited, pool_waited = (ctx.enter_context(nc.semaphore(n)) for n in (
            "const_in", "const_ready", "vector_waited", "pool_waited"))
        const = {"ident": ident[:], "ident_b": ident_b[:], "neg_low_rows": marks[:, 0:1],
                 "neg_low_halves": marks[:, 1:2], "eps": marks[:, 2:3], "experts": marks[:, 8:16],
                 "signs": marks[:, 16:24], "vector_waited": vector_waited, "pool_waited": pool_waited}
        with nc.Block() as block:
            @block.sync
            def _(sp):
                sp.dma_start(ident[:], dram["ident"]).then_inc(const_in, 16)
                sp.dma_start(marks[:], dram["marks"]).then_inc(const_in, 16)

            @block.vector
            def _(dve):
                dve.wait_ge(const_in, 32)
                dve.tensor_copy(ident_b[:], ident[:]).then_inc(const_ready, 1)
                dve.wait_ge(const_ready, 1)
        attention(nc, False, X, psum, const, dram)
        attention(nc, True, X, psum, const, dram)
        experts(nc, X, psum, const, dram)
        stored = ctx.enter_context(nc.semaphore("stored"))
        with nc.Block() as block:
            @block.sync
            def _(sp):
                sp.dma_start(out.rearrange("(t p) d -> p t d", p=P), X[:]).then_inc(stored, 16)
                sp.wait_ge(stored, 16)


INPUTS = {
    "x": "x", "ctx": "ctx_1024", "mask": "mask_Bx1xSxS2_if1",
    "ln_scale": "L0_attn_ln_scale", "ln_bias": "L0_attn_ln_bias", "w_qkv": "L0_attn_w_qkv",
    "w_proj": "L0_attn_w_proj", "b_proj": "L0_attn_b_proj",
    "Wq": "L0_xattn_Wq", "bq": "L0_xattn_bq", "Wk": "L0_xattn_Wk", "bk": "L0_xattn_bk",
    "Wv": "L0_xattn_Wv", "bv": "L0_xattn_bv", "Wo": "L0_xattn_Wo", "bo": "L0_xattn_bo",
    "gate_W": "L0_ffn_gate_W", "mlp_W1": "L0_ffn_mlp_W1", "mlp_b1": "L0_ffn_mlp_b1",
    "mlp_W2": "L0_ffn_mlp_W2", "mlp_b2": "L0_ffn_mlp_b2",
    "kan_ln_g0": "L0_ffn_kan_ln_g0", "kan_ln_b0": "L0_ffn_kan_ln_b0",
    "kan_sl_W0": "L0_ffn_kan_sl_W0", "kan_sl_b0": "L0_ffn_kan_sl_b0",
    "kan_ln_g1": "L0_ffn_kan_ln_g1", "kan_ln_b1": "L0_ffn_kan_ln_b1",
    "kan_sl_W1": "L0_ffn_kan_sl_W1", "kan_sl_b1": "L0_ffn_kan_sl_b1",
}
RESHAPED = {"x": (B * S, D), "ctx": (B * S, D), "mask": (B, S, S)}


def kernel(**inputs):
    import concourse.bacc as bacc
    from concourse.bass_utils import run_bass_kernel_spmd

    nc = bacc.Bacc("TRN2", target_bir_lowering=False, num_devices=1)
    ident, marks = constants_on_host()
    arrays = {"ident": ident, "marks": marks}
    for name, given in INPUTS.items():
        a = np.ascontiguousarray(inputs[given])
        arrays[name] = a.reshape(RESHAPED.get(name, a.shape))
    dram = {name: nc.dram_tensor(f"in_{name}", a.shape, mybir.dt.from_np(a.dtype), kind="ExternalInput").ap()
            for name, a in arrays.items()}
    out = nc.dram_tensor("out", (B * S, D), F32, kind="ExternalOutput").ap()
    build(nc, dram, out)
    result = run_bass_kernel_spmd(nc, [{f"in_{name}": a for name, a in arrays.items()}], core_ids=[0])
    return result.results[0]["out"].reshape(B, S, D)
```

```python
from contextlib import ExitStack

import numpy as np

import concourse.bass as bass
from concourse import mybir

F32 = mybir.dt.float32
F32R = mybir.dt.float32r
BF16 = mybir.dt.bfloat16
I32 = mybir.dt.int32
U32 = mybir.dt.uint32
ALU = mybir.AluOpType
ACT = mybir.ActivationFunctionType
AX_X = mybir.AxisListType.X

P = 128
B, S, D = 4, 512, 256
TT = S // P
NT = B * TT
KC = D // P
H, HD = 16, 16
HP = H // 2
HG = H // 4
GP = HP // HG
PAD = 32
EPS = 1e-5
MASKED = -2.0 ** 60
SCORE_SCALE = 1.0 / float(np.sqrt(HD))


class Count:

    def __init__(self, eng, sem, base=0):
        self.eng, self.sem, self.base, self.n = eng, sem, base, 0

    def link(self, ins):
        self.n += 1
        ins.then_inc(self.sem, 1)

    def settle(self):
        self.eng.wait_ge(self.sem, self.base + self.n)

    def __call__(self, ins):
        self.link(ins)
        self.settle()


def layer_norm_vector(dve, steps, src, dst, tiles, stats, moments, root, inverse,
                      variance_ready, root_ready, waited, at, last=None):
    for t in range(tiles):
        steps.link(dve.bn_stats(stats[:, t, :], src(t)))
    steps.settle()
    dve.sem_inc(waited, 1)
    for t in range(tiles):
        ins = dve.bn_aggr(moments[:, t, :], stats[:, t, :])
        if t == tiles - 1:
            ins.then_inc(variance_ready, 1)
        else:
            steps.link(ins)
    dve.wait_ge(variance_ready, at)
    dve.wait_ge(root_ready, at)
    steps.link(dve.reciprocal(inverse[:, 0:tiles], root[:, 0:tiles]))
    steps.settle()
    for t in range(tiles):
        ins = dve.tensor_scalar(dst(t), src(t), moments[:, t, 0:1], inverse[:, t:t + 1],
                                ALU.subtract, ALU.mult)
        if t == tiles - 1 and last is not None:
            ins.then_inc(last, 1)
        else:
            steps.link(ins)
    if last is None:
        steps.settle()


def inverse_deviation(settled, moments, variance, inverse, guess, bits):
    dve = settled.eng
    settled(dve.tensor_scalar(variance, moments, EPS, None, ALU.add))
    settled(dve.tensor_scalar(bits.bitcast(I32), variance.bitcast(I32), 1, None, ALU.logical_shift_right))
    settled(dve.tensor_scalar(inverse.bitcast(I32), bits.bitcast(I32), -1.0, float(0x5F3759DF), ALU.mult, ALU.add))
    for _ in range(3):
        settled(dve.tensor_tensor(guess, inverse, inverse, ALU.mult))
        settled(dve.tensor_tensor(guess, guess, variance, ALU.mult))
        settled(dve.tensor_scalar(guess, guess, -0.5, 1.5, ALU.mult, ALU.add))
        settled(dve.tensor_tensor(inverse, inverse, guess, ALU.mult))


def attention(nc, cross, X, psum, const, dram):
    k = "x" if cross else "s"
    SRC = 2 if cross else 1
    UNITS = 8
    SCORES = 4 * TT
    SCORES_IN = (3, 3, 3, 3, 2, 2, 0, 0)
    SPLITS = SRC * KC + 2 * KC
    LN = 1 if cross else 2
    NORM_STEPS = TT * LN - 1
    S_BANK, C_BANK, O_BANK, M_BANK = 0, 2, 6, 7

    def items(g, first=False, last=False):
        units = [([], []) for _ in range(UNITS)]

        def put(u, *item, late=False):
            units[u][late].append(item)

        ahead, group = divmod(g + 2, HG)
        if not (last and ahead):
            for i, (at_k, at_q) in enumerate(((2, 3), (5, 6)) if g == 2 else ((0, 1), (2, 5))):
                put(at_k, "KD", ahead, GP * group + i)
                put(at_q, "QD", ahead, GP * group + i, late=(g == 2 and i == 0))
        if not first:
            put(3, "SUM", -1 if g == 0 else 0, (g - 1) % HG)
            put(4, "R", -1 if g == 0 else 0, (g - 1) % HG)
        if not (last and g == HG - 1):
            put(7, "M", *divmod(g + 1, HG))
        if g == 0 and not first:
            if cross:
                put(2, "MT", 0, TT - 1, late=True)
            put(6, "OUT", -1, 0)
            put(7, "OUT", -1, 1, late=True)
        if g == 1 and not last:
            if cross:
                put(1, "T", 1, 0, late=True)
                put(4, "T", 1, 1, late=True)
            put(6, "T", 1, SRC * KC - 2)
            put(7, "T", 1, SRC * KC - 1, late=True)
        if g == 2 and not last:
            put(0, "K", 1, 0)
            put(1, "Q", 1, 0)
            put(4, "V", 1, 0, late=True)
            put(5, "V", 1, 1, late=True)
        if g == 3 and not last:
            put(6, "K", 1, 1)
            put(7, "Q", 1, 1, late=True)
            if cross:
                for t in range(TT - 1):
                    put(2 * t + 2, "MT", 1, t, late=True)
        return units

    prologue = [("T", 0, i) for i in range(SRC * KC)]
    prologue += [(kind, 0, c) for c in range(KC) for kind in ("K", "Q")] + [("V", 0, i) for i in range(2)]
    prologue += [(kind, 0, i) for i in range(2 * GP) for kind in ("KD", "QD")]
    if cross:
        prologue += [("MT", 0, t) for t in range(TT)]
    prologue += [("M", 0, 0)]
    count = lambda units: sum(len(early + late) for early, late in units)
    IN_FIRST = len(prologue) + count(items(0, first=True))
    IN_ROUND = sum(count(items(g)) for g in range(HG))
    SPLIT_OF = {("T", i): i for i in range(SRC * KC)}
    SPLIT_OF.update({(kind, c): SRC * KC + 2 * c + i for c in range(KC) for i, kind in enumerate(("K", "Q"))})

    with ExitStack() as ctx:
        def sb(name, shape, dt=F32):
            return ctx.enter_context(nc.sbuf_tensor(f"{k}_{name}", shape, dt))

        def sem(name):
            return ctx.enter_context(nc.semaphore(f"{k}_{name}"))

        wq, wk, wv = ([sb(f"{n}_{part}", [P, KC, D], F32R) for part in "hl"] for n in ("wq", "wk", "wv"))
        wo_h, wo_l = sb("wo_h", [P, HG, D], F32R), sb("wo_l", [P, HG, D], F32R)
        bias_out = sb("bias_out", [P, D])

        stats, moments = sb("stats", [P, NT, 6]), sb("moments", [P, LN, NT, 2])
        inverse, work = sb("inverse", [P, LN, NT]), sb("work", [P, 3, NT])
        Z = sb("Z", [P, TT, D])
        full = sb("full", [P, 2, S])
        source_h, source_l = sb("source_h", [P, SRC, KC, S], F32R), sb("source_l", [P, SRC, KC, S], F32R)
        base_h, base_l = sb("base_h", [P, KC, 2, S], F32R), sb("base_l", [P, KC, 2, S], F32R)
        KT = sb("KT", [P, H, S], F32R)
        QT = sb("QT", [P, HP, S], F32R)
        V = sb("V", [P, TT, H, PAD])
        V_next = Z
        neg_max = sb("neg_max", [P, 2, TT, 4])
        max_cols = sb("max_cols", [P, TT, P], F32R)
        probsT = sb("probsT", [P, 2, 4, S])
        OT = sb("OT", [P, 2, S])
        inv_sums, inv_rows = sb("inv_sums", [P, TT, 4]), sb("inv_rows", [P, TT, 4, PAD])
        OT_h, OT_l = sb("OT_h", [P, HG, S], F32R), sb("OT_l", [P, HG, S], F32R)

        weights_in, wo_cleared, wo_placed = sem("weights_in"), sem("wo_cleared"), sem("wo_placed")
        w_transposed, prep, cleared = sem("w_transposed"), sem("prep"), sem("cleared")
        item_ready, item_read = sem("item_ready"), sem("item_read")
        stats_step, ln_step, max_step, z_ready = sem("stats_step"), sem("ln_step"), sem("max_step"), sem("z_ready")
        residual_step, low_ready, v_placed = sem("residual_step"), sem("low_ready"), sem("v_placed")
        scores_ready, max_ready, max_split = sem("scores_ready"), sem("max_ready"), sem("max_split")
        scoresT_ready, probs_ready, inverted = sem("scoresT_ready"), sem("probs_ready"), sem("inverted")
        av_ready, o_out, norm_step = sem("av_ready"), sem("o_out"), sem("norm_step")
        if cross:
            CTX = sb("CTX", [P, TT, D])
            mask = sb("mask", [P, TT, S], I32)
            mask_bias, mask_biasT = sb("mask_bias", [P, TT, S], BF16), sb("mask_biasT", [P, TT, S], BF16)
            bias_kq = sb("bias_kq", [P, KC, 2])
            bias_v = sb("bias_v", [P, D])
            ctx_in, mask_in, mask_ready = sem("ctx_in"), sem("mask_in"), sem("mask_ready")
        else:
            X1 = sb("X1", [P, TT, D])
            ln_affine = sb("ln_affine", [P, 2, KC])

        room = probsT[:].rearrange("p a j q -> p (a j q)")
        w_all = room[:, 0:KC * 3 * D].rearrange("p (c e) -> p c e", c=KC)
        wo_pad = room[:, 1536:2560].rearrange("p (g e) -> p g e", g=HG)
        wo_cols = room[:, 2560:3584].rearrange("p (c h d) -> p c h d", c=KC, h=H)
        if cross:
            w_nat = [mask[:, i, :].bitcast(F32).rearrange("p (c d) -> p c d", c=KC) for i in range(4)]
        with nc.Block() as block:
            loads = 4 + 2 + 2 if cross else 9

            @block.sync
            def _(sp):
                n = 0

                def load(dst, src):
                    nonlocal n
                    n += 1
                    sp.dma_start(dst, src).then_inc(weights_in, 16)

                if cross:
                    for i, name in enumerate(("Wq", "Wk", "Wv", "Wo")):
                        load(w_nat[i], dram[name].rearrange("(c p) d -> p c d", p=P))
                    for i, name in enumerate(("bk", "bq")):
                        with nc.allow_non_contiguous_dma(reason="256 bias values, once"):
                            load(bias_kq[:, :, i], dram[name].rearrange("(c p) -> p c", p=P))
                    load(bias_v[:], dram["bv"].partition_broadcast(P))
                    load(bias_out[:], dram["bo"].partition_broadcast(P))
                else:
                    load(X[:], dram["x"].rearrange("(t p) d -> p t d", p=P))
                    load(w_all, dram["w_qkv"].rearrange("(c p) e -> p c e", p=P))
                    for i, name in enumerate(("ln_scale", "ln_bias")):
                        with nc.allow_non_contiguous_dma(reason="256 values, once"):
                            load(ln_affine[:, i, :], dram[name].rearrange("(c p) -> p c", p=P))
                    load(bias_out[:], dram["b_proj"].partition_broadcast(P))
                    sp.wait_ge(wo_cleared, 1)
                    rows = dram["w_proj"].rearrange("(g j d) e -> j d g e", g=HG, j=4)
                    for j in range(4):
                        load(wo_pad[PAD * j:PAD * j + HD], rows[j])
                assert n == loads

            @block.tensor
            def _(pe):
                if not cross:
                    return
                pe.wait_ge(weights_in, 16 * loads)
                for i in range(3):
                    for c in range(KC):
                        for e in range(KC):
                            ins = pe.transpose(psum[:, i, (c * KC + e) * P:(c * KC + e + 1) * P],
                                               w_nat[i][:, e, c * P:(c + 1) * P], const["ident"])
                ins.then_inc(w_transposed, 1)
                pe.wait_ge(wo_placed, 1)
                for g in range(HG):
                    for e in range(KC):
                        n = g * KC + e
                        ins = pe.transpose(psum[:, 4 + n // 4, (n % 4) * P:(n % 4 + 1) * P],
                                           wo_cols[:, e, 4 * g:4 * g + 4, :].rearrange("p h d -> p (h d)"),
                                           const["ident"])
                ins.then_inc(w_transposed, 1)

            @block.vector
            def _(dve):
                steps = Count(dve, prep)
                if cross:
                    dve.memset(wo_cols, 0.0).then_inc(wo_cleared, 1)
                    dve.wait_ge(wo_cleared, 1)
                    dve.wait_ge(weights_in, 16 * loads)
                    steps.link(dve.tensor_scalar(bias_kq[:, :, 1], bias_kq[:, :, 1], SCORE_SCALE, None, ALU.mult))
                    for e in range(KC):
                        ins = dve.tensor_copy(wo_cols[:, e, :, 0:HD],
                                              w_nat[3][:, e, :].rearrange("p (h d) -> p h d", h=H))
                    ins.then_inc(wo_placed, 1)
                    dve.wait_ge(w_transposed, 1)
                    for i in range(3):
                        steps.link(dve.tensor_copy(w_all[:, :, i * D:(i + 1) * D],
                                                   psum[:, i, :].rearrange("p (c e) -> p c e", c=KC)))
                    dve.wait_ge(w_transposed, 2)
                    for n in range(2):
                        steps.link(dve.tensor_copy(wo_pad[:, 2 * n:2 * n + 2, :],
                                                   psum[:, 4 + n, :].rearrange("p (g e) -> p g e", g=2)))
                    steps.settle()
                else:
                    dve.memset(wo_pad, 0.0).then_inc(wo_cleared, 1)
                    dve.wait_ge(wo_cleared, 1)
                    dve.wait_ge(weights_in, 16 * loads)

                def split_weight(hi, lo, one):
                    steps.link(dve.tensor_copy(hi, one))
                    steps.settle()
                    steps.link(dve.tensor_tensor(lo, one, hi.bitcast(F32), ALU.subtract))

                for i, (hi, lo) in enumerate((wq, wk, wv)):
                    if cross:
                        one = w_all[:, :, i * D:(i + 1) * D]
                    else:
                        one = w_all.rearrange("p c (e w) -> p c e w", w=3)[:, :, :, i]
                    split_weight(hi[:], lo[:], one)
                split_weight(wo_h[:], wo_l[:], wo_pad)
                dve.wait_ge(cleared, 1)
                for j in range(4):
                    rows = KT[96:P, :, :].rearrange("p (g j) s -> p g j s", j=4)[:, :, j, :]
                    steps.link(dve.tensor_scalar(rows, rows.bitcast(F32), const["select_max"][96:P, j:j + 1], None, ALU.mult))
                steps.settle()

            @block.gpsimd
            def _(pool):
                pool.memset(KT[96:P].bitcast(F32), 1.0).then_inc(cleared, 1)
                pool.wait_ge(cleared, 1)
                pool.memset(max_cols[:].bitcast(F32), 0.0).then_inc(cleared, 1)
                pool.memset(V[:], 0.0).then_inc(cleared, 1)
                pool.wait_ge(cleared, 3)
                pool.memset(V[:, :, :, HD:HD + 1], 1.0).then_inc(cleared, 1)
                pool.wait_ge(cleared, 4)

        def sections(eng, prepare, step):
            prepare()
            step(0, 0, len(prologue), True, False)
            with eng.Fori(0, B - 1) as b:
                n = 0
                for g in range(1, HG + 1):
                    step(b + g // HG, g % HG, b * IN_ROUND + IN_FIRST + n, False, False)
                    n += count(items(g % HG))
            n = IN_FIRST + (B - 1) * IN_ROUND
            for g in range(1, HG):
                step(B - 1, g, n, False, True)
                n += count(items(g, last=True))
            return n

        with nc.Block() as block:
            if cross:
                @block.sync
                def _(sp):
                    ctx_rows = dram["ctx"].rearrange("(b t p) d -> b p t d", b=B, p=P)
                    mask_rows = dram["mask"].rearrange("b (t p) s -> b p t s", p=P)
                    sp.dma_start(CTX[:], ctx_rows[0]).then_inc(ctx_in, 16)
                    sp.dma_start(mask[:], mask_rows[0]).then_inc(mask_in, 16)
                    with sp.Fori(1, B) as b:
                        sp.wait_ge(low_ready, b * SPLITS - SPLITS + KC)
                        sp.dma_start(CTX[:], ctx_rows[bass.ds(b, 1)].rearrange("o p t d -> (o p) t d")
                                     ).then_inc(ctx_in, 16)
                        sp.wait_ge(mask_ready, b * TT)
                        sp.dma_start(mask[:], mask_rows[bass.ds(b, 1)].rearrange("o p t s -> (o p) t s")
                                     ).then_inc(mask_in, 16)

            @block.gpsimd
            def _(pool):
                def add_residual(b):
                    tiles = bias_out[:].unsqueeze(1).to_broadcast([P, TT, D])
                    pool.wait_ge(z_ready, b + 1)
                    pool.sem_inc(const["pool_waited"], 1)
                    Xb = X[:, bass.ds(b * TT, TT), :]
                    if cross:
                        pool.tensor_tensor(Xb, Xb, tiles, ALU.add).then_inc(residual_step, 1)
                    else:
                        pool.tensor_tensor(Xb, Xb, X1[:], ALU.add).then_inc(residual_step, 1)
                        pool.wait_ge(residual_step, b * 2 + 1)
                        pool.sem_inc(const["pool_waited"], 1)
                        pool.tensor_tensor(Xb, Xb, tiles, ALU.add).then_inc(residual_step, 1)

                def low_part(item, b, n):
                    kind, _, i = item
                    s = SPLIT_OF[kind, i]
                    if kind == "T":
                        hi, lo = (x[:, i // KC, i % KC, :] for x in (source_h, source_l))
                    else:
                        hi, lo = (x[:, i, "KQ".index(kind), :] for x in (base_h, base_l))
                    pool.wait_ge(item_read, n + 1)
                    pool.tensor_tensor(lo, full[:, s % 2, :], hi.bitcast(F32), ALU.subtract).then_inc(low_ready, 1)

                def place_values(b, g):
                    at = V_next[:].rearrange("p t (h d) -> p t h d", h=H)
                    pool.sem_inc(const["pool_waited"], 1)
                    pool.tensor_copy(V[:, :, 4 * g:4 * g + 4, 0:HD], at[:, :, 4 * g:4 * g + 4, :]).then_inc(v_placed, 1)

                def convert_mask(b, t):
                    pool.sem_inc(const["pool_waited"], 1)
                    pool.tensor_scalar(mask_bias[:, t, :], mask[:, t, :], 0.0, MASKED,
                                       ALU.is_equal, ALU.mult).then_inc(mask_ready, 1)

                def split_weighted(b, g, n):
                    at = b * (2 * HG) + 2 * g + 2
                    o = OT[:, g % 2, :]
                    pool.wait_ge(item_read, n + 1)
                    pool.sem_inc(const["pool_waited"], 1)
                    pool.tensor_scalar(OT_h[:, g, :], o, 1.0, 0.0, ALU.mult, ALU.add).then_inc(norm_step, 1)
                    pool.wait_ge(norm_step, at + 1)
                    pool.tensor_tensor(OT_l[:, g, :], o, OT_h[:, g, :].bitcast(F32), ALU.subtract).then_inc(norm_step, 1)

                def prepare():
                    pool.sem_inc(norm_step, 2)
                    if cross:
                        pool.wait_ge(mask_in, 16)
                        for t in range(TT):
                            convert_mask(0, t)
                    for n, item in enumerate(prologue):
                        if item == ("K", 0, 0):
                            add_residual(0)
                        if item[0] in ("T", "K", "Q"):
                            low_part(item, 0, n)
                        if item == ("V", 0, 1):
                            pool.wait_ge(item_read, n + 1)
                            for g in range(HG):
                                place_values(0, g)

                def step(b, g, n, first, last):
                    for u, (early, late) in enumerate(items(g, first, last)):
                        if cross and not last and g == 2 and 2 <= u < 2 + TT:
                            if u == 2:
                                pool.wait_ge(mask_in, b * 16 + 32)
                            pool.wait_ge(scores_ready, b * (SCORES * HG) + SCORES * HG - SCORES + 4 * (u - 2) + 4)
                            convert_mask(b + 1, u - 2)
                        if u == 5 and g == 3 and not last:
                            for v in range(3):
                                pool.wait_ge(av_ready, b * NT + 4 * v + 4)
                                place_values(b + 1, v)
                        if u == 5 and g == 0 and not first:
                            pool.wait_ge(av_ready, b * NT)
                            place_values(b, 3)
                        for item in early + late:
                            if item[0] == "R":
                                split_weighted(b + item[1], item[2], n)
                            elif item[0] in ("T", "K", "Q"):
                                if item == ("T", 1, SRC * KC - 2):
                                    add_residual(b + 1)
                                low_part(item, b + 1, n)
                            n = n + 1

                n = sections(pool, prepare, step)
                split_weighted(B - 1, HG - 1, n + 1)
                pool.wait_ge(norm_step, 2 * HG * B + 2)

            @block.tensor
            def _(pe):
                ident, ident_b, ident_r = const["ident"], const["ident_b"], const["ident_r"]
                out = psum[:, M_BANK, :]

                def item_products(item, b, n):
                    kind, ahead, i = item
                    b = b + ahead
                    if not (isinstance(n, int) and n == 0):
                        pe.wait_ge(item_read, n)
                    if kind == "T":
                        if i == 0 and cross:
                            pe.wait_ge(ctx_in, b * 16 + 16)
                        if i == (SRC - 1) * KC:
                            pe.wait_ge(z_ready, b + 1)
                        what, c = (CTX if cross and i < KC else Z), i % KC
                        for t in range(TT):
                            ins = pe.transpose(out[:, t * P:(t + 1) * P], what[:, t, c * P:(c + 1) * P], ident)
                    elif kind in ("K", "Q"):
                        pe.wait_ge(low_ready, b * SPLITS + (KC if kind == "K" else SRC * KC))
                        (wh, wl), s = (wk, 0) if kind == "K" else (wq, SRC - 1)
                        at = slice(i * P, (i + 1) * P)
                        terms = [(wh[:, c, at], x[:, s, c, :]) for c in range(KC) for x in (source_h, source_l)]
                        terms += [(wl[:, c, at], source_h[:, s, c, :]) for c in range(KC)]
                        for j, (lhsT, rhs) in enumerate(terms):
                            ins = pe.matmul(out, lhsT, rhs, start=(j == 0), stop=(j == len(terms) - 1))
                    elif kind == "V":
                        pe.wait_ge(low_ready, b * SPLITS + KC)
                        for t in (2 * i, 2 * i + 1):
                            at = slice(t * P, (t + 1) * P)
                            terms = [(source_h[:, 0, c, at], w[:, c, :]) for c in range(KC) for w in wv]
                            terms += [(source_l[:, 0, c, at], wv[0][:, c, :]) for c in range(KC)]
                            for j, (lhsT, rhs) in enumerate(terms):
                                ins = pe.matmul(out[:, (t % 2) * D:(t % 2 + 1) * D], lhsT, rhs,
                                                start=(j == 0 and t % 2 == 0), stop=(j == len(terms) - 1),
                                                skip_group_check=True)
                    elif kind in ("KD", "QD"):
                        c, which = i // 4, "KQ".index(kind[0])
                        pe.wait_ge(low_ready, b * SPLITS + SPLIT_OF[kind[0], c] + 1)
                        for part, x in enumerate((base_h, base_l)):
                            ins = pe.matmul(out, const["select"][:, i % 4, which, part, :], x[:, c, which, :],
                                            start=(part == 0), stop=(part == 1))
                    elif kind == "MT":
                        pe.wait_ge(mask_ready, b * TT + TT)
                        for t in range(TT):
                            ins = pe.transpose(out[:, 0:S // 2].bitcast(BF16)[:, t * P:(t + 1) * P],
                                               mask_bias[:, t, i * P:(i + 1) * P], ident_b)
                    elif kind == "M":
                        pe.wait_ge(max_split, b * HG + i + 1)
                        for t in range(TT):
                            ins = pe.matmul(out[:, t * P:(t + 1) * P], max_cols[:, t, :], ident_r,
                                            start=True, stop=True)
                    elif kind == "SUM":
                        pe.wait_ge(o_out, b * HG + i + 1)
                        for t in range(TT):
                            ins = pe.matmul(out[:, 4 * t:4 * t + 4], OT[:, i % 2, t * P:(t + 1) * P],
                                            const["pick_sums"], start=True, stop=True)
                    elif kind == "R":
                        pe.wait_ge(item_read, n)
                        for t in range(TT):
                            ins = pe.matmul(out[:, t * P:(t + 1) * P], inv_rows[:, t].rearrange("p j d -> p (j d)"),
                                            ident, start=True, stop=True)
                    elif kind == "OUT":
                        pe.wait_ge(norm_step, b * (2 * HG) + 2 * HG + 2)
                        for t in (2 * i, 2 * i + 1):
                            at = slice(t * P, (t + 1) * P)
                            terms = [(OT_h[:, g, at], w[:, g, :]) for g in range(HG) for w in (wo_h, wo_l)]
                            terms += [(OT_l[:, g, at], wo_h[:, g, :]) for g in range(HG)]
                            for j, (lhsT, rhs) in enumerate(terms):
                                ins = pe.matmul(out[:, (t % 2) * D:(t % 2 + 1) * D], lhsT, rhs,
                                                start=(j == 0 and t % 2 == 0), stop=(j == len(terms) - 1),
                                                skip_group_check=True)
                    ins.then_inc(item_ready, 1)

                def scores(b, g, s):
                    t, h = s // 4, 4 * g + s % 4
                    if not (isinstance(b, int) and b == 0 and g == 0 and s < 2):
                        pe.wait_ge(max_ready, b * (SCORES * HG) + SCORES * g + s - 1)
                    if cross and s % 4 == 0:
                        pe.wait_ge(mask_ready, b * TT + t + 1)
                    out_s = psum[:, S_BANK + s % 2, :]
                    ins = pe.matmul(out_s, QT[:, h // 2, t * P:(t + 1) * P], KT[:, h, :], start=True, stop=not cross)
                    if cross:
                        ins = pe.matmul(out_s, ident_b, mask_bias[:, t, :], start=False, stop=True)
                    ins.then_inc(scores_ready, 1)

                def scores_transposed(b, g, u, i):
                    t, pair = u // 2, GP * g + u % 2
                    if i == 0 and not (isinstance(b, int) and b == 0 and g == 0 and u < 2):
                        pe.wait_ge(probs_ready, b * (UNITS * HG) + UNITS * g + u - 1)
                    out_c = psum[:, C_BANK + 2 * (u % 2) + i, :]
                    ins = pe.matmul(out_c, KT[:, 2 * pair + i, t * P:(t + 1) * P], QT[:, pair, :],
                                    start=True, stop=not cross)
                    if cross:
                        ins = pe.matmul(out_c, ident_b, mask_biasT[:, t, :], start=False, stop=True)
                    if i == 1:
                        ins.then_inc(scoresT_ready, 1)

                def weighted_values(b, g, t):
                    pe.wait_ge(probs_ready, b * (UNITS * HG) + UNITS * g + 2 * t + 2)
                    if t == 0:
                        pe.wait_ge(v_placed, b * HG + g + 1)
                        if not (isinstance(b, int) and b == 0 and g == 0):
                            pe.wait_ge(o_out, b * HG + g)
                    for j in range(4):
                        ins = pe.matmul(psum[PAD * j:PAD * j + PAD, O_BANK, :], V[:, t, 4 * g + j, :],
                                        probsT[:, t % 2, j, :], start=(t == 0), stop=(t == TT - 1),
                                        tile_position=(0, PAD * j))
                    ins.then_inc(av_ready, 1)

                def prepare():
                    for n, item in enumerate(prologue[:-1]):
                        item_products(item, 0, n)
                    pe.wait_ge(item_read, len(prologue) - 1)
                    for s in range(SCORES):
                        scores(0, 0, s)
                    item_products(prologue[-1], 0, len(prologue) - 1)

                def step(b, g, n, first, last):
                    ahead, group = divmod(g + 1, HG)
                    after = 0 if g == 1 or first else len(items(g - 1 if g else HG - 1, last=last)[-1][1])
                    pe.wait_ge(item_read, n - after)
                    s = 0
                    for u, (early, late) in enumerate(items(g, first, last)):
                        due = 0 if last and ahead else SCORES_IN[u]

                        def next_scores():
                            nonlocal due, s
                            if due:
                                scores(b + ahead, group, s)
                                due, s = due - 1, s + 1

                        next_scores()
                        scores_transposed(b, g, u, 0)
                        for item in early:
                            item_products(item, b, n)
                            n = n + 1
                        next_scores()
                        scores_transposed(b, g, u, 1)
                        if u == 1 and not first:
                            weighted_values(b - 1 if g == 0 else b, (g - 1) % HG, TT - 1)
                        if u in (3, 5, 7):
                            weighted_values(b, g, u // 2 - 1)
                        next_scores()
                        for item in late:
                            item_products(item, b, n)
                            n = n + 1

                n = sections(pe, prepare, step)
                weighted_values(B - 1, HG - 1, TT - 1)
                for i, item in enumerate((("SUM", 0, HG - 1), ("R", 0, HG - 1), ("OUT", 0, 0), ("OUT", 0, 1))):
                    item_products(item, B - 1, n + i)

            @block.scalar
            def _(act):
                def read_item(item, b, n):
                    kind, ahead, i = item
                    b = b + ahead
                    if kind not in ("T", "K", "Q", "KD", "QD", "M"):
                        return
                    act.wait_ge(item_ready, n + 1)
                    src = psum[:, M_BANK, :]
                    if kind in ("T", "K", "Q"):
                        s = SPLIT_OF[kind, i]
                        if not (isinstance(b, int) and b == 0 and s < 2):
                            act.wait_ge(low_ready, b * SPLITS + s - 1)
                        if kind == "T":
                            hi = source_h[:, i // KC, i % KC, :]
                        else:
                            hi = base_h[:, i, "KQ".index(kind), :]
                        for out in (full[:, s % 2, :], hi):
                            if kind == "T" and cross:
                                ins = act.activation(out, src, ACT.Copy)
                            elif kind == "T":
                                ins = act.activation(out, src, ACT.Identity, bias=ln_affine[:, 1, i:i + 1],
                                                     scale=ln_affine[:, 0, i:i + 1])
                            else:
                                scale = SCORE_SCALE if kind == "Q" else 1.0
                                if cross:
                                    bias = bias_kq[:, i, "KQ".index(kind):"KQ".index(kind) + 1]
                                    ins = act.activation(out, src, ACT.Identity, bias=bias, scale=scale)
                                else:
                                    ins = act.activation(out, src, ACT.Copy, scale=scale)
                    elif kind == "KD":
                        for j in range(2):
                            ins = act.activation(KT[0:96, 2 * i + j, :], src[0:96], ACT.Copy,
                                                 scale=const["keep_head"][0:96, j:j + 1])
                    elif kind == "QD":
                        ins = act.copy(QT[:, i, :], src)
                    elif kind == "M":
                        ins = act.copy(QT[96:P, GP * i:GP * i + GP, :],
                                       src[96:P].unsqueeze(1).to_broadcast([32, GP, S]))
                    ins.then_inc(item_read, 1)

                def exponentials(b, g, u):
                    act.wait_ge(scoresT_ready, b * (UNITS * HG) + UNITS * g + u + 1)
                    t = u // 2
                    if not (isinstance(b, int) and b == 0 and g == 0 and t < 2):
                        act.wait_ge(av_ready, b * NT + TT * g + t - 1)
                    at = C_BANK + 2 * (u % 2)
                    act.activation(probsT[:, t % 2, 2 * (u % 2):2 * (u % 2) + 2, :], psum[:, at:at + 2, :],
                                   ACT.Exp).then_inc(probs_ready, 1)

                def take_weighted(b, g):
                    act.wait_ge(av_ready, b * NT + TT * g + TT)
                    if not (isinstance(b, int) and b == 0 and g < 2):
                        act.wait_ge(norm_step, b * (2 * HG) + 2 * g)
                    act.copy(OT[:, g % 2, :], psum[:, O_BANK, :]).then_inc(o_out, 1)

                def prepare():
                    for n, item in enumerate(prologue):
                        read_item(item, 0, n)

                def step(b, g, n, first, last):
                    for u, (early, late) in enumerate(items(g, first, last)):
                        for item in early:
                            read_item(item, b, n)
                            n = n + 1
                        exponentials(b, g, u)
                        if u == 1 and not first:
                            take_weighted(b - 1 if g == 0 else b, (g - 1) % HG)
                        for item in late:
                            read_item(item, b, n)
                            n = n + 1

                sections(act, prepare, step)
                take_weighted(B - 1, HG - 1)

            @block.vector
            def _(dve):
                def read_item(item, b, n):
                    kind, ahead, i = item
                    b = b + ahead
                    if kind not in ("V", "MT", "SUM", "R", "OUT"):
                        return
                    dve.wait_ge(item_ready, n + 1)
                    src = psum[:, M_BANK, :]
                    two = src.rearrange("p (t e) -> p t e", t=2)
                    if kind == "V":
                        if not (isinstance(b, int) and b == 0):
                            dve.wait_ge(v_placed, b * HG)
                        out = V_next[:, 2 * i:2 * i + 2, :]
                        if cross:
                            ins = dve.tensor_tensor(out, two, bias_v[:].unsqueeze(1).to_broadcast([P, 2, D]), ALU.add)
                        else:
                            ins = dve.tensor_copy(out, two)
                    elif kind == "MT":
                        ins = dve.tensor_copy(mask_biasT[:, i, :], src[:, 0:S // 2].bitcast(BF16))
                    elif kind == "SUM":
                        dve.reciprocal(inv_sums[:].rearrange("p t j -> p (t j)"), src[:, 0:4 * TT]).then_inc(inverted, 1)
                        dve.wait_ge(inverted, b * HG + i + 1)
                        ins = dve.tensor_copy(inv_rows[:], inv_sums[:].unsqueeze(3).to_broadcast([P, TT, 4, PAD]))
                    elif kind == "R":
                        o = OT[:, i % 2, :]
                        ins = dve.tensor_tensor(o, o, src, ALU.mult)
                    elif kind == "OUT":
                        Xi = X[:, bass.ds(b * TT + 2 * i, 2), :]
                        dve.wait_ge(residual_step, (b + 1) * (1 if cross else 2))
                        ins = dve.tensor_tensor(Xi, two, Xi, ALU.add)
                    ins.then_inc(item_read, 1)

                def tile_of(x, b, t):
                    return x[:, bass.ds(b * TT + t, 1), :].rearrange("p o d -> p (o d)")

                def statistics(settled, i, tiles, src):
                    for t in tiles:
                        settled.link(dve.bn_stats(stats[:, t, :], src(t)))
                    settled.settle()
                    for t in tiles:
                        settled.link(dve.bn_aggr(moments[:, i, t, :], stats[:, t, :]))
                    settled.settle()
                    at = slice(tiles[0], tiles[-1] + 1)
                    variance, guess, bits = (work[:, w, at] for w in range(3))
                    inverse_deviation(settled, moments[:, i, at, 1], variance, inverse[:, i, at], guess, bits)

                def applied(i, dst, src, b, t):
                    at = b * TT + t
                    one = (lambda x: x[:, i, at:at + 1]) if isinstance(b, int) else (
                        lambda x: x[:, i, bass.ds(at, 1)])
                    mean = moments[:, i, at, 0:1] if isinstance(b, int) else moments[:, i].rearrange(
                        "p t w -> p (t w)")[:, bass.ds(2 * at, 1)]
                    return dve.tensor_scalar(dst, src, mean, one(inverse), ALU.subtract, ALU.mult)

                def layer_norms(b, i, steps):
                    if i == 0:
                        dve.wait_ge(v_placed, b * HG)
                        if not cross:
                            dve.wait_ge(residual_step, b * 2)
                    if i == 1:
                        steps.settle()
                    for t in range(TT):
                        src = tile_of(X, b, t) if i == 0 else X1[:, t, :]
                        dst = Z[:, t, :] if i == LN - 1 else X1[:, t, :]
                        ins = applied(i, dst, src, b, t)
                        if i == LN - 1 and t == TT - 1:
                            ins.then_inc(z_ready, 1)
                        else:
                            steps.link(ins)

                def prepare_norms():
                    settled = Count(dve, stats_step)
                    for b in range(B):
                        statistics(settled, 0, range(b * TT, b * TT + TT), lambda t: X[:, t, :])
                        if not cross:
                            if b == 1:
                                dve.wait_ge(residual_step, 2)
                            for t in range(TT):
                                settled.link(applied(0, X1[:, t, :], X[:, b * TT + t, :], b, t))
                            settled.settle()
                            statistics(settled, 1, range(b * TT, b * TT + TT), lambda t: X1[:, t % TT, :])
                        if b == 0:
                            for t in range(TT):
                                ins = applied(LN - 1, Z[:, t, :], X[:, t, :] if cross else X1[:, t, :], 0, t)
                                ins.then_inc(z_ready, 1) if t == TT - 1 else settled.link(ins)

                def maximum(b, g, s):
                    dve.wait_ge(scores_ready, b * (SCORES * HG) + SCORES * g + s + 1)
                    dve.tensor_reduce(neg_max[:, g % 2, s // 4, s % 4:s % 4 + 1], psum[:, S_BANK + s % 2, :], AX_X,
                                      ALU.max, negate=True).then_inc(max_ready, 1)
                    if s == SCORES - 1:
                        dve.wait_ge(max_ready, b * (SCORES * HG) + SCORES * g + SCORES)
                        hi = max_cols[:, :, 96:100]
                        dve.tensor_copy(hi, neg_max[:, g % 2]).then_inc(max_step, 1)
                        dve.wait_ge(max_step, b * HG + g + 1)
                        dve.tensor_tensor(max_cols[:, :, 100:104], neg_max[:, g % 2], hi.bitcast(F32),
                                          ALU.subtract).then_inc(max_split, 1)

                def prepare():
                    prepare_norms()
                    for n, item in enumerate(prologue[:-1]):
                        read_item(item, 0, n)
                    for s in range(SCORES):
                        maximum(0, 0, s)

                def step(b, g, n, first, last):
                    ahead, group = divmod(g + 1, HG)
                    s = 0
                    if g == 1 and not last:
                        steps = Count(dve, ln_step, b * NORM_STEPS)
                    for u, (early, late) in enumerate(items(g, first, last)):
                        if not (last and ahead):
                            for _ in range(SCORES_IN[u]):
                                maximum(b + ahead, group, s)
                                s += 1
                        if g == 1 and not last and u in (1, 4)[:LN]:
                            layer_norms(b + 1, u // 4, steps)
                        for item in early + late:
                            read_item(item, b, n)
                            n = n + 1

                n = sections(dve, prepare, step)
                for i, item in enumerate((("SUM", 0, HG - 1), ("R", 0, HG - 1), ("OUT", 0, 0), ("OUT", 0, 1))):
                    read_item(item, B - 1, n + i)




E = 4
F = 1024
FC = F // P
F2 = 512
C2 = F2 // P
G = 8
GRID = np.linspace(-1.2, 0.2, G).astype(np.float32)
N8 = 2 * E


def experts(nc, X, psum, const, dram):
    with ExitStack() as ctx:
        share = ctx.enter_context(nc.sbuf_tensor("share", [P, NT, N8], F32))
        h0T_dram = nc.dram_tensor("h0T_scratch", (B, P, KC * S), F32).ap()
        with ExitStack() as inner:
            hT_h = inner.enter_context(nc.sbuf_tensor("hT_h", [P, KC, NT * P], F32R))
            hT_l = inner.enter_context(nc.sbuf_tensor("hT_l", [P, KC, NT * P], F32R))
            route(nc, X, psum, const, dram, share, hT_h, hT_l, h0T_dram)
            mlp_experts(nc, X, psum, const, dram, share, hT_h, hT_l)
        kan_experts(nc, X, psum, const, dram, share, h0T_dram)


def route(nc, X, psum, const, dram, share, hT_h, hT_l, h0T_dram):
    LN = 2
    STEPS = LN * (3 * TT - 1) + 1 + 2 + 2 * TT + 4 + (2 * TT - 1) + 1
    with ExitStack() as ctx:
        def sb(name, shape, dt=F32):
            return ctx.enter_context(nc.sbuf_tensor(f"r_{name}", shape, dt))

        def sem(name):
            return ctx.enter_context(nc.semaphore(f"r_{name}"))

        gate = sb("gate", [P, KC, N8])
        bias8 = sb("bias8", [N8, D])
        stats, moments = sb("stats", [P, TT, 6]), sb("moments", [P, TT, 2])
        root, inverse = sb("root", [P, TT]), sb("inverse", [P, TT])
        Hn, H0 = sb("Hn", [P, TT, D]), sb("H0", [P, TT, D])
        hT, h0T = sb("hT", [P, KC, S]), sb("h0T", [P, KC, S])
        neg_top, total, inv_total = sb("neg_top", [P, TT]), sb("total", [P, TT]), sb("inv_total", [P, TT])
        expd, chance = sb("expd", [P, TT, N8]), sb("chance", [P, TT, N8])
        best, where = sb("best", [P, TT, 8]), sb("where", [P, TT, 8], U32)
        where_f = sb("where_f", [P, TT, 2])
        pair_sum, pair_inv, pair_share = sb("pair_sum", [P, TT]), sb("pair_inv", [P, TT]), sb("pair_share", [P, TT, 2])
        picked, shares = sb("picked", [P, 2, N8]), sb("shares", [P, TT, N8])
        sharesT = sb("sharesT", [N8, TT, P])

        weights_in, step = sem("weights_in"), sem("step")
        variance_ready, root_ready = sem("variance_ready"), sem("root_ready")
        h_ready, h0_ready, hT_psum, hT_ready = sem("h_ready"), sem("h0_ready"), sem("hT_psum"), sem("hT_ready")
        split_ready, stored = sem("split_ready"), sem("stored")
        logits_psum, top_ready, exp_ready = sem("logits_psum"), sem("top_ready"), sem("exp_ready")
        shares_ready, sharesT_psum, sharesT_ready = sem("shares_ready"), sem("sharesT_psum"), sem("sharesT_ready")
        bias_psum, x_done = sem("bias_psum"), sem("x_done")

        with nc.Block() as block:
            @block.sync
            def _(sp):
                with nc.allow_non_contiguous_dma(reason="the gate, once"):
                    sp.dma_start(gate[:], dram["gate_W"].rearrange("(c p) e -> p c e", p=P)).then_inc(weights_in, 16)
                sp.dma_start(bias8[0:E, :], dram["mlp_b2"]).then_inc(weights_in, 16)
                sp.dma_start(bias8[E:N8, :], dram["kan_sl_b1"]).then_inc(stored, 16)
                with sp.Fori(0, B) as b:
                    sp.wait_ge(hT_ready, b * 2 + 2)
                    sp.dma_start(h0T_dram[bass.ds(b, 1)].rearrange("o p s -> (o p) s"),
                                 h0T[:].rearrange("p c s -> p (c s)")).then_inc(stored, 16)
                sp.wait_ge(stored, 16 * B + 16)

            @block.tensor
            def _(pe):
                ident = const["ident"]
                pe.wait_ge(weights_in, 32)
                pe.wait_ge(stored, 16)
                with pe.Fori(0, B) as b:
                    for i, (src, ready) in enumerate(((Hn, h_ready), (H0, h0_ready))):
                        pe.wait_ge(ready, b + 1)
                        for c in range(KC):
                            for t in range(TT):
                                ins = pe.transpose(psum[:, 2 * i + c, t * P:(t + 1) * P],
                                                   src[:, t, c * P:(c + 1) * P], ident)
                        ins.then_inc(hT_psum, 1)
                    pe.wait_ge(hT_ready, b * 2 + 1)
                    for t in range(TT):
                        for c in range(KC):
                            ins = pe.matmul(psum[:, 4, t * N8:(t + 1) * N8], hT[:, c, t * P:(t + 1) * P],
                                            gate[:, c, :], start=(c == 0), stop=(c == KC - 1))
                    ins.then_inc(logits_psum, 1)
                    pe.wait_ge(shares_ready, b + 1)
                    for t in range(TT):
                        ins = pe.transpose(psum[0:N8, 5, t * P:(t + 1) * P], shares[:, t, :], ident)
                    ins.then_inc(sharesT_psum, 1)
                    pe.wait_ge(sharesT_ready, b + 1)
                    for t in range(TT):
                        ins = pe.matmul(psum[:, 6 + t // 2, t % 2 * D:(t % 2 + 1) * D], sharesT[:, t, :], bias8[:],
                                        start=True, stop=True)
                    ins.then_inc(bias_psum, 1)

            @block.scalar
            def _(act):
                with act.Fori(0, B) as b:
                    for i in range(LN):
                        act.wait_ge(variance_ready, b * LN + i + 1)
                        act.activation(root[:], moments[:, :, 1], ACT.Sqrt, bias=const["eps"]).then_inc(root_ready, 1)
                    for i, out in enumerate((hT, h0T)):
                        act.wait_ge(hT_psum, b * 2 + i + 1)
                        if i == 1:
                            act.wait_ge(stored, b * 16 + 16)
                        act.copy(out[:], psum[:, 2 * i:2 * i + 2, :]).then_inc(hT_ready, 1)
                    act.wait_ge(top_ready, b + 1)
                    for t in range(TT):
                        ins = act.activation(expd[:, t, :], psum[:, 4, t * N8:(t + 1) * N8], ACT.Exp,
                                             bias=neg_top[:, t:t + 1], accum_out=total[:, t:t + 1])
                    ins.then_inc(exp_ready, 1)
                    act.wait_ge(sharesT_psum, b + 1)
                    act.copy(sharesT[:].rearrange("e t p -> e (t p)"), psum[0:N8, 5, :]).then_inc(sharesT_ready, 1)

            @block.vector
            def _(dve):
                experts_row, signs = const["experts"], const["signs"]
                with dve.Fori(0, B) as b:
                    steps = Count(dve, step, b * STEPS)

                    def settled(ins):
                        steps.link(ins)
                        steps.settle()

                    Xt = lambda t: X[:, bass.ds(b * TT + t, 1), :].rearrange("p o d -> p (o d)")
                    rooms = (stats, moments, root, inverse, variance_ready, root_ready, const["vector_waited"])
                    layer_norm_vector(dve, steps, Xt, lambda t: Hn[:, t, :], TT, *rooms, b * LN + 1, h_ready)
                    dve.wait_ge(h_ready, b + 1)
                    layer_norm_vector(dve, steps, lambda t: Hn[:, t, :], lambda t: H0[:, t, :], TT, *rooms,
                                      b * LN + 2, h0_ready)
                    dve.wait_ge(hT_ready, b * 2 + 1)
                    at = bass.ds(b * S, S)
                    settled(dve.tensor_copy(hT_h[:, :, at], hT[:]))
                    dve.tensor_tensor(hT_l[:, :, at], hT[:], hT_h[:, :, at].bitcast(F32), ALU.subtract).then_inc(split_ready, 1)
                    dve.wait_ge(logits_psum, b + 1)
                    logits = psum[:, 4, 0:TT * N8].rearrange("p (t e) -> p t e", t=TT)
                    dve.tensor_reduce(neg_top[:], logits, AX_X, ALU.max, negate=True).then_inc(top_ready, 1)
                    dve.wait_ge(exp_ready, b + 1)
                    settled(dve.reciprocal(inv_total[:], total[:]))
                    steps.link(dve.tensor_tensor(chance[:], expd[:],
                                                 inv_total[:].unsqueeze(2).to_broadcast([P, TT, N8]), ALU.mult))
                    steps.settle()
                    dve.sem_inc(const["vector_waited"], 1)
                    for t in range(TT):
                        steps.link(dve.max(best[:, t, :], chance[:, t, :]))
                    steps.settle()
                    dve.sem_inc(const["vector_waited"], 1)
                    for t in range(TT):
                        steps.link(dve.max_index(where[:, t, :], best[:, t, :], chance[:, t, :]))
                    steps.settle()
                    settled(dve.tensor_copy(where_f[:], where[:, :, 0:2]))
                    settled(dve.tensor_tensor(pair_sum[:], best[:, :, 0], best[:, :, 1], ALU.add))
                    settled(dve.reciprocal(pair_inv[:], pair_sum[:]))
                    settled(dve.tensor_tensor(pair_share[:], best[:, :, 0:2],
                                              pair_inv[:].unsqueeze(2).to_broadcast([P, TT, 2]), ALU.mult))
                    for t in range(TT):
                        for i in range(2):
                            ins = dve.tensor_scalar(picked[:, i, :], experts_row, where_f[:, t, i:i + 1],
                                                    pair_share[:, t, i:i + 1], ALU.is_equal, ALU.mult)
                            if i == 1:
                                settled(ins)
                            else:
                                ins.then_inc(split_ready, 1)
                        ins = dve.tensor_tensor(shares[:, t, :], picked[:, 0, :], picked[:, 1, :], ALU.add)
                        if t == TT - 1:
                            ins.then_inc(shares_ready, 1)
                        else:
                            settled(ins)
                    dve.wait_ge(shares_ready, b + 1)
                    settled(dve.tensor_tensor(share[:, bass.ds(b * TT, TT), :], shares[:],
                                              signs.unsqueeze(1).to_broadcast([P, TT, N8]), ALU.mult))
                    dve.wait_ge(bias_psum, b + 1)
                    Xb = X[:, bass.ds(b * TT, TT), :]
                    dve.tensor_tensor(Xb, Xb, psum[:, 6:8, :].rearrange("p k (t d) -> p (k t) d", d=D),
                                      ALU.add).then_inc(x_done, 1)
                    assert steps.n == STEPS, (steps.n, STEPS)


def mlp_experts(nc, X, psum, const, dram, share, hT_h, hT_l):
    TURNS = E * B
    LAG = 2
    RING = 3
    UP_BANKS, DOWN_BANK = 4, 4
    CH = KC * P
    with ExitStack() as ctx:
        def sb(name, shape, dt=F32):
            return ctx.enter_context(nc.sbuf_tensor(f"m_{name}", shape, dt))

        def sem(name):
            return ctx.enter_context(nc.semaphore(f"m_{name}"))

        w1_h, w1_l = sb("w1_h", [P, FC, KC, P], F32R), sb("w1_l", [P, FC, KC, P], F32R)
        w2_h, w2_l = sb("w2_h", [P, FC, D], F32R), sb("w2_l", [P, FC, D], F32R)
        raw = sb("raw", [P, 2, FC, CH])
        b1 = sb("b1", [P, E, FC])
        hidden = sb("hidden", [P, 2, S])
        hid_h, hid_l = sb("hid_h", [P, 4, S], F32R), sb("hid_l", [P, 4, S], F32R)

        b1_in, w1_in, w2_in = sem("b1_in"), sem("w1_in"), sem("w2_in")
        high_ready, w1_ready, w2_ready = sem("high_ready"), sem("w1_ready"), sem("w2_ready")
        up_psum, gelu_ready, high_hidden, hidden_ready = (
            sem("up_psum"), sem("gelu_ready"), sem("high_hidden"), sem("hidden_ready"))
        down_used, out_ready, x_done = sem("down_used"), sem("out_ready"), sem("x_done")

        with nc.Block() as block:
            @block.sync
            def _(sp):
                with nc.allow_non_contiguous_dma(reason="4096 bias values, once"):
                    sp.dma_start(b1[:], dram["mlp_b1"].rearrange("e (f p) -> p e f", p=P)).then_inc(b1_in, 16)

                def load(e):
                    w1 = dram["mlp_W1"][e].rearrange("(c p) (f n) -> f p c n", p=P, f=FC)
                    w2 = dram["mlp_W2"][e].rearrange("(f p) d -> f p d", p=P)
                    return w1, w2

                w1 = dram["mlp_W1"].rearrange("e (c p) (f n) -> e c p f n", p=P, f=FC)
                w2 = dram["mlp_W2"].rearrange("e (f p) d -> e p f d", p=P)

                def fetch(e, first):
                    if not first:
                        sp.wait_ge(w1_ready, e * FC)
                    for c in range(KC):
                        src = w1[0, c] if first else w1[bass.ds(e, 1), c].rearrange("o p f n -> (o p) f n")
                        sp.dma_start(raw[:, 0].rearrange("p f (c n) -> p f c n", c=KC)[:, :, c, :],
                                     src).then_inc(w1_in, 16)
                    if not first:
                        sp.wait_ge(w2_ready, e * FC)
                    src = w2[0] if first else w2[bass.ds(e, 1)].rearrange("o p f d -> (o p) f d")
                    sp.dma_start(raw[:, 1], src).then_inc(w2_in, 16)

                fetch(0, True)
                with sp.Fori(1, E) as e:
                    fetch(e, False)

            @block.gpsimd
            def _(pool):
                def split_weights(e, first):
                    pool.wait_ge(w1_in, (e + 1) * 16 * KC)
                    pool.wait_ge(w2_in, (e + 1) * 16)
                    for f in range(FC):
                        last = (e * B - 1) * FC + f + 1
                        for i, (hi, lo, ready, used) in enumerate(
                                ((w1_h[:, f].rearrange("p c n -> p (c n)"), w1_l[:, f].rearrange("p c n -> p (c n)"),
                                  w1_ready, up_psum), (w2_h[:, f], w2_l[:, f], w2_ready, down_used))):
                            if not first:
                                pool.wait_ge(used, last)
                            pool.sem_inc(const["pool_waited"], 1)
                            pool.tensor_scalar(hi, raw[:, i, f], 1.0, 0.0, ALU.mult, ALU.add).then_inc(high_ready, 1)
                            pool.wait_ge(high_ready, e * 2 * FC + 2 * f + i + 1)
                            pool.tensor_tensor(lo, raw[:, i, f], hi.bitcast(F32), ALU.subtract).then_inc(ready, 1)

                split_weights(0, True)
                with pool.Fori(1, E) as e:
                    split_weights(e, False)

            @block.tensor
            def _(pe):
                def up(turn, e, batch, f):
                    pe.wait_ge(w1_ready, e * FC + f + 1)
                    n = turn * FC + f
                    if not (isinstance(turn, int) and f < UP_BANKS):
                        pe.wait_ge(gelu_ready, n - UP_BANKS + 1)
                    at = bass.ds(batch * S, S)
                    terms = [(w1_h[:, f, c, :], h[:, c, at]) for c in range(KC) for h in (hT_h, hT_l)]
                    terms += [(w1_l[:, f, c, :], hT_h[:, c, at]) for c in range(KC)]
                    for i, (lhsT, rhs) in enumerate(terms):
                        ins = pe.matmul(psum[:, f % UP_BANKS, :], lhsT, rhs, start=(i == 0), stop=(i == len(terms) - 1))
                    ins.then_inc(up_psum, 1)

                def down(turn, e, f):
                    pe.wait_ge(w2_ready, e * FC + f + 1)
                    pe.wait_ge(hidden_ready, turn * FC + f + 1)
                    if f == 0 and not isinstance(turn, int):
                        pe.wait_ge(x_done, turn * TT)
                    for t in range(TT):
                        out = psum[:, DOWN_BANK + t // 2, t % 2 * D:(t % 2 + 1) * D]
                        at = slice(t * P, (t + 1) * P)
                        for i, (hid, w) in enumerate(((hid_h, w2_h), (hid_h, w2_l), (hid_l, w2_h))):
                            ins = pe.matmul(out, hid[:, f % 4, at], w[:, f, :],
                                            start=(f == 0 and i == 0 and t % 2 == 0), stop=(f == FC - 1 and i == 2),
                                            skip_group_check=True)
                    ins.then_inc(down_used, 1)

                for f in range(FC):
                    up(0, 0, 0, f)
                    if f >= LAG:
                        down(0, 0, f - LAG)
                with pe.Fori(1, TURNS) as turn:
                    e, batch = turn // B, turn % B
                    before, e_before = turn - 1, (turn - 1) // B
                    for f in range(FC):
                        up(turn, e, batch, f)
                        if f >= LAG:
                            down(turn, e, f - LAG)
                        else:
                            down(before, e_before, FC + f - LAG)
                for f in range(FC - LAG, FC):
                    down(TURNS - 1, E - 1, f)

            @block.scalar
            def _(act):
                def gelu(turn, e, f):
                    n = turn * FC + f
                    act.wait_ge(up_psum, n + 1)
                    if not (isinstance(turn, int) and f < 2):
                        act.wait_ge(hidden_ready, n - 1)
                    act.activation(hidden[:, f % 2, :], psum[:, f % UP_BANKS, :], ACT.Gelu,
                                   bias=b1[:, bass.ds(e, 1), f]).then_inc(gelu_ready, 1)

                act.wait_ge(b1_in, 16)
                for f in range(FC):
                    gelu(0, 0, f)
                with act.Fori(1, TURNS) as turn:
                    e = turn // B
                    for f in range(FC):
                        gelu(turn, e, f)

            @block.vector
            def _(dve):
                def split_hidden(turn, f):
                    n = turn * FC + f
                    dve.wait_ge(gelu_ready, n + 1)
                    if not (isinstance(turn, int) and f < 4):
                        dve.wait_ge(down_used, n - 3)
                    dve.tensor_copy(hid_h[:, f % 4, :], hidden[:, f % 2, :]).then_inc(high_hidden, 1)
                    dve.wait_ge(high_hidden, n + 1)
                    dve.tensor_tensor(hid_l[:, f % 4, :], hidden[:, f % 2, :], hid_h[:, f % 4, :].bitcast(F32),
                                      ALU.subtract).then_inc(hidden_ready, 1)

                def add_output(turn, e, batch):
                    dve.wait_ge(down_used, turn * FC + FC)
                    for t in range(TT):
                        tile = batch * TT + t
                        Xt = X[:, bass.ds(tile, 1), :].rearrange("p o d -> p (o d)")
                        dve.scalar_tensor_tensor(Xt, psum[:, DOWN_BANK + t // 2, t % 2 * D:(t % 2 + 1) * D],
                                                 share_flat[:, bass.ds(tile * N8 + e, 1)], Xt,
                                                 ALU.mult, ALU.add).then_inc(x_done, 1)

                share_flat = share[:].rearrange("p t e -> p (t e)")
                for f in range(FC):
                    split_hidden(0, f)
                with dve.Fori(1, TURNS) as turn:
                    for f in range(FC):
                        split_hidden(turn, f)
                        if f == LAG - 1:
                            add_output(turn - 1, (turn - 1) // B, (turn - 1) % B)
                add_output(TURNS - 1, E - 1, B - 1)


def m_parity(layer, p):
    return p % 2


def kan_experts(nc, X, psum, const, dram, share, h0T_dram):
    TURNS = E * B
    PAIRS0, PAIRS1 = KC * G // 2, C2 * G // 2
    BODY = PAIRS0 + PAIRS1
    CHUNK = 1024
    CH0, CH1 = KC * G * F2 // CHUNK, C2 * G * D // CHUNK
    Z_BANKS, Y_BANK, T_BANK = TT, 4, 6
    LN_AT, T_AT, EVAC_AT = (1, 2, 3), (4, 6), 2
    STEPS = TT + TT + 3 + 4 * 3 + TT - 1

    def pair0(turn, p):
        return p if isinstance(turn, int) and turn == 0 else PAIRS0 + (turn - 1) * BODY + p

    def pair1(turn, p):
        if isinstance(turn, int) and turn == TURNS - 1:
            return PAIRS0 + (TURNS - 1) * BODY + p
        return PAIRS0 + turn * BODY + PAIRS0 + p

    with ExitStack() as ctx:
        def sb(name, shape, dt=F32):
            return ctx.enter_context(nc.sbuf_tensor(f"k_{name}", shape, dt))

        def sem(name):
            return ctx.enter_context(nc.semaphore(f"k_{name}"))

        w0_h, w0_l = sb("w0_h", [P, KC * G, F2], F32R), sb("w0_l", [P, KC * G, F2], F32R)
        w1_h, w1_l = sb("w1_h", [P, C2 * G, D], F32R), sb("w1_l", [P, C2 * G, D], F32R)
        raw = sb("raw", [P, 2, CHUNK])
        bias0 = sb("bias0", [P, E, F2])
        gains0, offsets0 = sb("gains0", [P, E * KC]), sb("offsets0", [P, E * KC])
        gains1, offsets1 = sb("gains1", [P, E * C2]), sb("offsets1", [P, E * C2])
        shifts0, shifts1 = sb("shifts0", [P, E * KC, G]), sb("shifts1", [P, E * C2, G])
        h0T = sb("h0T", [P, KC, S])
        h1T = sb("h1T", [P, C2, S])
        square = sb("square", [P, 2, 2, S])
        basis_h, basis_l = sb("basis_h", [P, 2, 2, S], F32R), sb("basis_l", [P, 2, 2, S], F32R)
        Z = sb("Z", [P, TT, F2])
        stats, moments = sb("stats", [P, TT, 6]), sb("moments", [P, TT, 2])
        variance, inverse = sb("variance", [P, TT]), sb("inverse", [P, TT])
        work = sb("work", [P, 2, TT])

        params_in, params_ready, params_step = sem("params_in"), sem("params_ready"), sem("params_step")
        raw_in = [sem("raw_in0"), sem("raw_in1")]
        w_high, w_ready = sem("w_high"), sem("w_ready")
        h0_in = sem("h0_in")
        tanh_ready, square_ready, basis_high, basis_ready, pair_used = (
            sem("tanh_ready"), sem("square_ready"), sem("basis_high"), sem("basis_ready"), sem("pair_used"))
        z_out, norm_step, z_normed, h1T_psum, h1T_ready = (
            sem("z_out"), sem("norm_step"), sem("z_normed"), sem("h1T_psum"), sem("h1T_ready"))
        z_tile, x_done = sem("z_tile"), sem("x_done")
        layers = ((KC, h0T, gains0, shifts0), (C2, h1T, gains1, shifts1))

        with nc.Block() as block:
            @block.sync
            def _(sp):
                with nc.allow_non_contiguous_dma(reason="6144 values, once"):
                    for name, dst in (("kan_ln_g0", gains0), ("kan_ln_b0", offsets0),
                                      ("kan_ln_g1", gains1), ("kan_ln_b1", offsets1)):
                        sp.dma_start(dst[:], dram[name].rearrange("e (c p) -> p (e c)", p=P)).then_inc(params_in, 16)
                for e in range(E):
                    sp.dma_start(bias0[:, e, :], dram["kan_sl_b0"][e].partition_broadcast(P)).then_inc(params_in, 16)
                w0 = dram["kan_sl_W0"].rearrange("e (c p g) n -> e c p g n", p=P, g=G)
                w1 = dram["kan_sl_W1"].rearrange("e (c p g) n -> e c p g n", p=P, g=G)
                G0, G1 = CHUNK // F2, CHUNK // D

                def fetch(e, first):
                    for layer, (w, step, chunks) in enumerate(((w0, G0, CH0), (w1, G1, CH1))):
                        for n in range(chunks):
                            place = e * (CH0 + CH1) + layer * CH0 + n
                            if not (first and place < 2):
                                sp.wait_ge(w_ready, place - 1)
                            c, g = divmod(n * step, G)
                            src = w[0, c] if first else w[bass.ds(e, 1), c].rearrange("o p g n -> (o p) g n")
                            sp.dma_start(raw[:, n % 2].rearrange("p (g n) -> p g n", g=step),
                                         src[:, g:g + step, :]).then_inc(raw_in[n % 2], 16)

                fetch(0, True)
                with sp.Fori(1, E) as e:
                    fetch(e, False)

            @block.gpsimd
            def _(pool):
                def split_weights(e, first):
                    for layer, (wh, wl, chunks) in enumerate(((w0_h, w0_l, CH0), (w1_h, w1_l, CH1))):
                        rows = wh.shape[1] // chunks
                        for n in range(chunks):
                            place = e * (CH0 + CH1) + layer * CH0 + n
                            pool.wait_ge(raw_in[n % 2], e * 8 * (CH0 + CH1) + (layer * CH0 + n) // 2 * 16 + 16)
                            if not first:
                                last = pair0(e * B - 1, n) if layer == 0 else pair1(e * B - 1, 2 * n + 1)
                                pool.wait_ge(pair_used, last + 1)
                            hi, lo = (w[:, n * rows:(n + 1) * rows, :].rearrange("p k n -> p (k n)") for w in (wh, wl))
                            pool.sem_inc(const["pool_waited"], 1)
                            pool.tensor_scalar(hi, raw[:, n % 2], 1.0, 0.0, ALU.mult, ALU.add).then_inc(w_high, 1)
                            pool.wait_ge(w_high, place + 1)
                            pool.tensor_tensor(lo, raw[:, n % 2], hi.bitcast(F32), ALU.subtract).then_inc(w_ready, 1)

                split_weights(0, True)
                with pool.Fori(1, E) as e:
                    split_weights(e, False)

            @block.scalar
            def _(act):
                def fetch_h0(batch):
                    src = h0T_dram[batch] if isinstance(batch, int) else h0T_dram[bass.ds(batch, 1)].rearrange(
                        "o p s -> (o p) s")
                    act.dma_start(h0T[:].rearrange("p c s -> p (c s)"), src).then_inc(h0_in, 16)

                def basis(layer, e, p, m):
                    chunks, x, gains, shifts = layers[layer]
                    c, g = divmod(2 * p, G)
                    room = square[:, m_parity(layer, p), :, :]
                    if not (isinstance(m, int) and m < 2):
                        act.wait_ge(basis_ready, m - 1)
                    at = bass.ds(e * chunks + c, 1)
                    for q in range(2):
                        ins = act.activation(room[:, q, :], x[:, c, :], ACT.Tanh, bias=shifts[:, at, g + q],
                                             scale=gains[:, at])
                    ins.then_inc(tanh_ready, 1)
                    act.wait_ge(tanh_ready, m + 1)
                    act.activation(room, room, ACT.Square).then_inc(square_ready, 1)

                def transposed(turn):
                    act.wait_ge(h1T_psum, turn * 2 + 1)
                    act.copy(h1T[:, 0:2, :], psum[:, T_BANK:T_BANK + 2, :]).then_inc(h1T_ready, 1)

                def transposed_rest(turn):
                    act.wait_ge(h1T_psum, turn * 2 + 2)
                    act.copy(h1T[:, 2:4, :], psum[:, T_BANK:T_BANK + 2, :]).then_inc(h1T_ready, 1)

                def first_layer(turn, e, with_last=True):
                    act.wait_ge(h0_in, turn * 16 + 16)
                    for p in range(PAIRS0):
                        basis(0, e, p, pair0(turn, p))
                        if with_last and p == T_AT[0]:
                            transposed(turn - 1)
                        if with_last and p == T_AT[1]:
                            transposed_rest(turn - 1)
                    fetch_h0((turn + 1) % B)

                def second_layer(turn, e):
                    act.wait_ge(h1T_ready, turn * 2 + 2)
                    for p in range(PAIRS1):
                        basis(1, e, p, pair1(turn, p))

                act.wait_ge(params_ready, 1)
                fetch_h0(0)
                first_layer(0, 0, with_last=False)
                first_layer(1, 0)
                second_layer(0, 0)
                with act.Fori(2, TURNS) as turn:
                    first_layer(turn, turn // B)
                    second_layer(turn - 1, (turn - 1) // B)
                transposed(TURNS - 1)
                transposed_rest(TURNS - 1)
                second_layer(TURNS - 1, E - 1)
                act.wait_ge(h0_in, 16 * TURNS + 16)

            @block.tensor
            def _(pe):
                def products(outs, layer, p, m, w_h, w_l, first, last):
                    pe.wait_ge(basis_ready, m + 1)
                    r = m_parity(layer, p)
                    for q in range(2):
                        k = 2 * p + q
                        for t, (out, opens) in enumerate(outs):
                            at = slice(t * P, (t + 1) * P)
                            for i, (x, w) in enumerate(((basis_h, w_h), (basis_h, w_l), (basis_l, w_h))):
                                ins = pe.matmul(out, x[:, r, q, at], w[:, k, :],
                                                start=(first and q == 0 and i == 0 and opens),
                                                stop=(last and q == 1 and i == 2), skip_group_check=True)
                    ins.then_inc(pair_used, 1)

                def transposes(turn, half):
                    pe.wait_ge(z_normed, turn + 1)
                    n = turn * 2 + half
                    if not (isinstance(turn, int) and n == 0):
                        pe.wait_ge(h1T_ready, n)
                    for c in range(2):
                        for t in range(TT):
                            ins = pe.transpose(psum[:, T_BANK + c, t * P:(t + 1) * P],
                                               Z[:, t, (2 * half + c) * P:(2 * half + c + 1) * P], const["ident"])
                    ins.then_inc(h1T_psum, 1)

                def first_layer(turn, e, with_last=True):
                    if with_last:
                        pe.wait_ge(z_out, turn)
                    for p in range(PAIRS0):
                        pe.wait_ge(w_ready, e * (CH0 + CH1) + p + 1)
                        products([(psum[:, t, :], True) for t in range(TT)], 0, p, pair0(turn, p),
                                 w0_h, w0_l, p == 0, p == PAIRS0 - 1)
                        if with_last and p + 1 in T_AT:
                            transposes(turn - 1, T_AT.index(p + 1))

                def second_layer(turn, e):
                    if not (isinstance(turn, int) and turn == 0):
                        pe.wait_ge(x_done, turn * TT)
                    for p in range(PAIRS1):
                        pe.wait_ge(w_ready, e * (CH0 + CH1) + CH0 + p // 2 + 1)
                        products([(psum[:, Y_BANK + t // 2, t % 2 * D:(t % 2 + 1) * D], t % 2 == 0)
                                  for t in range(TT)], 1, p, pair1(turn, p), w1_h, w1_l, p == 0, p == PAIRS1 - 1)

                first_layer(0, 0, with_last=False)
                first_layer(1, 0)
                second_layer(0, 0)
                with pe.Fori(2, TURNS) as turn:
                    first_layer(turn, turn // B)
                    second_layer(turn - 1, (turn - 1) // B)
                for half in range(2):
                    transposes(TURNS - 1, half)
                second_layer(TURNS - 1, E - 1)

            @block.vector
            def _(dve):
                share_flat = share[:].rearrange("p t e -> p (t e)")

                def basis(layer, p, m):
                    r = m_parity(layer, p)
                    dve.wait_ge(square_ready, m + 1)
                    if not (isinstance(m, int) and m < 2):
                        dve.wait_ge(pair_used, m - 1)
                    dve.tensor_scalar(basis_h[:, r], square[:, r], -1.0, None, ALU.add).then_inc(basis_high, 1)
                    dve.wait_ge(basis_high, m + 1)
                    flat = [x[:, r].rearrange("p q s -> p (q s)") for x in (basis_l, square, basis_h)]
                    dve.scalar_tensor_tensor(flat[0], flat[1], 1.0, flat[2].bitcast(F32),
                                             ALU.subtract, ALU.subtract).then_inc(basis_ready, 1)

                def evacuate(turn, e):
                    dve.wait_ge(pair_used, pair0(turn, PAIRS0 - 1) + 1)
                    if not (isinstance(turn, int) and turn == 0):
                        dve.wait_ge(h1T_psum, turn * 2)
                    for t in range(TT):
                        ins = dve.scalar_tensor_tensor(Z[:, t, :], psum[:, t, :], -1.0, bias0[:, bass.ds(e, 1), :].rearrange(
                            "p o n -> p (o n)"), ALU.mult, ALU.add)
                        ins.then_inc(z_out, 1) if t == TT - 1 else ins.then_inc(z_tile, 1)

                def layer_norm(turn, part, steps):
                    if part == 0:
                        dve.wait_ge(z_out, turn + 1)
                        for t in range(TT):
                            steps.link(dve.bn_stats(stats[:, t, :], Z[:, t, :]))
                        steps.settle()
                    elif part == 1:
                        for t in range(TT):
                            steps.link(dve.bn_aggr(moments[:, t, :], stats[:, t, :]))
                        steps.settle()
                        def settled(ins):
                            steps.link(ins)
                            steps.settle()

                        guess, bits = work[:, 0, :], work[:, 1, :].bitcast(I32)
                        settled(dve.tensor_scalar(variance[:], moments[:, :, 1], EPS, None, ALU.add))
                        settled(dve.tensor_scalar(bits, variance[:].bitcast(I32), 1, None, ALU.logical_shift_right))
                        settled(dve.tensor_scalar(inverse[:].bitcast(I32), bits, -1.0, float(0x5F3759DF),
                                                  ALU.mult, ALU.add))
                        for _ in range(3):
                            settled(dve.tensor_tensor(guess, inverse[:], inverse[:], ALU.mult))
                            settled(dve.tensor_tensor(guess, guess, variance[:], ALU.mult))
                            settled(dve.tensor_scalar(guess, guess, -0.5, 1.5, ALU.mult, ALU.add))
                            settled(dve.tensor_tensor(inverse[:], inverse[:], guess, ALU.mult))
                    else:
                        for t in range(TT):
                            ins = dve.tensor_scalar(Z[:, t, :], Z[:, t, :], moments[:, t, 0:1], inverse[:, t:t + 1],
                                                    ALU.subtract, ALU.mult)
                            if t == TT - 1:
                                ins.then_inc(z_normed, 1)
                            else:
                                steps.link(ins)
                        assert steps.n == STEPS, (steps.n, STEPS)

                def add_output(turn, e, batch):
                    dve.wait_ge(pair_used, pair1(turn, PAIRS1 - 1) + 1)
                    for t in range(TT):
                        tile = batch * TT + t
                        Xt = X[:, bass.ds(tile, 1), :].rearrange("p o d -> p (o d)")
                        dve.scalar_tensor_tensor(Xt, psum[:, Y_BANK + t // 2, t % 2 * D:(t % 2 + 1) * D],
                                                 share_flat[:, bass.ds(tile * N8 + E + e, 1)], Xt,
                                                 ALU.mult, ALU.add).then_inc(x_done, 1)

                def body(turn, e, before, e_before, second=False):
                    steps = Count(dve, norm_step, before * STEPS)
                    for p in range(PAIRS0):
                        basis(0, p, pair0(turn, p))
                        if p == 0 and not second:
                            add_output(turn - 2, (turn - 2) // B, (turn - 2) % B)
                        if p in LN_AT:
                            layer_norm(before, LN_AT.index(p), steps)
                    for p in range(PAIRS1):
                        basis(1, p, pair1(before, p))
                        if p == EVAC_AT:
                            evacuate(turn, e)

                dve.wait_ge(params_in, 16 * (4 + E))
                n = 0
                for gains in (gains0, gains1):
                    dve.tensor_scalar(gains[:], gains[:], 0.5, None, ALU.mult).then_inc(params_step, 1)
                    n += 1
                for offsets, shifts in ((offsets0, shifts0), (offsets1, shifts1)):
                    for g in range(G):
                        dve.tensor_scalar(shifts[:, :, g], offsets[:], float(-GRID[g]), 0.5,
                                          ALU.add, ALU.mult).then_inc(params_step, 1)
                        n += 1
                dve.wait_ge(params_step, n)
                dve.tensor_copy(work[:, 0, :], gains0[:, 0:TT]).then_inc(params_ready, 1)

                for p in range(PAIRS0):
                    basis(0, p, pair0(0, p))
                evacuate(0, 0)
                body(1, 0, 0, 0, second=True)
                with dve.Fori(2, TURNS) as turn:
                    body(turn, turn // B, turn - 1, (turn - 1) // B)
                add_output(TURNS - 2, E - 1, B - 2)
                steps = Count(dve, norm_step, (TURNS - 1) * STEPS)
                for part in range(3):
                    layer_norm(TURNS - 1, part, steps)
                for p in range(PAIRS1):
                    basis(1, p, pair1(TURNS - 1, p))
                add_output(TURNS - 1, E - 1, B - 1)


def constants_on_host():
    marks = np.zeros((P, 28), np.float32)
    marks[np.arange(4) * PAD + HD, 24 + np.arange(4)] = 1
    for j in range(4):
        marks[[96 + j, 100 + j], j] = 1
    marks[0:48, 4] = marks[48:96, 5] = 1
    marks[:, 6] = EPS
    marks[:, 8:16] = np.arange(8)
    marks[:, 16:24] = np.where(np.arange(8) < 4, 1, -1)
    select = np.zeros((P, 4, 2, 2, P), np.float32)
    for pair in range(4):
        for which, parts in enumerate(((0, 1, 0), (0, 0, 1))):
            for place, part in enumerate(parts):
                for head in range(2):
                    for d in range(HD):
                        select[2 * HD * pair + HD * head + d, pair, which, part, 48 * head + HD * place + d] = 1
    return {"ident": np.eye(P, dtype=np.float32), "marks": marks, "select": select}


def build(nc, dram, out):
    with ExitStack() as ctx:
        def keep(name, shape, dt=F32):
            return ctx.enter_context(nc.sbuf_tensor(name, shape, dt))

        X = keep("X", [P, NT, D])
        ident, ident_b, marks = keep("ident", [P, P]), keep("ident_b", [P, P], BF16), keep("marks", [P, 28])
        psum = ctx.enter_context(nc.psum_tensor("psum", [P, 8, 512], F32))
        const_in, const_ready, vector_waited, pool_waited = (ctx.enter_context(nc.semaphore(n)) for n in (
            "const_in", "const_ready", "vector_waited", "pool_waited"))
        const = {"ident": ident[:], "ident_b": ident_b[:], "select_max": marks[:, 0:4], "keep_head": marks[:, 4:6],
                 "eps": marks[:, 6:7], "experts": marks[:, 8:16], "signs": marks[:, 16:24], "pick_sums": marks[:, 24:28],
                 "vector_waited": vector_waited, "pool_waited": pool_waited}
        with ExitStack() as inner:
            def sb(name, shape, dt=F32):
                return inner.enter_context(nc.sbuf_tensor(name, shape, dt))

            ident_r = sb("ident_r", [P, P], F32R)
            select = sb("select", [P, 4, 2, 2, P], F32R)
            const.update(ident_r=ident_r[:], select=select)
            with nc.sbuf_tensor("select_in", [P, 4, 2, 2, P], F32) as select_in, nc.Block() as block:
                @block.sync
                def _(sp):
                    for dst, name in ((ident, "ident"), (marks, "marks"), (select_in, "select")):
                        sp.dma_start(dst[:], dram[name]).then_inc(const_in, 16)

                @block.vector
                def _(dve):
                    dve.wait_ge(const_in, 48)
                    dve.tensor_copy(ident_b[:], ident[:]).then_inc(const_ready, 1)
                    dve.tensor_copy(ident_r[:], ident[:]).then_inc(const_ready, 1)
                    dve.tensor_copy(select[:], select_in[:]).then_inc(const_ready, 1)
                    dve.wait_ge(const_ready, 3)
            attention(nc, False, X, psum, const, dram)
            attention(nc, True, X, psum, const, dram)
        experts(nc, X, psum, const, dram)
        stored = ctx.enter_context(nc.semaphore("stored"))
        with nc.Block() as block:
            @block.sync
            def _(sp):
                sp.dma_start(out.rearrange("(t p) d -> p t d", p=P), X[:]).then_inc(stored, 16)
                sp.wait_ge(stored, 16)


INPUTS = {
    "x": "x", "ctx": "ctx_1024", "mask": "mask_Bx1xSxS2_if1",
    "ln_scale": "L0_attn_ln_scale", "ln_bias": "L0_attn_ln_bias", "w_qkv": "L0_attn_w_qkv",
    "w_proj": "L0_attn_w_proj", "b_proj": "L0_attn_b_proj",
    "Wq": "L0_xattn_Wq", "bq": "L0_xattn_bq", "Wk": "L0_xattn_Wk", "bk": "L0_xattn_bk",
    "Wv": "L0_xattn_Wv", "bv": "L0_xattn_bv", "Wo": "L0_xattn_Wo", "bo": "L0_xattn_bo",
    "gate_W": "L0_ffn_gate_W", "mlp_W1": "L0_ffn_mlp_W1", "mlp_b1": "L0_ffn_mlp_b1",
    "mlp_W2": "L0_ffn_mlp_W2", "mlp_b2": "L0_ffn_mlp_b2",
    "kan_ln_g0": "L0_ffn_kan_ln_g0", "kan_ln_b0": "L0_ffn_kan_ln_b0",
    "kan_sl_W0": "L0_ffn_kan_sl_W0", "kan_sl_b0": "L0_ffn_kan_sl_b0",
    "kan_ln_g1": "L0_ffn_kan_ln_g1", "kan_ln_b1": "L0_ffn_kan_ln_b1",
    "kan_sl_W1": "L0_ffn_kan_sl_W1", "kan_sl_b1": "L0_ffn_kan_sl_b1",
}
RESHAPED = {"x": (B * S, D), "ctx": (B * S, D), "mask": (B, S, S)}


def kernel(**inputs):
    import concourse.bacc as bacc
    from concourse.bass_utils import run_bass_kernel_spmd

    nc = bacc.Bacc("TRN2", target_bir_lowering=False, num_devices=1)
    arrays = constants_on_host()
    for name, given in INPUTS.items():
        a = np.ascontiguousarray(inputs[given])
        arrays[name] = a.reshape(RESHAPED.get(name, a.shape))
    dram = {name: nc.dram_tensor(f"in_{name}", a.shape, mybir.dt.from_np(a.dtype), kind="ExternalInput").ap()
            for name, a in arrays.items()}
    out = nc.dram_tensor("out", (B * S, D), F32, kind="ExternalOutput").ap()
    build(nc, dram, out)
    result = run_bass_kernel_spmd(nc, [{f"in_{name}": a for name, a in arrays.items()}], core_ids=[0])
    return result.results[0]["out"].reshape(B, S, D)
```

```python
from contextlib import ExitStack

import numpy as np

import concourse.bass as bass
from concourse import mybir

F32 = mybir.dt.float32
F32R = mybir.dt.float32r
BF16 = mybir.dt.bfloat16
I32 = mybir.dt.int32
U32 = mybir.dt.uint32
ALU = mybir.AluOpType
ACT = mybir.ActivationFunctionType
AX_X = mybir.AxisListType.X

P = 128
B, S, D = 4, 512, 256
TT = S // P
NT = B * TT
KC = D // P
H, HD = 16, 16
HP = H // 2
HG = H // 4
GP = HP // HG
PAD = 32
EPS = 1e-5
MASKED = -2.0 ** 60
SCORE_SCALE = 1.0 / float(np.sqrt(HD))


class Count:

    def __init__(self, eng, sem, base=0):
        self.eng, self.sem, self.base, self.n = eng, sem, base, 0

    def link(self, ins):
        self.n += 1
        ins.then_inc(self.sem, 1)

    def settle(self):
        self.eng.wait_ge(self.sem, self.base + self.n)

    def __call__(self, ins):
        self.link(ins)
        self.settle()


def inverse_deviation(settled, moments, variance, inverse, guess, bits):
    dve = settled.eng
    settled(dve.tensor_scalar(variance, moments, EPS, None, ALU.add))
    settled(dve.tensor_scalar(bits.bitcast(I32), variance.bitcast(I32), 1, None, ALU.logical_shift_right))
    settled(dve.tensor_scalar(inverse.bitcast(I32), bits.bitcast(I32), -1.0, float(0x5F3759DF), ALU.mult, ALU.add))
    for _ in range(3):
        settled(dve.tensor_tensor(guess, inverse, inverse, ALU.mult))
        settled(dve.tensor_tensor(guess, guess, variance, ALU.mult))
        settled(dve.tensor_scalar(guess, guess, -0.5, 1.5, ALU.mult, ALU.add))
        settled(dve.tensor_tensor(inverse, inverse, guess, ALU.mult))


def attention(nc, cross, X, psum, const, dram, load_constants=None, prepare_constants=None):
    k = "x" if cross else "s"
    SRC = 2 if cross else 1
    UNITS = 8
    SCORES = 4 * TT
    SCORES_IN = (3, 3, 3, 3, 2, 2, 0, 0)
    TILES = H * TT
    SPLITS = SRC * KC + 2 * KC
    LN = 1 if cross else 2
    NORM_STEPS = TT * LN - 1
    S_BANK, C_BANK, ITEM_BANK, O_BANK = 0, 2, 5, 7

    def items(g, first=False, last=False):
        units = [([], []) for _ in range(UNITS)]

        def put(u, *item, late=False):
            units[u][late].append(item)

        ahead, group = divmod(g + 2, HG)
        if not (last and ahead):
            for i, (at_k, at_q) in enumerate(((2, 3), (5, 6)) if g == 2 else ((0, 1), (2, 5))):
                put(at_k, "KD", ahead, GP * group + i)
                put(at_q, "QD", ahead, GP * group + i, late=(g == 2 and i == 0))
        if not first:
            put(2, "SUM", -1 if g == 0 else 0, (g - 1) % HG, late=True)
            put(4, "R", -1 if g == 0 else 0, (g - 1) % HG)
        if not (last and g == HG - 1):
            put(7, "M", *divmod(g + 1, HG))
        if g == 0 and not first:
            if cross:
                put(2, "MT", 0, TT - 1, late=True)
            put(6, "OUT", -1, 0)
            put(7, "OUT", -1, 1, late=True)
        if g == 1 and not last:
            if cross:
                put(1, "T", 1, 0, late=True)
                put(4, "T", 1, 1, late=True)
            put(5, "T", 1, SRC * KC - 2, late=True)
            put(6, "T", 1, SRC * KC - 1)
        if g == 2 and not last:
            put(0, "K", 1, 0)
            put(1, "Q", 1, 0)
            put(4, "V", 1, 0, late=True)
            put(5, "V", 1, 1, late=True)
        if g == 3 and not last:
            put(6, "K", 1, 1)
            put(7, "Q", 1, 1, late=True)
            if cross:
                for t in range(TT - 1):
                    put(2 * t + 2, "MT", 1, t, late=True)
        return units

    prologue = [("T", 0, i) for i in range(SRC * KC)]
    for c in range(KC):
        prologue += [("K", 0, c), ("Q", 0, c)]
        prologue += [(kind, 0, GP * c + i) for i in range(GP) for kind in ("KD", "QD")]
    SCORES_FROM = prologue.index(("QD", 0, GP - 1)) + 1
    prologue += [("V", 0, i) for i in range(2)]
    if cross:
        prologue += [("MT", 0, t) for t in range(TT)]
    prologue += [("M", 0, 0)]
    count = lambda units: sum(len(early + late) for early, late in units)
    END = [("SUM", 0, HG - 1), ("R", 0, HG - 1), ("OUT", 0, 0), ("OUT", 0, 1)]
    IN_FIRST = len(prologue) + count(items(0, first=True))
    IN_ROUND = sum(count(items(g)) for g in range(HG))
    assert IN_ROUND % 2 == 0
    SPLIT_OF = {("T", i): i for i in range(SRC * KC)}
    SPLIT_OF.update({(kind, c): SRC * KC + 2 * c + i for c in range(KC) for i, kind in enumerate(("K", "Q"))})

    with ExitStack() as ctx:
        def sb(name, shape, dt=F32):
            return ctx.enter_context(nc.sbuf_tensor(f"{k}_{name}", shape, dt))

        def sem(name):
            return ctx.enter_context(nc.semaphore(f"{k}_{name}"))

        wq, wk, wv = ([sb(f"{n}_{part}", [P, KC, D], F32R) for part in "hl"] for n in ("wq", "wk", "wv"))
        wo_h, wo_l = sb("wo_h", [P, HG, D], F32R), sb("wo_l", [P, HG, D], F32R)
        bias_out = sb("bias_out", [P, D])

        stats = const["x_stats"] if cross else sb("stats", [P, NT, 6])
        moments = sb("moments", [P, LN, NT, 2])
        inverse, work = sb("inverse", [P, LN, NT]), sb("work", [P, 3, NT])
        Z = sb("Z", [P, TT, D])
        full = sb("full", [P, 2, S])
        source_h, source_l = sb("source_h", [P, SRC, KC, S], F32R), sb("source_l", [P, SRC, KC, S], F32R)
        base_h, base_l = sb("base_h", [P, KC, 2, S], F32R), sb("base_l", [P, KC, 2, S], F32R)
        KT = sb("KT", [P, H, S], F32R)
        QT = sb("QT", [P, HP, S], F32R)
        V = sb("V", [P, TT, H, PAD])
        V_next = Z
        neg_max = sb("neg_max", [P, 2, TT, 4])
        max_cols = sb("max_cols", [P, TT, P], F32R)
        probsT = sb("probsT", [P, 2, 4, S])
        OT = sb("OT", [P, 2, S])
        inv_sums, inv_rows = sb("inv_sums", [P, TT, 4]), sb("inv_rows", [P, TT, 4, PAD])
        OT_h, OT_l = sb("OT_h", [P, HG, S], F32R), sb("OT_l", [P, HG, S], F32R)

        weights_in, small_in, wo_cleared, wo_placed = (sem(n) for n in ("weights_in", "small_in", "wo_cleared", "wo_placed"))
        w_full, w_high, w_low, w_transposed = (sem(n) for n in ("w_full", "w_high", "w_low", "w_transposed"))
        x_rest_in = sem("x_rest_in")
        prep, cleared, x_in, wo_in, const_in = sem("prep"), sem("cleared"), sem("x_in"), sem("wo_in"), const["in"]
        new_stats = sem("new_stats")
        stats_steps = []
        item_ready, item_read = sem("item_ready"), [sem("item_read_0"), sem("item_read_1")]
        stats_step, ln_step, max_step, z_ready = sem("stats_step"), sem("ln_step"), sem("max_step"), sem("z_ready")
        residual_step, low_ready, v_placed = sem("residual_step"), sem("low_ready"), sem("v_placed")
        scores_ready, max_ready, max_split = sem("scores_ready"), sem("max_ready"), sem("max_split")
        scoresT_ready, probs_ready, inverted = sem("scoresT_ready"), sem("probs_ready"), sem("inverted")
        av_ready, o_out, norm_step = sem("av_ready"), sem("o_out"), sem("norm_step")
        if cross:
            CTX = sb("CTX", [P, TT, D])
            mask = sb("mask", [P, TT, S], I32)
            mask_bias, mask_biasT = sb("mask_bias", [P, TT, S], BF16), sb("mask_biasT", [P, TT, S], BF16)
            bias_kq = sb("bias_kq", [P, KC, 2])
            bias_v = sb("bias_v", [P, D])
            ctx_in, mask_in, mask_ready = sem("ctx_in"), sem("mask_in"), sem("mask_ready")
        else:
            X1 = sb("X1", [P, TT, D])
            ln_affine = sb("ln_affine", [P, 2, KC])

        room = probsT[:].rearrange("p a j q -> p (a j q)")
        w_all = room[:, 0:KC * 3 * D].rearrange("p (c e) -> p c e", c=KC)
        wo_pad = room[:, 1536:2560].rearrange("p (g e) -> p g e", g=HG)
        wo_cols = room[:, 2560:3584].rearrange("p (c h d) -> p c h d", c=KC, h=H)
        if cross:
            w_nat = [mask[:, i, :].bitcast(F32).rearrange("p (c d) -> p c d", c=KC) for i in range(4)]
        def tile_of(x, b, t):
            return x[:, bass.ds(b * TT + t, 1), :].rearrange("p o d -> p (o d)")

        def applied(dve, i, dst, src, b, t):
            at = b * TT + t
            if isinstance(b, int):
                mean, inv = moments[:, i, at, 0:1], inverse[:, i, at:at + 1]
            else:
                mean = moments[:, i].rearrange("p t w -> p (t w)")[:, bass.ds(2 * at, 1)]
                inv = inverse[:, i, bass.ds(at, 1)]
            return dve.tensor_scalar(dst, src, mean, inv, ALU.subtract, ALU.mult)

        def statistics(dve, settled, i, tiles):
            settled.settle()
            for t in tiles:
                settled.link(dve.bn_aggr(moments[:, i, t, :], stats[:, t, :]))
            settled.settle()
            at = slice(tiles[0], tiles[-1] + 1)
            variance, guess, bits = (work[:, w, at] for w in range(3))
            inverse_deviation(settled, moments[:, i, at, 1], variance, inverse[:, i, at], guess, bits)

        def norms_of(dve, settled, tiles, room):
            for t in tiles:
                settled.link(dve.bn_stats(stats[:, t, :], X[:, t, :]))
            statistics(dve, settled, 0, tiles)
            for t in tiles:
                if t >= 2 * TT:
                    settled.settle()
                settled.link(applied(dve, 0, room[:, t % TT, :], X[:, t, :], 0, t))
                if t % TT == TT - 1:
                    settled.settle()
                    for v in range(TT):
                        settled.link(dve.bn_stats(stats[:, t - TT + 1 + v, :], room[:, v, :]))
            statistics(dve, settled, 1, tiles)

        weights = [wq, wk, wv, (wo_h, wo_l)]
        if cross:
            wide = [w_all[:, :, i * D:(i + 1) * D] for i in range(3)] + [wo_pad]
        else:
            wide = [w_all.rearrange("p c (e w) -> p c e w", w=3)[:, :, :, i] for i in range(3)] + [wo_pad]
        with nc.Block() as block:
            @block.sync
            def _(sp):
                def load(dst, src, loaded):
                    with nc.allow_non_contiguous_dma(reason="the biases and gains, once"):
                        sp.dma_start(dst, src).then_inc(loaded, 16)

                if cross:
                    load(CTX[:], dram["ctx"].rearrange("(b t p) d -> b p t d", b=B, p=P)[0], ctx_in)
                    for i, name in enumerate(("Wq", "Wk", "Wv", "Wo")):
                        load(w_nat[i], dram[name].rearrange("(c p) d -> p c d", p=P), weights_in)
                    for i, name in enumerate(("bk", "bq")):
                        load(bias_kq[:, :, i], dram[name].rearrange("(c p) -> p c", p=P), small_in)
                    load(bias_v[:], dram["bv"].partition_broadcast(P), small_in)
                    load(bias_out[:], dram["bo"].partition_broadcast(P), small_in)
                else:
                    x_rows = dram["x"].rearrange("(t p) d -> p t d", p=P)
                    load(X[:, 0:TT, :], x_rows[:, 0:TT, :], x_in)
                    load(w_all, dram["w_qkv"].rearrange("(c p) e -> p c e", p=P), weights_in)
                    sp.wait_ge(wo_cleared, 1)
                    rows = dram["w_proj"].rearrange("(g j d) e -> j d g e", g=HG, j=4)
                    for j in range(4):
                        load(wo_pad[PAD * j:PAD * j + HD], rows[j], wo_in)
                    for i, name in enumerate(("ln_scale", "ln_bias")):
                        load(ln_affine[:, i, :], dram[name].rearrange("(c p) -> p c", p=P), small_in)
                    load(bias_out[:], dram["b_proj"].partition_broadcast(P), small_in)
                    load_constants(sp)
                    load(X[:, TT:NT, :], x_rows[:, TT:NT, :], x_rest_in)
                sp.wait_ge(small_in, 16 * (4 if cross else 3))

            @block.tensor
            def _(pe):
                if not cross:
                    return
                pe.wait_ge(weights_in, 16 * 4)
                for i in range(3):
                    for c in range(KC):
                        for e in range(KC):
                            ins = pe.transpose(psum[:, i, (c * KC + e) * P:(c * KC + e + 1) * P],
                                               w_nat[i][:, e, c * P:(c + 1) * P], const["ident"])
                    ins.then_inc(w_transposed, 1)
                pe.wait_ge(wo_placed, 1)
                for g in range(HG):
                    for e in range(KC):
                        n = g * KC + e
                        ins = pe.transpose(psum[:, 4 + n // 4, (n % 4) * P:(n % 4 + 1) * P],
                                           wo_cols[:, e, 4 * g:4 * g + 4, :].rearrange("p h d -> p (h d)"),
                                           const["ident"])
                ins.then_inc(w_transposed, 1)

            @block.vector
            def _(dve):
                if not cross:
                    dve.memset(wo_pad, 0.0).then_inc(wo_cleared, 1)
                    dve.wait_ge(x_in, 16)
                settled = Count(dve, stats_step)
                if cross:
                    statistics(dve, settled, 0, range(NT))
                else:
                    norms_of(dve, settled, range(TT), X1)
                for t in range(TT):
                    ins = applied(dve, LN - 1, Z[:, t, :], X[:, t, :] if cross else X1[:, t, :], 0, t)
                    ins.then_inc(z_ready, 1) if t == TT - 1 else settled.link(ins)
                settled.settle()
                stats_steps.append(settled.n)
                if cross:
                    dve.wait_ge(small_in, 16 * 4)
                    dve.tensor_scalar(bias_kq[:, :, 1], bias_kq[:, :, 1], SCORE_SCALE, None, ALU.mult).then_inc(prep, 1)
                dve.wait_ge(cleared, 1)
                if not cross:
                    dve.wait_ge(const_in, 16 * 2)
                for j in range(4):
                    rows = KT[96:P, :, :].rearrange("p (g j) s -> p g j s", j=4)[:, :, j, :]
                    dve.tensor_scalar(rows, rows.bitcast(F32), const["select_max"][96:P, j:j + 1], None,
                                      ALU.mult).then_inc(prep, 1)
                dve.wait_ge(prep, 4 + cross)
                dve.wait_ge(z_ready, 1)

            @block.scalar
            def _(act):
                if cross:
                    act.wait_ge(weights_in, 16 * 4)
                    act.wait_ge(wo_cleared, 1)
                    for e in range(KC):
                        ins = act.copy(wo_cols[:, e, :, 0:HD], w_nat[3][:, e, :].rearrange("p (h d) -> p h d", h=H))
                    ins.then_inc(wo_placed, 1)
                    for i in range(3):
                        act.wait_ge(w_transposed, i + 1)
                        act.copy(wide[i], psum[:, i, :].rearrange("p (c e) -> p c e", c=KC)).then_inc(w_full, 1)
                    act.wait_ge(w_transposed, 4)
                    act.copy(wo_pad, psum[:, 4:6, :].rearrange("p n (g e) -> p (n g) e", g=2)).then_inc(w_full, 1)
                for i, ((hi, _), one) in enumerate(zip(weights, wide)):
                    if cross:
                        act.wait_ge(w_full, i + 1)
                    elif i == 0:
                        act.wait_ge(weights_in, 16)
                    elif i == 3:
                        act.wait_ge(wo_in, 64)
                    act.copy(hi[:], one).then_inc(w_high, 1)

            @block.gpsimd
            def _(pool):
                n = 0
                if cross:
                    pool.memset(wo_cols, 0.0).then_inc(wo_cleared, 1)
                    pool.wait_ge(wo_cleared, 1)
                for at, value in ((KT[96:P].bitcast(F32), 1.0), (max_cols[:].bitcast(F32), 0.0), (V[:], 0.0),
                                  (V[:, :, :, HD:HD + 1], 1.0)):
                    pool.memset(at, value).then_inc(cleared, 1)
                    n += 1
                    pool.wait_ge(cleared, n)
                for i, ((hi, lo), one) in enumerate(zip(weights, wide)):
                    pool.wait_ge(w_high, i + 1)
                    pool.tensor_tensor(lo[:], one, hi[:].bitcast(F32), ALU.subtract).then_inc(w_low, 1)
                pool.wait_ge(w_low, len(weights))

        def sections(eng, prepare, step):
            prepare()
            step(0, 0, (0, len(prologue)), True, False)
            with eng.Fori(0, B - 1) as b:
                n = IN_FIRST
                for g in range(1, HG + 1):
                    step(b + g // HG, g % HG, (b, n), False, False)
                    n += count(items(g % HG))
            n = IN_FIRST
            for g in range(1, HG):
                step(B - 1, g, (B - 1, n), False, True)
                n += count(items(g, last=True))
            return B - 1, n

        def next_item(at):
            return at[0], at[1] + 1

        def bank_of(at):
            return psum[:, ITEM_BANK + at[1] % 2, :]

        def wait_item(eng, at):
            eng.wait_ge(item_ready, at[0] * IN_ROUND + at[1] + 1)

        def wait_read(eng, at):
            eng.wait_ge(item_read[at[1] % 2], at[0] * (IN_ROUND // 2) + at[1] // 2 + 1)

        with nc.Block() as block:
            if cross:
                @block.sync
                def _(sp):
                    ctx_rows = dram["ctx"].rearrange("(b t p) d -> b p t d", b=B, p=P)
                    mask_rows = dram["mask"].rearrange("b (t p) s -> b p t s", p=P)
                    sp.dma_start(mask[:], mask_rows[0]).then_inc(mask_in, 16)
                    with sp.Fori(1, B) as b:
                        sp.wait_ge(low_ready, b * SPLITS - SPLITS + KC)
                        sp.dma_start(CTX[:], ctx_rows[bass.ds(b, 1)].rearrange("o p t d -> (o p) t d")
                                     ).then_inc(ctx_in, 16)
                        sp.wait_ge(mask_ready, b * TT)
                        sp.dma_start(mask[:], mask_rows[bass.ds(b, 1)].rearrange("o p t s -> (o p) t s")
                                     ).then_inc(mask_in, 16)

            @block.gpsimd
            def _(pool):
                def add_residual(b):
                    tiles = bias_out[:].unsqueeze(1).to_broadcast([P, TT, D])
                    pool.wait_ge(z_ready, b + 1)
                    pool.sem_inc(const["pool_waited"], 1)
                    Xb = X[:, bass.ds(b * TT, TT), :]
                    if cross:
                        pool.tensor_tensor(Xb, Xb, tiles, ALU.add).then_inc(residual_step, 1)
                    else:
                        pool.tensor_tensor(Xb, Xb, X1[:], ALU.add).then_inc(residual_step, 1)
                        pool.wait_ge(residual_step, b * 2 + 1)
                        pool.sem_inc(const["pool_waited"], 1)
                        pool.tensor_tensor(Xb, Xb, tiles, ALU.add).then_inc(residual_step, 1)

                def low_part(item, b, n):
                    kind, _, i = item
                    s = SPLIT_OF[kind, i]
                    if kind == "T":
                        hi, lo = (x[:, i // KC, i % KC, :] for x in (source_h, source_l))
                    else:
                        hi, lo = (x[:, i, "KQ".index(kind), :] for x in (base_h, base_l))
                    wait_read(pool, n)
                    pool.tensor_tensor(lo, full[:, s % 2, :], hi.bitcast(F32), ALU.subtract).then_inc(low_ready, 1)

                def place_values(b, g):
                    at = V_next[:].rearrange("p t (h d) -> p t h d", h=H)
                    pool.sem_inc(const["pool_waited"], 1)
                    pool.tensor_copy(V[:, :, 4 * g:4 * g + 4, 0:HD], at[:, :, 4 * g:4 * g + 4, :]).then_inc(v_placed, 1)

                def convert_mask(b, t):
                    pool.sem_inc(const["pool_waited"], 1)
                    pool.tensor_scalar(mask_bias[:, t, :], mask[:, t, :], 0.0, MASKED,
                                       ALU.is_equal, ALU.mult).then_inc(mask_ready, 1)

                def split_weighted(b, g, n):
                    at = b * (2 * HG) + 2 * g + 2
                    o = OT[:, g % 2, :]
                    wait_read(pool, n)
                    pool.sem_inc(const["pool_waited"], 1)
                    pool.tensor_scalar(OT_h[:, g, :], o, 1.0, 0.0, ALU.mult, ALU.add).then_inc(norm_step, 1)
                    pool.wait_ge(norm_step, at + 1)
                    pool.tensor_tensor(OT_l[:, g, :], o, OT_h[:, g, :].bitcast(F32), ALU.subtract).then_inc(norm_step, 1)

                def prepare():
                    pool.sem_inc(norm_step, 2)
                    for i, item in enumerate(prologue):
                        n = (0, i)
                        if item[0] in ("T", "K", "Q"):
                            low_part(item, 0, n)
                        if cross and item == ("K", 0, 1):
                            pool.wait_ge(mask_in, 16)
                            for t in range(TT):
                                convert_mask(0, t)
                        if item == ("V", 0, 0):
                            add_residual(0)
                        if item == ("V", 0, 1):
                            wait_read(pool, n)
                            for g in range(HG):
                                place_values(0, g)

                def step(b, g, n, first, last):
                    for u, (early, late) in enumerate(items(g, first, last)):
                        if cross and not last and g == 2 and 2 <= u < 2 + TT:
                            if u == 2:
                                pool.wait_ge(mask_in, b * 16 + 32)
                            pool.wait_ge(max_ready, b * (SCORES * HG) + SCORES * HG - SCORES + 4 * (u - 2) + 4)
                            convert_mask(b + 1, u - 2)
                        if u == 6 and g == 2 and not last:
                            add_residual(b + 1)
                        if u == 5 and g == 3 and not last:
                            for v in range(3):
                                pool.wait_ge(av_ready, b * NT + 4 * v + 4)
                                place_values(b + 1, v)
                        if u == 5 and g == 0 and not first:
                            pool.wait_ge(av_ready, b * NT)
                            place_values(b, 3)
                        for item in early + late:
                            if item[0] == "R":
                                split_weighted(b + item[1], item[2], n)
                            elif item[0] in ("T", "K", "Q"):
                                low_part(item, b + 1, n)
                            n = next_item(n)

                n = sections(pool, prepare, step)
                split_weighted(B - 1, HG - 1, next_item(n))
                pool.wait_ge(norm_step, 2 * HG * B + 2)

            @block.tensor
            def _(pe):
                ident, ident_b, ident_r = const["ident"], const["ident_b"], const["ident_r"]

                def item_products(item, b, n):
                    kind, ahead, i = item
                    b = b + ahead
                    out = bank_of(n)
                    if n[1] >= 2:
                        wait_read(pe, (n[0], n[1] - 2))
                    if kind == "T":
                        if i == 0 and cross:
                            pe.wait_ge(ctx_in, b * 16 + 16)
                        if i == (SRC - 1) * KC:
                            pe.wait_ge(z_ready, b + 1)
                        what, c = (CTX if cross and i < KC else Z), i % KC
                        for t in range(TT):
                            ins = pe.transpose(out[:, t * P:(t + 1) * P], what[:, t, c * P:(c + 1) * P], ident)
                    elif kind in ("K", "Q"):
                        pe.wait_ge(low_ready, b * SPLITS + (KC if kind == "K" else SRC * KC))
                        (wh, wl), s = (wk, 0) if kind == "K" else (wq, SRC - 1)
                        at = slice(i * P, (i + 1) * P)
                        terms = [(wh[:, c, at], x[:, s, c, :]) for c in range(KC) for x in (source_h, source_l)]
                        terms += [(wl[:, c, at], source_h[:, s, c, :]) for c in range(KC)]
                        for j, (lhsT, rhs) in enumerate(terms):
                            ins = pe.matmul(out, lhsT, rhs, start=(j == 0), stop=(j == len(terms) - 1))
                    elif kind == "V":
                        pe.wait_ge(low_ready, b * SPLITS + KC)
                        for t in (2 * i, 2 * i + 1):
                            at = slice(t * P, (t + 1) * P)
                            terms = [(source_h[:, 0, c, at], w[:, c, :]) for c in range(KC) for w in wv]
                            terms += [(source_l[:, 0, c, at], wv[0][:, c, :]) for c in range(KC)]
                            for j, (lhsT, rhs) in enumerate(terms):
                                ins = pe.matmul(out[:, (t % 2) * D:(t % 2 + 1) * D], lhsT, rhs,
                                                start=(j == 0 and t % 2 == 0), stop=(j == len(terms) - 1),
                                                skip_group_check=True)
                    elif kind in ("KD", "QD"):
                        c, which = i // 4, "KQ".index(kind[0])
                        pe.wait_ge(low_ready, b * SPLITS + SPLIT_OF[kind[0], c] + 1)
                        for part, x in enumerate((base_h, base_l)):
                            ins = pe.matmul(out, const["select"][:, i % 4, which, part, :], x[:, c, which, :],
                                            start=(part == 0), stop=(part == 1))
                    elif kind == "MT":
                        pe.wait_ge(mask_ready, b * TT + TT)
                        for t in range(TT):
                            ins = pe.transpose(out[:, 0:S // 2].bitcast(BF16)[:, t * P:(t + 1) * P],
                                               mask_bias[:, t, i * P:(i + 1) * P], ident_b)
                    elif kind == "M":
                        pe.wait_ge(max_split, b * HG + i + 1)
                        for t in range(TT):
                            ins = pe.matmul(out[:, t * P:(t + 1) * P], max_cols[:, t, :], ident_r,
                                            start=True, stop=True)
                    elif kind == "SUM":
                        pe.wait_ge(o_out, b * HG + i + 1)
                        for t in range(TT):
                            ins = pe.matmul(out[:, 4 * t:4 * t + 4], OT[:, i % 2, t * P:(t + 1) * P],
                                            const["pick_sums"], start=True, stop=True)
                    elif kind == "R":
                        for back in (1, 2):
                            wait_read(pe, (n[0], n[1] - back))
                        for t in range(TT):
                            ins = pe.matmul(out[:, t * P:(t + 1) * P], inv_rows[:, t].rearrange("p j d -> p (j d)"),
                                            ident, start=True, stop=True)
                    elif kind == "OUT":
                        pe.wait_ge(norm_step, b * (2 * HG) + 2 * HG + 2)
                        for t in (2 * i, 2 * i + 1):
                            at = slice(t * P, (t + 1) * P)
                            terms = [(OT_h[:, g, at], w[:, g, :]) for g in range(HG) for w in (wo_h, wo_l)]
                            terms += [(OT_l[:, g, at], wo_h[:, g, :]) for g in range(HG)]
                            for j, (lhsT, rhs) in enumerate(terms):
                                ins = pe.matmul(out[:, (t % 2) * D:(t % 2 + 1) * D], lhsT, rhs,
                                                start=(j == 0 and t % 2 == 0), stop=(j == len(terms) - 1),
                                                skip_group_check=True)
                    ins.then_inc(item_ready, 1)

                def scores(b, g, s):
                    t, h = s // 4, 4 * g + s % 4
                    if not (isinstance(b, int) and b == 0 and g == 0 and s < 2):
                        pe.wait_ge(max_ready, b * (SCORES * HG) + SCORES * g + s - 1)
                    pe.matmul(psum[:, S_BANK + s % 2, :], QT[:, h // 2, t * P:(t + 1) * P], KT[:, h, :],
                              start=True, stop=True).then_inc(scores_ready, 1)

                def scores_transposed(b, g, u, i):
                    t, pair = u // 2, GP * g + u % 2
                    c = 2 * (UNITS * g + u) + i
                    if c >= 3:
                        pe.wait_ge(probs_ready, b * TILES + c - 2)
                    elif c == 0 and not (isinstance(b, int) and b == 0):
                        pe.wait_ge(probs_ready, b * TILES)
                    out_c = psum[:, C_BANK + c % 3, :]
                    ins = pe.matmul(out_c, KT[:, 2 * pair + i, t * P:(t + 1) * P], QT[:, pair, :],
                                    start=True, stop=not cross)
                    if cross:
                        ins = pe.matmul(out_c, ident_b, mask_biasT[:, t, :], start=False, stop=True)
                    ins.then_inc(scoresT_ready, 1)

                def weighted_values(b, g, t):
                    pe.wait_ge(probs_ready, b * TILES + 4 * (TT * g + t) + 4)
                    if t == 0:
                        pe.wait_ge(v_placed, b * HG + g + 1)
                        if not (isinstance(b, int) and b == 0 and g == 0):
                            pe.wait_ge(o_out, b * HG + g)
                    for j in range(4):
                        ins = pe.matmul(psum[PAD * j:PAD * j + PAD, O_BANK, :], V[:, t, 4 * g + j, :],
                                        probsT[:, t % 2, j, :], start=(t == 0), stop=(t == TT - 1),
                                        tile_position=(0, PAD * j))
                    ins.then_inc(av_ready, 1)

                def prepare():
                    s = 0
                    for i, item in enumerate(prologue[:-1]):
                        if item == ("KD", 0, 0):
                            pe.wait_ge(const["ready"], 3)
                        item_products(item, 0, (0, i))
                        if i == SCORES_FROM:
                            for back in (1, 2):
                                wait_read(pe, (0, i - back))
                        if i >= SCORES_FROM:
                            for _ in range(min(3, SCORES - s)):
                                scores(0, 0, s)
                                s += 1
                    item_products(prologue[-1], 0, (0, len(prologue) - 1))

                def step(b, g, n, first, last):
                    ahead, group = divmod(g + 1, HG)
                    after = 0 if g == 1 or first else len(items((g - 1) % HG, last=last)[-1][1])
                    for back in (1, 2):
                        wait_read(pe, (n[0], n[1] - after - back))
                    s = 0
                    for u, (early, late) in enumerate(items(g, first, last)):
                        due = 0 if last and ahead else SCORES_IN[u]

                        def next_scores():
                            nonlocal due, s
                            if due:
                                scores(b + ahead, group, s)
                                due, s = due - 1, s + 1

                        next_scores()
                        scores_transposed(b, g, u, 0)
                        for item in early:
                            item_products(item, b, n)
                            n = next_item(n)
                        next_scores()
                        scores_transposed(b, g, u, 1)
                        if u == 1 and not first:
                            weighted_values(b - 1 if g == 0 else b, (g - 1) % HG, TT - 1)
                        if u in (3, 5, 7):
                            weighted_values(b, g, u // 2 - 1)
                        next_scores()
                        for item in late:
                            item_products(item, b, n)
                            n = next_item(n)

                n = sections(pe, prepare, step)
                weighted_values(B - 1, HG - 1, TT - 1)
                for item in END:
                    item_products(item, B - 1, n)
                    n = next_item(n)

            @block.scalar
            def _(act):
                def read_item(item, b, n):
                    kind, ahead, i = item
                    b = b + ahead
                    if kind not in ("T", "K", "Q", "KD", "QD", "M"):
                        return
                    wait_item(act, n)
                    src = bank_of(n)
                    if kind in ("T", "K", "Q"):
                        s = SPLIT_OF[kind, i]
                        if not (isinstance(b, int) and b == 0 and s < 2):
                            act.wait_ge(low_ready, b * SPLITS + s - 1)
                        if kind == "T":
                            hi = source_h[:, i // KC, i % KC, :]
                        else:
                            hi = base_h[:, i, "KQ".index(kind), :]
                        for out in (full[:, s % 2, :], hi):
                            if kind == "T" and cross:
                                ins = act.activation(out, src, ACT.Copy)
                            elif kind == "T":
                                ins = act.activation(out, src, ACT.Identity, bias=ln_affine[:, 1, i:i + 1],
                                                     scale=ln_affine[:, 0, i:i + 1])
                            else:
                                scale = SCORE_SCALE if kind == "Q" else 1.0
                                if cross:
                                    bias = bias_kq[:, i, "KQ".index(kind):"KQ".index(kind) + 1]
                                    ins = act.activation(out, src, ACT.Identity, bias=bias, scale=scale)
                                else:
                                    ins = act.activation(out, src, ACT.Copy, scale=scale)
                    elif kind == "KD":
                        for j in range(2):
                            ins = act.activation(KT[0:96, 2 * i + j, :], src[0:96], ACT.Copy,
                                                 scale=const["keep_head"][0:96, j:j + 1])
                    elif kind == "QD":
                        ins = act.copy(QT[:, i, :], src)
                    elif kind == "M":
                        ins = act.copy(QT[96:P, GP * i:GP * i + GP, :],
                                       src[96:P].unsqueeze(1).to_broadcast([32, GP, S]))
                    ins.then_inc(item_read[n[1] % 2], 1)

                def exponentials(b, g, u):
                    t = u // 2
                    if not (isinstance(b, int) and b == 0 and g == 0 and t < 2):
                        act.wait_ge(av_ready, b * NT + TT * g + t - 1)
                    for i in range(2):
                        c = 2 * (UNITS * g + u) + i
                        act.wait_ge(scoresT_ready, b * TILES + c + 1)
                        act.activation(probsT[:, t % 2, 2 * (u % 2) + i, :], psum[:, C_BANK + c % 3, :],
                                       ACT.Exp).then_inc(probs_ready, 1)

                def take_weighted(b, g):
                    act.wait_ge(av_ready, b * NT + TT * g + TT)
                    if not (isinstance(b, int) and b == 0 and g < 2):
                        act.wait_ge(norm_step, b * (2 * HG) + 2 * g)
                    act.copy(OT[:, g % 2, :], psum[:, O_BANK, :]).then_inc(o_out, 1)

                def prepare():
                    for i, item in enumerate(prologue):
                        n = (0, i)
                        read_item(item, 0, n)

                def step(b, g, n, first, last):
                    for u, (early, late) in enumerate(items(g, first, last)):
                        for item in early:
                            read_item(item, b, n)
                            n = next_item(n)
                        exponentials(b, g, u)
                        if u == 1 and not first:
                            take_weighted(b - 1 if g == 0 else b, (g - 1) % HG)
                        for item in late:
                            read_item(item, b, n)
                            n = next_item(n)

                sections(act, prepare, step)
                take_weighted(B - 1, HG - 1)

            @block.vector
            def _(dve):
                def read_item(item, b, n):
                    kind, ahead, i = item
                    b = b + ahead
                    if kind not in ("V", "MT", "SUM", "R", "OUT"):
                        return
                    wait_item(dve, n)
                    src = bank_of(n)
                    two = src.rearrange("p (t e) -> p t e", t=2)
                    if kind == "V":
                        if not (isinstance(b, int) and b == 0):
                            dve.wait_ge(v_placed, b * HG)
                        out = V_next[:, 2 * i:2 * i + 2, :]
                        if cross:
                            ins = dve.tensor_tensor(out, two, bias_v[:].unsqueeze(1).to_broadcast([P, 2, D]), ALU.add)
                        else:
                            ins = dve.tensor_copy(out, two)
                    elif kind == "MT":
                        ins = dve.tensor_copy(mask_biasT[:, i, :], src[:, 0:S // 2].bitcast(BF16))
                    elif kind == "SUM":
                        dve.reciprocal(inv_sums[:].rearrange("p t j -> p (t j)"), src[:, 0:4 * TT]).then_inc(inverted, 1)
                        dve.wait_ge(inverted, b * HG + i + 1)
                        ins = dve.tensor_copy(inv_rows[:], inv_sums[:].unsqueeze(3).to_broadcast([P, TT, 4, PAD]))
                    elif kind == "R":
                        o = OT[:, i % 2, :]
                        ins = dve.tensor_tensor(o, o, src, ALU.mult)
                    elif kind == "OUT":
                        Xi = X[:, bass.ds(b * TT + 2 * i, 2), :]
                        dve.wait_ge(residual_step, (b + 1) * (1 if cross else 2))
                        ins = dve.tensor_tensor(Xi, two, Xi, ALU.add)
                    ins.then_inc(item_read[n[1] % 2], 1)
                    if kind == "OUT":
                        wait_read(dve, n)
                        dve.sem_inc(const["vector_waited"], 1)
                        for t in (2 * i, 2 * i + 1):
                            new = const["x_stats"][:, bass.ds(b * TT + t, 1), :].rearrange("p o w -> p (o w)")
                            dve.bn_stats(new, tile_of(X, b, t)).then_inc(new_stats, 1)

                def layer_norm_tile(b, k, steps):
                    i, t = divmod(k, TT)
                    if k == 0:
                        dve.wait_ge(v_placed, b * HG)
                        if not cross:
                            dve.wait_ge(residual_step, b * 2)
                    if i == 1:
                        steps.settle()
                    src = tile_of(X, b, t) if i == 0 else X1[:, t, :]
                    dst = Z[:, t, :] if i == LN - 1 else X1[:, t, :]
                    ins = applied(dve, i, dst, src, b, t)
                    if k == LN * TT - 1:
                        ins.then_inc(z_ready, 1)
                    else:
                        steps.link(ins)

                def maximum(b, g, s):
                    bank, out = psum[:, S_BANK + s % 2, :], neg_max[:, g % 2, s // 4, s % 4:s % 4 + 1]
                    if cross and s % 4 == 0:
                        dve.wait_ge(mask_ready, b * TT + s // 4 + 1)
                    dve.wait_ge(scores_ready, b * (SCORES * HG) + SCORES * g + s + 1)
                    if cross:
                        dve.sem_inc(const["vector_waited"], 1)
                        ins = dve.tensor_tensor_reduce(out=bank, in0=bank, in1=mask_bias[:, s // 4, :], scale=-1.0,
                                                       scalar=3e38, op0=ALU.add, op1=ALU.min, accum_out=out)
                    else:
                        ins = dve.tensor_reduce(out, bank, AX_X, ALU.max, negate=True)
                    ins.then_inc(max_ready, 1)
                    if s == SCORES - 1:
                        dve.wait_ge(max_ready, b * (SCORES * HG) + SCORES * g + SCORES)
                        hi = max_cols[:, :, 96:100]
                        dve.tensor_copy(hi, neg_max[:, g % 2]).then_inc(max_step, 1)
                        dve.wait_ge(max_step, b * HG + g + 1)
                        dve.tensor_tensor(max_cols[:, :, 100:104], neg_max[:, g % 2], hi.bitcast(F32),
                                          ALU.subtract).then_inc(max_split, 1)

                def prepare():
                    if not cross:
                        prepare_constants(dve)
                        dve.wait_ge(x_rest_in, 16)
                        scratch = OT[:].rearrange("p i (t d) -> p (i t) d", d=D)
                        norms_of(dve, Count(dve, stats_step, stats_steps[0]), range(TT, NT), scratch)
                    for s in range(SCORES):
                        maximum(0, 0, s)
                    for i, item in enumerate(prologue[:-1]):
                        read_item(item, 0, (0, i))

                def step(b, g, n, first, last):
                    ahead, group = divmod(g + 1, HG)
                    s = normed = 0
                    if g == 1 and not last:
                        steps = Count(dve, ln_step, b * NORM_STEPS)
                    for u, (early, late) in enumerate(items(g, first, last)):
                        if not (last and ahead):
                            for _ in range(SCORES_IN[u]):
                                maximum(b + ahead, group, s)
                                s += 1
                            if g == 1 and not last and normed < LN * TT:
                                layer_norm_tile(b + 1, normed, steps)
                                normed += 1
                        for item in early + late:
                            read_item(item, b, n)
                            n = next_item(n)

                n = sections(dve, prepare, step)
                for item in END:
                    read_item(item, B - 1, n)
                    n = next_item(n)
                dve.wait_ge(new_stats, NT)




E = 4
F = 1024
FC = F // P
F2 = 512
C2 = F2 // P
G = 8
GRID = np.linspace(-1.2, 0.2, G).astype(np.float32)
N8 = 2 * E


def experts(nc, X, psum, const, dram, out):
    with ExitStack() as ctx:
        share = ctx.enter_context(nc.sbuf_tensor("share", [P, NT, N8], F32))
        h0T_dram = nc.dram_tensor("h0T_scratch", (B, P, KC * S), F32).ap()
        early = KanEarly(nc, ctx, dram, h0T_dram)
        with ExitStack() as inner:
            hT_h = inner.enter_context(nc.sbuf_tensor("hT_h", [P, KC, NT * P], F32R))
            hT_l = inner.enter_context(nc.sbuf_tensor("hT_l", [P, KC, NT * P], F32R))
            router = make_router(nc, inner, X, psum, const, dram, share, hT_h, hT_l, h0T_dram)
            mlp_experts(nc, X, psum, const, dram, share, hT_h, hT_l, *router, early)
        kan_experts(nc, X, psum, const, dram, share, h0T_dram, early, out)


R_BANK = 6


def make_router(nc, ctx, X, psum, const, dram, share, hT_h, hT_l, h0T_dram):
    STEPS = (3 * TT + 15) + TT - 2 + 2 + 2 * TT + 4 + 2 + 1

    def sb(name, shape, dt=F32):
        return ctx.enter_context(nc.sbuf_tensor(f"r_{name}", shape, dt))

    def sem(name):
        return ctx.enter_context(nc.semaphore(f"r_{name}"))

    gate, bias8 = sb("gate", [P, KC, N8]), sb("bias8", [N8, D])
    stats, moments = sb("stats", [P, TT, 6]), sb("moments", [P, TT, 2])
    inverse, work = sb("inverse", [P, TT]), sb("work", [P, 3, TT])
    x_moments, x_inverse, x_work = sb("x_moments", [P, NT, 2]), sb("x_inverse", [P, NT]), sb("x_work", [P, 3, NT])
    Hn, H0 = sb("Hn", [P, TT, D]), sb("H0", [P, TT, D])
    hT, h0T = sb("hT", [P, KC, S]), sb("h0T", [P, KC, S])
    neg_top, total, inv_total = sb("neg_top", [P, TT]), sb("total", [P, TT]), sb("inv_total", [P, TT])
    expd, chance = sb("expd", [P, TT, N8]), sb("chance", [P, TT, N8])
    best, where = sb("best", [P, TT, 8]), sb("where", [P, TT, 8], U32)
    where_f, pair_share = sb("where_f", [P, TT, 2]), sb("pair_share", [P, TT, 2])
    pair_sum, pair_inv = sb("pair_sum", [P, TT]), sb("pair_inv", [P, TT])
    picked, shares = sb("picked", [P, TT, 2, N8]), sb("shares", [P, TT, N8])
    sharesT = sb("sharesT", [N8, TT, P])

    weights_in, step, stored = sem("weights_in"), sem("step"), sem("stored")
    h_ready, h0_ready, hT_psum, hT_ready = sem("h_ready"), sem("h0_ready"), sem("hT_psum"), sem("hT_ready")
    split_ready, logits_psum, top_ready, exp_ready = (
        sem("split_ready"), sem("logits_psum"), sem("top_ready"), sem("exp_ready"))
    shares_ready, sharesT_psum, sharesT_ready = sem("shares_ready"), sem("sharesT_psum"), sem("sharesT_ready")
    x_step = sem("x_step")
    bias_psum, x_done, high_ready = sem("bias_psum"), sem("x_done"), sem("high_ready")
    pair = psum[:, R_BANK:R_BANK + 2, :]

    def load(sp):
        with nc.allow_non_contiguous_dma(reason="the gate, once"):
            sp.dma_start(gate[:], dram["gate_W"].rearrange("(c p) e -> p c e", p=P)).then_inc(weights_in, 16)
        sp.dma_start(bias8[0:E, :], dram["mlp_b2"]).then_inc(weights_in, 16)
        sp.dma_start(bias8[E:N8, :], dram["kan_sl_b1"]).then_inc(weights_in, 16)

    def tensor(pe, b):
        ident = const["ident"]

        def transposes(src, ready):
            pe.wait_ge(ready, b + 1)
            for c in range(KC):
                for t in range(TT):
                    ins = pe.transpose(pair[:, c, t * P:(t + 1) * P], src[:, t, c * P:(c + 1) * P], ident)
            ins.then_inc(hT_psum, 1)

        def h_transposes():
            if not (isinstance(b, int) and b == 0):
                pe.wait_ge(x_done, b)
            transposes(Hn, h_ready)

        def h0_transposes():
            pe.wait_ge(hT_ready, b * 2 + 1)
            transposes(H0, h0_ready)

        def logits():
            pe.wait_ge(hT_ready, b * 2 + 2)
            for t in range(TT):
                for c in range(KC):
                    ins = pe.matmul(pair[:, 0, t * N8:(t + 1) * N8], hT[:, c, t * P:(t + 1) * P],
                                    gate[:, c, :], start=(c == 0), stop=(c == KC - 1))
            ins.then_inc(logits_psum, 1)

        def biases():
            pe.wait_ge(shares_ready, b + 1)
            for t in range(TT):
                ins = pe.transpose(pair[0:N8, 1, t * P:(t + 1) * P], shares[:, t, :], ident)
            ins.then_inc(sharesT_psum, 1)
            pe.wait_ge(sharesT_ready, b + 1)
            for t in range(TT):
                ins = pe.matmul(pair[:, t // 2, t % 2 * D:(t % 2 + 1) * D], sharesT[:, t, :], bias8[:],
                                start=True, stop=True)
            ins.then_inc(bias_psum, 1)

        return h_transposes, h0_transposes, logits, biases

    def scalar(act, b):
        def copy_h():
            act.wait_ge(hT_psum, b * 2 + 1)
            if not (isinstance(b, int) and b == 0):
                act.wait_ge(split_ready, b)
            act.copy(hT_h[:, :, bass.ds(b * S, S)], pair).then_inc(high_ready, 1)
            act.copy(hT[:], pair).then_inc(hT_ready, 1)

        def copy_h0():
            act.wait_ge(hT_psum, b * 2 + 2)
            if not (isinstance(b, int) and b == 0):
                act.wait_ge(stored, b * 16)
            act.copy(h0T[:], pair).then_inc(hT_ready, 1)
            act.wait_ge(hT_ready, b * 2 + 2)
            act.dma_start(h0T_dram[bass.ds(b, 1)].rearrange("o p s -> (o p) s"),
                          h0T[:].rearrange("p c s -> p (c s)")).then_inc(stored, 16)

        def exponentials():
            act.wait_ge(top_ready, b + 1)
            for t in range(TT):
                ins = act.activation(expd[:, t, :], pair[:, 0, t * N8:(t + 1) * N8], ACT.Exp,
                                     bias=neg_top[:, t:t + 1], accum_out=total[:, t:t + 1])
            ins.then_inc(exp_ready, 1)

        def copy_shares():
            act.wait_ge(sharesT_psum, b + 1)
            act.copy(sharesT[:].rearrange("e t p -> e (t p)"), pair[0:N8, 1, :]).then_inc(sharesT_ready, 1)

        return copy_h, copy_h0, exponentials, copy_shares

    def low_part(pool, b):
        at = bass.ds(b * S, S)
        pool.wait_ge(high_ready, b + 1)
        pool.wait_ge(hT_ready, b * 2 + 1)
        pool.sem_inc(const["pool_waited"], 1)
        pool.tensor_tensor(hT_l[:, :, at], hT[:], hT_h[:, :, at].bitcast(F32), ALU.subtract).then_inc(split_ready, 1)

    def statistics_of_x(dve):
        settled = Count(dve, x_step)
        for t in range(NT):
            settled.link(dve.bn_aggr(x_moments[:, t, :], const["x_stats"][:, t, :]))
        settled.settle()
        inverse_deviation(settled, x_moments[:, :, 1], x_work[:, 0, :], x_inverse[:], x_work[:, 1, :], x_work[:, 2, :])

    def vector(dve, b):
        settled = Count(dve, step, b * STEPS)
        Xt = lambda t: X[:, bass.ds(b * TT + t, 1), :].rearrange("p o d -> p (o d)")

        def statistics(src):
            for t in range(TT):
                settled.link(dve.bn_stats(stats[:, t, :], src(t)))
            settled.settle()
            dve.sem_inc(const["vector_waited"], 1)
            for t in range(TT):
                settled.link(dve.bn_aggr(moments[:, t, :], stats[:, t, :]))
            settled.settle()
            inverse_deviation(settled, moments[:, :, 1], work[:, 0, :], inverse[:], work[:, 1, :], work[:, 2, :])

        def normalised(dst, src, ready):
            for t in range(TT):
                ins = dve.tensor_scalar(dst[:, t, :], src(t), moments[:, t, 0:1], inverse[:, t:t + 1],
                                        ALU.subtract, ALU.mult)
                if t == TT - 1:
                    ins.then_inc(ready, 1)
                else:
                    settled.link(ins)

        def norm_h():
            for t in range(TT):
                at = b * TT + t
                mean = x_moments[:].rearrange("p t w -> p (t w)")[:, bass.ds(2 * at, 1)]
                ins = dve.tensor_scalar(Hn[:, t, :], Xt(t), mean, x_inverse[:, bass.ds(at, 1)],
                                        ALU.subtract, ALU.mult)
                if t == TT - 1:
                    ins.then_inc(h_ready, 1)
                else:
                    settled.link(ins)

        def norm_h0():
            dve.wait_ge(h_ready, b + 1)
            h = lambda t: Hn[:, t, :]
            statistics(h)
            normalised(H0, h, h0_ready)

        def top_logit():
            dve.wait_ge(logits_psum, b + 1)
            dve.tensor_reduce(neg_top[:], pair[:, 0, 0:TT * N8].rearrange("p (t e) -> p t e", t=TT), AX_X, ALU.max,
                              negate=True).then_inc(top_ready, 1)

        def find_shares():
            dve.wait_ge(exp_ready, b + 1)
            settled(dve.reciprocal(inv_total[:], total[:]))
            settled(dve.tensor_tensor(chance[:], expd[:], inv_total[:].unsqueeze(2).to_broadcast([P, TT, N8]),
                                      ALU.mult))
            dve.sem_inc(const["vector_waited"], 1)
            for t in range(TT):
                settled.link(dve.max(best[:, t, :], chance[:, t, :]))
            settled.settle()
            dve.sem_inc(const["vector_waited"], 1)
            for t in range(TT):
                settled.link(dve.max_index(where[:, t, :], best[:, t, :], chance[:, t, :]))
            settled.settle()
            settled(dve.tensor_copy(where_f[:], where[:, :, 0:2]))
            settled(dve.tensor_tensor(pair_sum[:], best[:, :, 0], best[:, :, 1], ALU.add))
            settled(dve.reciprocal(pair_inv[:], pair_sum[:]))
            settled(dve.tensor_tensor(pair_share[:], best[:, :, 0:2],
                                      pair_inv[:].unsqueeze(2).to_broadcast([P, TT, 2]), ALU.mult))
            wide = [P, TT, 2, N8]
            settled(dve.tensor_tensor(picked[:], const["experts"].unsqueeze(1).unsqueeze(1).to_broadcast(wide),
                                      where_f[:].unsqueeze(3).to_broadcast(wide), ALU.is_equal))
            settled(dve.tensor_tensor(picked[:], picked[:], pair_share[:].unsqueeze(3).to_broadcast(wide), ALU.mult))
            dve.tensor_tensor(shares[:], picked[:, :, 0, :], picked[:, :, 1, :], ALU.add).then_inc(shares_ready, 1)
            dve.wait_ge(shares_ready, b + 1)
            settled(dve.tensor_tensor(share[:, bass.ds(b * TT, TT), :], shares[:],
                                      const["signs"].unsqueeze(1).to_broadcast([P, TT, N8]), ALU.mult))
            assert settled.n == STEPS, (settled.n, STEPS)

        def add_biases():
            dve.wait_ge(bias_psum, b + 1)
            Xb = X[:, bass.ds(b * TT, TT), :]
            dve.tensor_tensor(Xb, Xb, pair.rearrange("p k (t d) -> p (k t) d", d=D), ALU.add).then_inc(x_done, 1)

        return norm_h, norm_h0, top_logit, find_shares, add_biases

    return load, tensor, scalar, vector, statistics_of_x, low_part, weights_in, split_ready, stored


def mlp_experts(nc, X, psum, const, dram, share, hT_h, hT_l, load_router, router_tensor, router_scalar,
                router_vector, statistics_of_x, router_pool, router_in, split_ready, stored, early):
    TURNS = E * B
    LAG = 2
    TENSOR_AT, SCALAR_AT, VECTOR_AT = (3, 4, 5, 7), (3, 4, 5, 7), (1, 2, 4, 5, 7)
    RING = 3
    UP_BANKS, DOWN_BANK = 4, 4
    CH = KC * P
    with ExitStack() as ctx:
        def sb(name, shape, dt=F32):
            return ctx.enter_context(nc.sbuf_tensor(f"m_{name}", shape, dt))

        def sem(name):
            return ctx.enter_context(nc.semaphore(f"m_{name}"))

        w1_h, w1_l = sb("w1_h", [P, FC, KC, P], F32R), sb("w1_l", [P, FC, KC, P], F32R)
        w2_h, w2_l = sb("w2_h", [P, FC, D], F32R), sb("w2_l", [P, FC, D], F32R)
        raw = sb("raw", [P, 2, FC, CH])
        b1 = sb("b1", [P, E, FC])
        hidden = sb("hidden", [P, 2, S])
        hid_h, hid_l = sb("hid_h", [P, 4, S], F32R), sb("hid_l", [P, 4, S], F32R)

        b1_in, w1_in, w2_in = sem("b1_in"), sem("w1_in"), sem("w2_in")
        high_ready, w1_ready, w2_ready = sem("high_ready"), sem("w1_ready"), sem("w2_ready")
        up_psum, gelu_ready, high_hidden, hidden_ready = (
            sem("up_psum"), sem("gelu_ready"), sem("high_hidden"), sem("hidden_ready"))
        down_used, out_ready, x_done = sem("down_used"), sem("out_ready"), sem("x_done")

        with nc.Block() as block:
            @block.sync
            def _(sp):

                def load(e):
                    w1 = dram["mlp_W1"][e].rearrange("(c p) (f n) -> f p c n", p=P, f=FC)
                    w2 = dram["mlp_W2"][e].rearrange("(f p) d -> f p d", p=P)
                    return w1, w2

                w1 = dram["mlp_W1"].rearrange("e (c p) (f n) -> e c p f n", p=P, f=FC)
                w2 = dram["mlp_W2"].rearrange("e (f p) d -> e p f d", p=P)

                def fetch(e, first):
                    if not first:
                        sp.wait_ge(w1_ready, e * FC)
                    for c in range(KC):
                        src = w1[0, c] if first else w1[bass.ds(e, 1), c].rearrange("o p f n -> (o p) f n")
                        sp.dma_start(raw[:, 0].rearrange("p f (c n) -> p f c n", c=KC)[:, :, c, :],
                                     src).then_inc(w1_in, 16)
                    if not first:
                        sp.wait_ge(w2_ready, e * FC)
                    src = w2[0] if first else w2[bass.ds(e, 1)].rearrange("o p f d -> (o p) f d")
                    sp.dma_start(raw[:, 1], src).then_inc(w2_in, 16)

                load_router(sp)
                fetch(0, True)
                with nc.allow_non_contiguous_dma(reason="4096 bias values, once"):
                    sp.dma_start(b1[:], dram["mlp_b1"].rearrange("e (f p) -> p e f", p=P)).then_inc(b1_in, 16)
                with sp.Fori(1, E) as e:
                    fetch(e, False)
                early.load(sp)

            @block.gpsimd
            def _(pool):
                def split_weights(e, first):
                    pool.wait_ge(w1_in, (e + 1) * 16 * KC)
                    pool.wait_ge(w2_in, (e + 1) * 16)
                    for f in range(FC):
                        if first and f == 2:
                            router_pool(pool, 0)
                        last = (e * B - 1) * FC + f + 1
                        for i, (hi, lo, ready, used) in enumerate(
                                ((w1_h[:, f].rearrange("p c n -> p (c n)"), w1_l[:, f].rearrange("p c n -> p (c n)"),
                                  w1_ready, up_psum), (w2_h[:, f], w2_l[:, f], w2_ready, down_used))):
                            if not first:
                                pool.wait_ge(used, last)
                            pool.sem_inc(const["pool_waited"], 1)
                            pool.tensor_scalar(hi, raw[:, i, f], 1.0, 0.0, ALU.mult, ALU.add).then_inc(high_ready, 1)
                            pool.wait_ge(high_ready, e * 2 * FC + 2 * f + i + 1)
                            pool.tensor_tensor(lo, raw[:, i, f], hi.bitcast(F32), ALU.subtract).then_inc(ready, 1)

                split_weights(0, True)
                with pool.Fori(1, B) as b:
                    router_pool(pool, b)
                with pool.Fori(1, E) as e:
                    split_weights(e, False)

            @block.tensor
            def _(pe):
                def up(turn, e, batch, f):
                    pe.wait_ge(w1_ready, e * FC + f + 1)
                    n = turn * FC + f
                    if not (isinstance(turn, int) and n < UP_BANKS):
                        pe.wait_ge(gelu_ready, n - UP_BANKS + 1)
                    at = bass.ds(batch * S, S)
                    terms = [(w1_h[:, f, c, :], h[:, c, at]) for c in range(KC) for h in (hT_h, hT_l)]
                    terms += [(w1_l[:, f, c, :], hT_h[:, c, at]) for c in range(KC)]
                    for i, (lhsT, rhs) in enumerate(terms):
                        ins = pe.matmul(psum[:, f % UP_BANKS, :], lhsT, rhs, start=(i == 0), stop=(i == len(terms) - 1))
                    ins.then_inc(up_psum, 1)

                def down(turn, e, f):
                    pe.wait_ge(w2_ready, e * FC + f + 1)
                    pe.wait_ge(hidden_ready, turn * FC + f + 1)
                    if f == 0 and not (isinstance(turn, int) and turn == 0):
                        pe.wait_ge(x_done, turn * TT)
                    for t in range(TT):
                        out = psum[:, DOWN_BANK + t // 2, t % 2 * D:(t % 2 + 1) * D]
                        at = slice(t * P, (t + 1) * P)
                        for i, (hid, w) in enumerate(((hid_h, w2_h), (hid_h, w2_l), (hid_l, w2_h))):
                            ins = pe.matmul(out, hid[:, f % 4, at], w[:, f, :],
                                            start=(f == 0 and i == 0 and t % 2 == 0), stop=(f == FC - 1 and i == 2),
                                            skip_group_check=True)
                    ins.then_inc(down_used, 1)

                def chunks(turn, route=None):
                    e, batch = (0, turn) if isinstance(turn, int) else (turn // B, turn % B)
                    if route is not None:
                        stages = router_tensor(pe, route)
                    if isinstance(turn, int) and turn < B or route is not None:
                        pe.wait_ge(split_ready, turn + 1)
                    for f in range(FC):
                        up(turn, e, batch, f)
                        if f > LAG:
                            if f == LAG + 1:
                                down(turn, e, 0)
                            down(turn, e, f - LAG)
                        elif f == LAG:
                            pass
                        elif not isinstance(turn, int):
                            down(turn - 1, (turn - 1) // B, FC + f - LAG)
                        elif turn > 0:
                            down(turn - 1, 0, FC + f - LAG)
                        if route is not None and f in TENSOR_AT:
                            stages[TENSOR_AT.index(f)]()

                pe.wait_ge(router_in, 16 * 3)
                for stage in router_tensor(pe, 0):
                    stage()
                chunks(0, 1)
                with pe.Fori(1, B - 1) as turn:
                    chunks(turn, turn + 1)
                chunks(B - 1)
                with pe.Fori(B, TURNS) as turn:
                    chunks(turn)
                for f in range(FC - LAG, FC):
                    down(TURNS - 1, E - 1, f)

            @block.scalar
            def _(act):
                def gelu(turn, e, f):
                    n = turn * FC + f
                    act.wait_ge(up_psum, n + 1)
                    if not (isinstance(turn, int) and n < 2):
                        act.wait_ge(hidden_ready, n - 1)
                    act.activation(hidden[:, f % 2, :], psum[:, f % UP_BANKS, :], ACT.Gelu,
                                   bias=b1[:, bass.ds(e, 1), f]).then_inc(gelu_ready, 1)

                def chunks(turn, route=None):
                    if route is not None:
                        stages = router_scalar(act, route)
                    for f in range(FC):
                        gelu(turn, 0 if isinstance(turn, int) else turn // B, f)
                        if route is not None and f in SCALAR_AT:
                            stages[SCALAR_AT.index(f)]()

                for stage in router_scalar(act, 0):
                    stage()
                act.wait_ge(b1_in, 16)
                chunks(0, 1)
                with act.Fori(1, B - 1) as turn:
                    chunks(turn, turn + 1)
                chunks(B - 1)
                with act.Fori(B, TURNS) as turn:
                    chunks(turn)
                act.wait_ge(stored, 16 * B)
                early.load_h0(act, 0)

            @block.vector
            def _(dve):
                def split_hidden(turn, f):
                    n = turn * FC + f
                    dve.wait_ge(gelu_ready, n + 1)
                    if not (isinstance(turn, int) and n < 4):
                        dve.wait_ge(down_used, n - 3)
                    dve.tensor_copy(hid_h[:, f % 4, :], hidden[:, f % 2, :]).then_inc(high_hidden, 1)
                    dve.wait_ge(high_hidden, n + 1)
                    dve.tensor_tensor(hid_l[:, f % 4, :], hidden[:, f % 2, :], hid_h[:, f % 4, :].bitcast(F32),
                                      ALU.subtract).then_inc(hidden_ready, 1)

                def add_output(turn, e, batch):
                    dve.wait_ge(down_used, turn * FC + FC)
                    for t in range(TT):
                        tile = batch * TT + t
                        Xt = X[:, bass.ds(tile, 1), :].rearrange("p o d -> p (o d)")
                        dve.scalar_tensor_tensor(Xt, psum[:, DOWN_BANK + t // 2, t % 2 * D:(t % 2 + 1) * D],
                                                 share_flat[:, bass.ds(tile * N8 + e, 1)], Xt,
                                                 ALU.mult, ALU.add).then_inc(x_done, 1)

                share_flat = share[:].rearrange("p t e -> p (t e)")

                def chunks(turn, route=None):
                    if route is not None:
                        stages = router_vector(dve, route)
                    for f in range(FC):
                        split_hidden(turn, f)
                        if f == LAG - 1 and not (isinstance(turn, int) and turn == 0):
                            before = turn - 1
                            if isinstance(turn, int):
                                add_output(before, 0, before)
                            else:
                                add_output(before, before // B, before % B)
                        if route is not None and f in VECTOR_AT:
                            stages[VECTOR_AT.index(f)]()

                statistics_of_x(dve)
                for stage in router_vector(dve, 0):
                    stage()
                chunks(0, 1)
                with dve.Fori(1, B - 1) as turn:
                    chunks(turn, turn + 1)
                chunks(B - 1)
                with dve.Fori(B, TURNS) as turn:
                    chunks(turn)
                early.prepare(dve)
                add_output(TURNS - 1, E - 1, B - 1)


KAN_CHUNK = 1024


class KanEarly:

    def __init__(self, nc, ctx, dram, h0T_dram):
        def sb(name, shape, dt=F32):
            return ctx.enter_context(nc.sbuf_tensor(f"k_{name}", shape, dt))

        def sem(name):
            return ctx.enter_context(nc.semaphore(f"k_{name}"))

        self.nc, self.dram, self.h0T_dram = nc, dram, h0T_dram
        self.raw = sb("raw", [P, 2, KAN_CHUNK])
        self.bias0 = sb("bias0", [P, E, F2])
        self.gains0, self.offsets0 = sb("gains0", [P, E * KC]), sb("offsets0", [P, E * KC])
        self.gains1, self.offsets1 = sb("gains1", [P, E * C2]), sb("offsets1", [P, E * C2])
        self.shifts0, self.shifts1 = sb("shifts0", [P, E * KC, G]), sb("shifts1", [P, E * C2, G])
        self.h0T = sb("h0T", [P, KC, S])
        self.params_in, self.params_ready = sem("params_in"), sem("params_ready")
        self.raw_in = [sem("raw_in0"), sem("raw_in1")]
        self.h0_in = sem("h0_in")

    def load_chunk(self, sp, e, layer, n):
        w, width = (self.dram["kan_sl_W0"], F2) if layer == 0 else (self.dram["kan_sl_W1"], D)
        w = w.rearrange("e (c p g) n -> e c p g n", p=P, g=G)
        step = KAN_CHUNK // width
        c, g = divmod(n * step, G)
        src = w[0, c] if isinstance(e, int) else w[bass.ds(e, 1), c].rearrange("o p g n -> (o p) g n")
        sp.dma_start(self.raw[:, n % 2].rearrange("p (g n) -> p g n", g=step),
                     src[:, g:g + step, :]).then_inc(self.raw_in[n % 2], 16)

    def load(self, sp):
        with self.nc.allow_non_contiguous_dma(reason="6144 values, once"):
            for name, dst in (("kan_ln_g0", self.gains0), ("kan_ln_b0", self.offsets0),
                              ("kan_ln_g1", self.gains1), ("kan_ln_b1", self.offsets1)):
                sp.dma_start(dst[:], self.dram[name].rearrange("e (c p) -> p (e c)", p=P)).then_inc(self.params_in, 16)
        for e in range(E):
            sp.dma_start(self.bias0[:, e, :],
                         self.dram["kan_sl_b0"][e].partition_broadcast(P)).then_inc(self.params_in, 16)
        for n in range(2):
            self.load_chunk(sp, 0, 0, n)

    def load_h0(self, act, batch):
        src = self.h0T_dram[batch] if isinstance(batch, int) else self.h0T_dram[bass.ds(batch, 1)].rearrange(
            "o p s -> (o p) s")
        act.dma_start(self.h0T[:].rearrange("p c s -> p (c s)"), src).then_inc(self.h0_in, 16)

    def prepare(self, dve):
        dve.wait_ge(self.params_in, 16 * (4 + E))
        for gains in (self.gains0, self.gains1):
            dve.tensor_scalar(gains[:], gains[:], 0.5, None, ALU.mult).then_inc(self.params_ready, 1)
        for offsets, shifts in ((self.offsets0, self.shifts0), (self.offsets1, self.shifts1)):
            for g in range(G):
                dve.tensor_scalar(shifts[:, :, g], offsets[:], float(-GRID[g]), 0.5,
                                  ALU.add, ALU.mult).then_inc(self.params_ready, 1)
        dve.wait_ge(self.params_ready, 2 + 2 * G)


def room_of(p):
    return p % 2


def kan_experts(nc, X, psum, const, dram, share, h0T_dram, early, out):
    TURNS = E * B
    PAIRS0, PAIRS1 = KC * G // 2, C2 * G // 2
    BODY = PAIRS0 + PAIRS1
    CHUNK = KAN_CHUNK
    CH0, CH1 = KC * G * F2 // CHUNK, C2 * G * D // CHUNK
    Z_BANKS, Y_BANK, T_BANK = TT, 4, 6
    LN_AT, T_AT, EVAC_AT = (1, 2, 3), (4, 6), 2
    STEPS = 3 * TT + 15 - 1

    def pair0(turn, p):
        return p if isinstance(turn, int) and turn == 0 else PAIRS0 + (turn - 1) * BODY + p

    def pair1(turn, p):
        if isinstance(turn, int) and turn == TURNS - 1:
            return PAIRS0 + (TURNS - 1) * BODY + p
        return PAIRS0 + turn * BODY + PAIRS0 + p

    with ExitStack() as ctx:
        def sb(name, shape, dt=F32):
            return ctx.enter_context(nc.sbuf_tensor(f"k_{name}", shape, dt))

        def sem(name):
            return ctx.enter_context(nc.semaphore(f"k_{name}"))

        w0_h, w0_l = sb("w0_h", [P, KC * G, F2], F32R), sb("w0_l", [P, KC * G, F2], F32R)
        w1_h, w1_l = sb("w1_h", [P, C2 * G, D], F32R), sb("w1_l", [P, C2 * G, D], F32R)
        raw, bias0, h0T, gains0, gains1 = early.raw, early.bias0, early.h0T, early.gains0, early.gains1
        shifts0, shifts1 = early.shifts0, early.shifts1
        h1T = sb("h1T", [P, C2, S])
        square = sb("square", [P, 2, 2, S])
        basis_h, basis_l = sb("basis_h", [P, 2, 2, S], F32R), sb("basis_l", [P, 2, 2, S], F32R)
        Z = sb("Z", [P, TT, F2])
        stats, moments = sb("stats", [P, TT, 6]), sb("moments", [P, TT, 2])
        variance, inverse = sb("variance", [P, TT]), sb("inverse", [P, TT])
        work = sb("work", [P, 2, TT])

        w_high, w_ready = sem("w_high"), sem("w_ready")
        raw_in, h0_in = early.raw_in, early.h0_in
        tanh_ready, square_ready, basis_high, basis_ready, pair_used = (
            sem("tanh_ready"), sem("square_ready"), sem("basis_high"), sem("basis_ready"), sem("pair_used"))
        z_out, norm_step, z_normed, h1T_psum, h1T_ready = (
            sem("z_out"), sem("norm_step"), sem("z_normed"), sem("h1T_psum"), sem("h1T_ready"))
        z_tile, x_done, out_stored = sem("z_tile"), sem("x_done"), sem("out_stored")
        layers = ((KC, h0T, gains0, shifts0), (C2, h1T, gains1, shifts1))

        with nc.Block() as block:
            @block.sync
            def _(sp):
                def fetch(e, first):
                    for layer, chunks in enumerate((CH0, CH1)):
                        for n in range(chunks):
                            place = e * (CH0 + CH1) + layer * CH0 + n
                            if first and place < 2:
                                continue
                            sp.wait_ge(w_ready, place - 1)
                            early.load_chunk(sp, e, layer, n)

                fetch(0, True)
                with sp.Fori(1, E) as e:
                    fetch(e, False)
                rows = out.rearrange("(t p) d -> p t d", p=P)
                for batch in range(B):
                    at = slice(batch * TT, (batch + 1) * TT)
                    sp.wait_ge(x_done, (TURNS - B + batch + 1) * TT)
                    sp.dma_start(rows[:, at, :], X[:, at, :]).then_inc(out_stored, 16)
                sp.wait_ge(out_stored, 16 * B)

            @block.gpsimd
            def _(pool):
                def split_weights(e, first):
                    for layer, (wh, wl, chunks) in enumerate(((w0_h, w0_l, CH0), (w1_h, w1_l, CH1))):
                        rows = wh.shape[1] // chunks
                        for n in range(chunks):
                            place = e * (CH0 + CH1) + layer * CH0 + n
                            pool.wait_ge(raw_in[n % 2], e * 8 * (CH0 + CH1) + (layer * CH0 + n) // 2 * 16 + 16)
                            if not first:
                                last = pair0(e * B - 1, n) if layer == 0 else pair1(e * B - 1, 2 * n + 1)
                                pool.wait_ge(pair_used, last + 1)
                            hi, lo = (w[:, n * rows:(n + 1) * rows, :].rearrange("p k n -> p (k n)") for w in (wh, wl))
                            pool.sem_inc(const["pool_waited"], 1)
                            pool.tensor_scalar(hi, raw[:, n % 2], 1.0, 0.0, ALU.mult, ALU.add).then_inc(w_high, 1)
                            pool.wait_ge(w_high, place + 1)
                            pool.tensor_tensor(lo, raw[:, n % 2], hi.bitcast(F32), ALU.subtract).then_inc(w_ready, 1)

                split_weights(0, True)
                with pool.Fori(1, E) as e:
                    split_weights(e, False)

            @block.scalar
            def _(act):
                def basis(layer, e, p, m):
                    chunks, x, gains, shifts = layers[layer]
                    c, g = divmod(2 * p, G)
                    room = square[:, room_of(p), :, :]
                    if not (isinstance(m, int) and m < 2):
                        act.wait_ge(basis_ready, m - 1)
                    at = bass.ds(e * chunks + c, 1)
                    for q in range(2):
                        ins = act.activation(room[:, q, :], x[:, c, :], ACT.Tanh, bias=shifts[:, at, g + q],
                                             scale=gains[:, at])
                    ins.then_inc(tanh_ready, 1)
                    act.wait_ge(tanh_ready, m + 1)
                    act.activation(room, room, ACT.Square).then_inc(square_ready, 1)

                def transposed(turn):
                    act.wait_ge(h1T_psum, turn * 2 + 1)
                    act.copy(h1T[:, 0:2, :], psum[:, T_BANK:T_BANK + 2, :]).then_inc(h1T_ready, 1)

                def transposed_rest(turn):
                    act.wait_ge(h1T_psum, turn * 2 + 2)
                    act.copy(h1T[:, 2:4, :], psum[:, T_BANK:T_BANK + 2, :]).then_inc(h1T_ready, 1)

                def first_layer(turn, e, with_last=True):
                    act.wait_ge(h0_in, turn * 16 + 16)
                    for p in range(PAIRS0):
                        basis(0, e, p, pair0(turn, p))
                        if with_last and p == T_AT[0]:
                            transposed(turn - 1)
                        if with_last and p == T_AT[1]:
                            transposed_rest(turn - 1)
                    early.load_h0(act, (turn + 1) % B)

                def second_layer(turn, e):
                    act.wait_ge(h1T_ready, turn * 2 + 2)
                    for p in range(PAIRS1):
                        basis(1, e, p, pair1(turn, p))

                first_layer(0, 0, with_last=False)
                first_layer(1, 0)
                second_layer(0, 0)
                with act.Fori(2, TURNS) as turn:
                    first_layer(turn, turn // B)
                    second_layer(turn - 1, (turn - 1) // B)
                transposed(TURNS - 1)
                transposed_rest(TURNS - 1)
                second_layer(TURNS - 1, E - 1)
                act.wait_ge(h0_in, 16 * TURNS + 16)

            @block.tensor
            def _(pe):
                def products(rooms, layer, p, m, w_h, w_l, first, last):
                    pe.wait_ge(basis_ready, m + 1)
                    r = room_of(p)
                    for q in range(2):
                        k = 2 * p + q
                        for t, (room, opens) in enumerate(rooms):
                            at = slice(t * P, (t + 1) * P)
                            for i, (x, w) in enumerate(((basis_h, w_h), (basis_h, w_l), (basis_l, w_h))):
                                ins = pe.matmul(room, x[:, r, q, at], w[:, k, :],
                                                start=(first and q == 0 and i == 0 and opens),
                                                stop=(last and q == 1 and i == 2), skip_group_check=True)
                    ins.then_inc(pair_used, 1)

                def transposes(turn, half):
                    pe.wait_ge(z_normed, turn + 1)
                    n = turn * 2 + half
                    if not (isinstance(turn, int) and n == 0):
                        pe.wait_ge(h1T_ready, n)
                    for c in range(2):
                        for t in range(TT):
                            ins = pe.transpose(psum[:, T_BANK + c, t * P:(t + 1) * P],
                                               Z[:, t, (2 * half + c) * P:(2 * half + c + 1) * P], const["ident"])
                    ins.then_inc(h1T_psum, 1)

                def first_layer(turn, e, with_last=True):
                    if with_last:
                        pe.wait_ge(z_out, turn)
                    for p in range(PAIRS0):
                        pe.wait_ge(w_ready, e * (CH0 + CH1) + p + 1)
                        products([(psum[:, t, :], True) for t in range(TT)], 0, p, pair0(turn, p),
                                 w0_h, w0_l, p == 0, p == PAIRS0 - 1)
                        if with_last and p + 1 in T_AT:
                            transposes(turn - 1, T_AT.index(p + 1))

                def second_layer(turn, e):
                    if not (isinstance(turn, int) and turn == 0):
                        pe.wait_ge(x_done, turn * TT)
                    for p in range(PAIRS1):
                        pe.wait_ge(w_ready, e * (CH0 + CH1) + CH0 + p // 2 + 1)
                        products([(psum[:, Y_BANK + t // 2, t % 2 * D:(t % 2 + 1) * D], t % 2 == 0)
                                  for t in range(TT)], 1, p, pair1(turn, p), w1_h, w1_l, p == 0, p == PAIRS1 - 1)

                first_layer(0, 0, with_last=False)
                first_layer(1, 0)
                second_layer(0, 0)
                with pe.Fori(2, TURNS) as turn:
                    first_layer(turn, turn // B)
                    second_layer(turn - 1, (turn - 1) // B)
                for half in range(2):
                    transposes(TURNS - 1, half)
                second_layer(TURNS - 1, E - 1)

            @block.vector
            def _(dve):
                share_flat = share[:].rearrange("p t e -> p (t e)")

                def basis(layer, p, m):
                    r = room_of(p)
                    dve.wait_ge(square_ready, m + 1)
                    if not (isinstance(m, int) and m < 2):
                        dve.wait_ge(pair_used, m - 1)
                    dve.tensor_scalar(basis_h[:, r], square[:, r], -1.0, None, ALU.add).then_inc(basis_high, 1)
                    dve.wait_ge(basis_high, m + 1)
                    flat = [x[:, r].rearrange("p q s -> p (q s)") for x in (basis_l, square, basis_h)]
                    dve.scalar_tensor_tensor(flat[0], flat[1], 1.0, flat[2].bitcast(F32),
                                             ALU.subtract, ALU.subtract).then_inc(basis_ready, 1)

                def evacuate(turn, e):
                    dve.wait_ge(pair_used, pair0(turn, PAIRS0 - 1) + 1)
                    if not (isinstance(turn, int) and turn == 0):
                        dve.wait_ge(h1T_psum, turn * 2)
                    for t in range(TT):
                        ins = dve.scalar_tensor_tensor(Z[:, t, :], psum[:, t, :], -1.0, bias0[:, bass.ds(e, 1), :].rearrange(
                            "p o n -> p (o n)"), ALU.mult, ALU.add)
                        ins.then_inc(z_out, 1) if t == TT - 1 else ins.then_inc(z_tile, 1)

                def layer_norm(turn, part, steps):
                    if part == 0:
                        dve.wait_ge(z_out, turn + 1)
                        for t in range(TT):
                            steps.link(dve.bn_stats(stats[:, t, :], Z[:, t, :]))
                        steps.settle()
                    elif part == 1:
                        for t in range(TT):
                            steps.link(dve.bn_aggr(moments[:, t, :], stats[:, t, :]))
                        steps.settle()
                        inverse_deviation(steps, moments[:, :, 1], variance[:], inverse[:], work[:, 0, :], work[:, 1, :])
                    else:
                        for t in range(TT):
                            ins = dve.tensor_scalar(Z[:, t, :], Z[:, t, :], moments[:, t, 0:1], inverse[:, t:t + 1],
                                                    ALU.subtract, ALU.mult)
                            if t == TT - 1:
                                ins.then_inc(z_normed, 1)
                            else:
                                steps.link(ins)
                        assert steps.n == STEPS, (steps.n, STEPS)

                def add_output(turn, e, batch):
                    dve.wait_ge(pair_used, pair1(turn, PAIRS1 - 1) + 1)
                    for t in range(TT):
                        tile = batch * TT + t
                        Xt = X[:, bass.ds(tile, 1), :].rearrange("p o d -> p (o d)")
                        dve.scalar_tensor_tensor(Xt, psum[:, Y_BANK + t // 2, t % 2 * D:(t % 2 + 1) * D],
                                                 share_flat[:, bass.ds(tile * N8 + E + e, 1)], Xt,
                                                 ALU.mult, ALU.add).then_inc(x_done, 1)

                def body(turn, e, before, e_before, second=False):
                    steps = Count(dve, norm_step, before * STEPS)
                    for p in range(PAIRS0):
                        basis(0, p, pair0(turn, p))
                        if p == 0 and not second:
                            add_output(turn - 2, (turn - 2) // B, (turn - 2) % B)
                        if p in LN_AT:
                            layer_norm(before, LN_AT.index(p), steps)
                    for p in range(PAIRS1):
                        basis(1, p, pair1(before, p))
                        if p == EVAC_AT:
                            evacuate(turn, e)

                for p in range(PAIRS0):
                    basis(0, p, pair0(0, p))
                evacuate(0, 0)
                body(1, 0, 0, 0, second=True)
                with dve.Fori(2, TURNS) as turn:
                    body(turn, turn // B, turn - 1, (turn - 1) // B)
                add_output(TURNS - 2, E - 1, B - 2)
                steps = Count(dve, norm_step, (TURNS - 1) * STEPS)
                for part in range(3):
                    layer_norm(TURNS - 1, part, steps)
                for p in range(PAIRS1):
                    basis(1, p, pair1(TURNS - 1, p))
                add_output(TURNS - 1, E - 1, B - 1)


def constants_on_host():
    marks = np.zeros((P, 28), np.float32)
    marks[np.arange(4) * PAD + HD, 24 + np.arange(4)] = 1
    for j in range(4):
        marks[[96 + j, 100 + j], j] = 1
    marks[0:48, 4] = marks[48:96, 5] = 1
    marks[:, 8:16] = np.arange(8)
    marks[:, 16:24] = np.where(np.arange(8) < 4, 1, -1)
    select = np.zeros((P, 4, 2, 2, P), np.float32)
    for pair in range(4):
        for which, parts in enumerate(((0, 1, 0), (0, 0, 1))):
            for place, part in enumerate(parts):
                for head in range(2):
                    for d in range(HD):
                        select[2 * HD * pair + HD * head + d, pair, which, part, 48 * head + HD * place + d] = 1
    return {"ident": np.eye(P, dtype=np.float32), "marks": marks, "select": select}


def build(nc, dram, out):
    with ExitStack() as ctx:
        def keep(name, shape, dt=F32):
            return ctx.enter_context(nc.sbuf_tensor(name, shape, dt))

        X = keep("X", [P, NT, D])
        ident, ident_b, marks = keep("ident", [P, P]), keep("ident_b", [P, P], BF16), keep("marks", [P, 28])
        psum = ctx.enter_context(nc.psum_tensor("psum", [P, 8, 512], F32))
        const_in, select_loaded, const_ready, vector_waited, pool_waited = (
            ctx.enter_context(nc.semaphore(n)) for n in (
                "const_in", "select_loaded", "const_ready", "vector_waited", "pool_waited"))
        const = {"ident": ident[:], "ident_b": ident_b[:], "select_max": marks[:, 0:4], "keep_head": marks[:, 4:6],
                 "experts": marks[:, 8:16], "signs": marks[:, 16:24], "pick_sums": marks[:, 24:28],
                 "x_stats": keep("x_stats", [P, NT, 6]), "in": const_in, "ready": const_ready, "vector_waited": vector_waited, "pool_waited": pool_waited}
        with ExitStack() as inner:
            def sb(name, shape, dt=F32):
                return inner.enter_context(nc.sbuf_tensor(name, shape, dt))

            ident_r = sb("ident_r", [P, P], F32R)
            select = sb("select", [P, 4, 2, 2, P], F32R)
            const.update(ident_r=ident_r[:], select=select)

            def load_constants(sp):
                sp.dma_start(marks[:], dram["marks"]).then_inc(const_in, 16)
                sp.dma_start(ident[:], dram["ident"]).then_inc(const_in, 16)
                sp.dma_start(select_in[:], dram["select"]).then_inc(select_loaded, 16)

            def prepare_constants(dve):
                dve.wait_ge(const_in, 32)
                dve.wait_ge(select_loaded, 16)
                dve.tensor_copy(ident_b[:], ident[:]).then_inc(const_ready, 1)
                dve.tensor_copy(ident_r[:], ident[:]).then_inc(const_ready, 1)
                dve.tensor_copy(select[:], select_in[:]).then_inc(const_ready, 1)

            with nc.sbuf_tensor("select_in", [P, 4, 2, 2, P], F32) as select_in:
                    attention(nc, False, X, psum, const, dram, load_constants, prepare_constants)
            attention(nc, True, X, psum, const, dram)
        experts(nc, X, psum, const, dram, out)


INPUTS = {
    "x": "x", "ctx": "ctx_1024", "mask": "mask_Bx1xSxS2_if1",
    "ln_scale": "L0_attn_ln_scale", "ln_bias": "L0_attn_ln_bias", "w_qkv": "L0_attn_w_qkv",
    "w_proj": "L0_attn_w_proj", "b_proj": "L0_attn_b_proj",
    "Wq": "L0_xattn_Wq", "bq": "L0_xattn_bq", "Wk": "L0_xattn_Wk", "bk": "L0_xattn_bk",
    "Wv": "L0_xattn_Wv", "bv": "L0_xattn_bv", "Wo": "L0_xattn_Wo", "bo": "L0_xattn_bo",
    "gate_W": "L0_ffn_gate_W", "mlp_W1": "L0_ffn_mlp_W1", "mlp_b1": "L0_ffn_mlp_b1",
    "mlp_W2": "L0_ffn_mlp_W2", "mlp_b2": "L0_ffn_mlp_b2",
    "kan_ln_g0": "L0_ffn_kan_ln_g0", "kan_ln_b0": "L0_ffn_kan_ln_b0",
    "kan_sl_W0": "L0_ffn_kan_sl_W0", "kan_sl_b0": "L0_ffn_kan_sl_b0",
    "kan_ln_g1": "L0_ffn_kan_ln_g1", "kan_ln_b1": "L0_ffn_kan_ln_b1",
    "kan_sl_W1": "L0_ffn_kan_sl_W1", "kan_sl_b1": "L0_ffn_kan_sl_b1",
}
RESHAPED = {"x": (B * S, D), "ctx": (B * S, D), "mask": (B, S, S)}


def kernel(**inputs):
    import concourse.bacc as bacc
    from concourse.bass_utils import run_bass_kernel_spmd

    nc = bacc.Bacc("TRN2", target_bir_lowering=False, num_devices=1)
    arrays = constants_on_host()
    for name, given in INPUTS.items():
        a = np.ascontiguousarray(inputs[given])
        arrays[name] = a.reshape(RESHAPED.get(name, a.shape))
    dram = {name: nc.dram_tensor(f"in_{name}", a.shape, mybir.dt.from_np(a.dtype), kind="ExternalInput").ap()
            for name, a in arrays.items()}
    out = nc.dram_tensor("out", (B * S, D), F32, kind="ExternalOutput").ap()
    build(nc, dram, out)
    result = run_bass_kernel_spmd(nc, [{f"in_{name}": a for name, a in arrays.items()}], core_ids=[0])
    return result.results[0]["out"].reshape(B, S, D)
```
